# Optimizing a Trainium2 kernel written in Bass

```python
import numpy as np
import jax
import jax.numpy as jnp

def _softmax(x, axis=-1):
    return jax.nn.softmax(x, axis=axis)

def _gelu(x):
    return jax.nn.gelu(x, approximate=True)

def _silu(x):
    return jax.nn.silu(x)

def _sigmoid(x):
    return jax.nn.sigmoid(x)

def _layernorm(x, axis=-1, eps=1e-05):
    m = jnp.mean(x, axis=axis, keepdims=True)
    v = jnp.var(x, axis=axis, keepdims=True)
    return (x - m) / jnp.sqrt(v + eps)

def _scatter_add(tgt, idx, src, axis=0):
    return tgt.at[idx].add(src)

def _segment_sum(src, seg, n):
    return jax.ops.segment_sum(src, seg, n)
kernel_name = 'mk_recurrent_d1_jaxref_r8_1667d9'

def setup_inputs(seed: int=0):
    np.random.seed(seed)
    _w = jnp.asarray

    def _L0_attn_setup():
        import jax, jax.numpy as jnp
        import numpy as np
        B_, L_, D_MODEL = (2, 256, 256)
        EXPAND = 2
        D_IN = EXPAND * D_MODEL
        HEADS = 64
        HEAD_DIM = D_IN // HEADS
        STATE = 128
        NGROUPS = 1
        K = 4
        CONV_DIM = D_IN + 2 * NGROUPS * STATE
        PROJ = D_IN + CONV_DIM + HEADS
        CHUNK = 32
        EPS = 1e-05

        def _segsum(x):
            T = x.shape[-1]
            c = jnp.cumsum(x, axis=-1)
            seg = c[..., :, None] - c[..., None, :]
            return jnp.where(jnp.tril(jnp.ones((T, T), bool)), seg, -jnp.inf)

        def _ssd(x, dA, Bm, Cm):
            b, l, h, p = x.shape
            n = Bm.shape[-1]
            c = l // CHUNK
            rep = h // Bm.shape[2]
            Bh = jnp.repeat(Bm, rep, axis=2).reshape(b, c, CHUNK, h, n)
            Ch = jnp.repeat(Cm, rep, axis=2).reshape(b, c, CHUNK, h, n)
            x = x.reshape(b, c, CHUNK, h, p)
            dA = dA.reshape(b, c, CHUNK, h).transpose(0, 3, 1, 2)
            dA_cum = jnp.cumsum(dA, axis=-1)
            Lmat = jnp.exp(_segsum(dA))
            Y_diag = jnp.einsum('bcthn,bcshn,bhcts,bcshp->bcthp', Ch, Bh, Lmat, x)
            decay_states = jnp.exp(dA_cum[..., -1:] - dA_cum)
            states = jnp.einsum('bcshn,bhcs,bcshp->bchpn', Bh, decay_states, x)
            chunk_decay = jnp.exp(_segsum(jnp.pad(dA_cum[..., -1], ((0, 0), (0, 0), (1, 0)))))
            states = jnp.concatenate([jnp.zeros_like(states[:, :1]), states], axis=1)
            prev = jnp.einsum('bhzc,bchpn->bzhpn', chunk_decay, states)[:, :-1]
            Y_off = jnp.einsum('bcthn,bchpn,bhct->bcthp', Ch, prev, jnp.exp(dA_cum))
            return (Y_diag + Y_off).reshape(b, l, h, p)
        key = jax.random.key(seed)
        ks = jax.random.split(key, 4)
        return {'hidden_states': jax.random.normal(ks[0], (B_, L_, D_MODEL), jnp.float32), 'in_proj_w': jax.random.normal(ks[1], (PROJ, D_MODEL), jnp.float32) * 0.02, 'conv_w': jax.random.normal(ks[2], (CONV_DIM, K), jnp.float32) * 0.2, 'conv_b': jnp.zeros((CONV_DIM,), jnp.float32), 'dt_bias': jnp.ones((HEADS,), jnp.float32), 'A_log': jnp.log(jnp.arange(1, HEADS + 1, dtype=jnp.float32)), 'D': jnp.ones((HEADS,), jnp.float32), 'norm_w': jnp.ones((D_IN,), jnp.float32), 'out_proj_w': jax.random.normal(ks[3], (D_MODEL, D_IN), jnp.float32) * 0.02}
    _L0_attn_in = _L0_attn_setup()

    def _L0_ffn_setup():
        import jax, jax.numpy as jnp
        import numpy as np
        H, I, E = (256, 512, 8)
        B, S = (2, 256)
        key = jax.random.key(seed)
        ks = jax.random.split(key, 5)
        scale = 0.02
        return {'hidden_states': jax.random.normal(ks[0], (B, S, H), dtype=jnp.float32), 'router_w': jax.random.normal(ks[1], (H, E), dtype=jnp.float32) * scale, 'gate_w': jax.random.normal(ks[2], (E, H, I), dtype=jnp.float32) * scale, 'up_w': jax.random.normal(ks[3], (E, H, I), dtype=jnp.float32) * scale, 'down_w': jax.random.normal(ks[4], (E, I, H), dtype=jnp.float32) * scale}
    _L0_ffn_in = _L0_ffn_setup()
    _d = {'L0_attn_hidden_states': _L0_attn_in['hidden_states'], 'L0_attn_in_proj_w': _L0_attn_in['in_proj_w'], 'L0_attn_conv_w': _L0_attn_in['conv_w'], 'L0_attn_conv_b': _L0_attn_in['conv_b'], 'L0_attn_dt_bias': _L0_attn_in['dt_bias'], 'L0_attn_A_log': _L0_attn_in['A_log'], 'L0_attn_D': _L0_attn_in['D'], 'L0_attn_norm_w': _L0_attn_in['norm_w'], 'L0_attn_out_proj_w': _L0_attn_in['out_proj_w'], 'L0_ffn_router_w': _L0_ffn_in['router_w'], 'L0_ffn_gate_w': _L0_ffn_in['gate_w'], 'L0_ffn_up_w': _L0_ffn_in['up_w'], 'L0_ffn_down_w': _L0_ffn_in['down_w']}
    _x0 = _d['L0_attn_hidden_states']
    _d['L0_attn_hidden_states'] = jax.random.normal(jax.random.fold_in(jax.random.key(seed), 1), (2, 1024, 256), dtype=_x0.dtype)
    del _x0
    return _d

def reference(L0_attn_hidden_states, L0_attn_in_proj_w, L0_attn_conv_w, L0_attn_conv_b, L0_attn_dt_bias, L0_attn_A_log, L0_attn_D, L0_attn_norm_w, L0_attn_out_proj_w, L0_ffn_router_w, L0_ffn_gate_w, L0_ffn_up_w, L0_ffn_down_w):

    def _L0_attn_ref(hidden_states, in_proj_w, conv_w, conv_b, dt_bias, A_log, D, norm_w, out_proj_w):
        import jax, jax.numpy as jnp
        import numpy as np
        B_, L_, D_MODEL = (2, 256, 256)
        EXPAND = 2
        D_IN = EXPAND * D_MODEL
        HEADS = 64
        HEAD_DIM = D_IN // HEADS
        STATE = 128
        NGROUPS = 1
        K = 4
        CONV_DIM = D_IN + 2 * NGROUPS * STATE
        PROJ = D_IN + CONV_DIM + HEADS
        CHUNK = 32
        EPS = 1e-05

        def _segsum(x):
            T = x.shape[-1]
            c = jnp.cumsum(x, axis=-1)
            seg = c[..., :, None] - c[..., None, :]
            return jnp.where(jnp.tril(jnp.ones((T, T), bool)), seg, -jnp.inf)

        def _ssd(x, dA, Bm, Cm):
            b, l, h, p = x.shape
            n = Bm.shape[-1]
            c = l // CHUNK
            rep = h // Bm.shape[2]
            Bh = jnp.repeat(Bm, rep, axis=2).reshape(b, c, CHUNK, h, n)
            Ch = jnp.repeat(Cm, rep, axis=2).reshape(b, c, CHUNK, h, n)
            x = x.reshape(b, c, CHUNK, h, p)
            dA = dA.reshape(b, c, CHUNK, h).transpose(0, 3, 1, 2)
            dA_cum = jnp.cumsum(dA, axis=-1)
            Lmat = jnp.exp(_segsum(dA))
            Y_diag = jnp.einsum('bcthn,bcshn,bhcts,bcshp->bcthp', Ch, Bh, Lmat, x)
            decay_states = jnp.exp(dA_cum[..., -1:] - dA_cum)
            states = jnp.einsum('bcshn,bhcs,bcshp->bchpn', Bh, decay_states, x)
            chunk_decay = jnp.exp(_segsum(jnp.pad(dA_cum[..., -1], ((0, 0), (0, 0), (1, 0)))))
            states = jnp.concatenate([jnp.zeros_like(states[:, :1]), states], axis=1)
            prev = jnp.einsum('bhzc,bchpn->bzhpn', chunk_decay, states)[:, :-1]
            Y_off = jnp.einsum('bcthn,bchpn,bhct->bcthp', Ch, prev, jnp.exp(dA_cum))
            return (Y_diag + Y_off).reshape(b, l, h, p)
        b, l, _ = hidden_states.shape
        proj = hidden_states @ in_proj_w.T
        gate = proj[..., :D_IN]
        xBC = proj[..., D_IN:D_IN + CONV_DIM]
        dt = proj[..., D_IN + CONV_DIM:]
        xp = jnp.pad(xBC, ((0, 0), (K - 1, 0), (0, 0)))
        conv = conv_b + sum((conv_w[:, i] * xp[:, i:i + l, :] for i in range(K)))
        xBC = jax.nn.silu(conv)
        x = xBC[..., :D_IN].reshape(b, l, HEADS, HEAD_DIM)
        Bm = xBC[..., D_IN:D_IN + NGROUPS * STATE].reshape(b, l, NGROUPS, STATE)
        Cm = xBC[..., D_IN + NGROUPS * STATE:].reshape(b, l, NGROUPS, STATE)
        dt = jax.nn.softplus(dt + dt_bias)
        A = -jnp.exp(A_log)
        y = _ssd(x * dt[..., None], dt * A, Bm, Cm)
        y = y + D[None, None, :, None] * x
        y = y.reshape(b, l, D_IN)
        hg = y * jax.nn.silu(gate)
        var = jnp.mean(hg * hg, axis=-1, keepdims=True)
        y = hg * jax.lax.rsqrt(var + EPS) * norm_w
        return y @ out_proj_w.T

    def _L0_ffn_ref(hidden_states, router_w, gate_w, up_w, down_w):
        import jax, jax.numpy as jnp
        import numpy as np
        H, I, E = (256, 512, 8)
        B, S = (2, 256)
        hidden_shape = hidden_states.shape
        x = hidden_states.reshape(-1, hidden_shape[-1])
        route = jax.nn.sigmoid(x @ router_w)
        max_ind = jnp.argmax(route, axis=1)
        max_prob = jnp.take_along_axis(route, max_ind[:, None], axis=1)
        out = jnp.zeros_like(x)
        num_experts = gate_w.shape[0]
        for e in range(num_experts):
            mask = (max_ind == e)[:, None]
            h = jax.nn.silu(x @ gate_w[e]) * (x @ up_w[e])
            out = out + jnp.where(mask, h @ down_w[e], 0.0)
        out = out * max_prob
        return out.reshape(hidden_shape)
    x = L0_attn_hidden_states
    xn = _layernorm(x, axis=-1)
    s = _L0_attn_ref(xn, L0_attn_in_proj_w, L0_attn_conv_w, L0_attn_conv_b, L0_attn_dt_bias, L0_attn_A_log, L0_attn_D, L0_attn_norm_w, L0_attn_out_proj_w)
    g = _silu(_L0_ffn_ref(xn, L0_ffn_router_w, L0_ffn_gate_w, L0_ffn_up_w, L0_ffn_down_w))
    x = x + s * g
    return x

_drawn_inputs = setup_inputs


def setup_inputs(seed=0):
    import zlib

    import numpy as np

    out = dict(_drawn_inputs(seed))
    spreads = {'L0_attn_conv_b': (0.0, 0.8),
     'L0_attn_dt_bias': (1.0, 0.6),
     'L0_attn_D': (1.0, 0.6),
     'L0_attn_norm_w': (1.0, 0.6)}
    factors = {'L0_attn_in_proj_w': 8.0,
     'L0_attn_conv_w': 8.0,
     'L0_attn_A_log': 8.0,
     'L0_attn_out_proj_w': 8.0,
     'L0_ffn_router_w': 8.0,
     'L0_ffn_gate_w': 8.0,
     'L0_ffn_up_w': 8.0,
     'L0_ffn_down_w': 8.0}
    for name, (base, spread) in spreads.items():
        noise = np.random.default_rng([zlib.crc32(name.encode()), seed]).standard_normal(out[name].shape)
        drawn = base * np.exp(spread * noise) if base else spread * noise
        out[name] = jnp.asarray(drawn.astype(out[name].dtype))
    for name, factor in factors.items():
        out[name] = (out[name] * factor).astype(out[name].dtype)
    return out
```

```python
from contextlib import ExitStack

import concourse.bass as bass
import numpy as np
from concourse import mybir

FP32 = mybir.dt.float32
I32 = mybir.dt.int32
U32 = mybir.dt.uint32
ALU = mybir.AluOpType
ACT = mybir.ActivationFunctionType
AX = mybir.AxisListType

P = 128
BATCH, SEQ, DM = 2, 1024, 256
DIN, HEADS, HD, NST, KC = 512, 64, 8, 128, 4
EXPERTS, DFF = 8, 512
EPS = 1e-5
TOK = BATCH * SEQ
TILES = TOK // P
TB = SEQ // P
GT = 4
GROUPS = TILES // GT
GW = GT * P
QB = TB // GT
DK = DM // P
HB = DIN // P
XB = HB + 2
LEVELS = 7
PRE = LEVELS
SUF, TOT = 0, 1
SLOTS = LEVELS + 1
KF = DFF // P
NT = TILES + EXPERTS - 1
WE = DK * DFF * 2 + KF * DM
RW = HEADS + EXPERTS
RING = 4

C_ID, C_LEV, C_PRE, C_SUF, C_ONE, C_TRI, C_MASK = 0, 1, 8, 9, 10, 11, 12
N_CONST = C_MASK + LEVELS
D_BASE = 4
V_BIAS, V_ALOG, V_D = 0, HEADS, 2 * HEADS
LOG1P_DEGREE = 10


def constant_matrices():
    k, t = np.arange(P)[:, None], np.arange(P)[None, :]
    mats = [k == t]
    for lev in range(LEVELS):
        same = (k >> lev) == (t >> lev)
        mats.append(same & np.where((t >> lev) & 1, k <= t, k > t))
    mats += [k <= t, k > t, k >= 0 * t, k < t]
    for lev in range(LEVELS):
        mats.append(((k >> lev) & 1 == 0) & ((t >> lev) & 1 == 1) & ((k >> lev + 1) == (t >> lev + 1)))
    return np.stack([m.astype(np.float32) for m in mats], axis=1)


def log1p_coefficients():
    cheb = np.polynomial.chebyshev.Chebyshev.interpolate(
        lambda u: np.log1p(u) / u, LOG1P_DEGREE, domain=[0, 1])
    power = cheb.convert(kind=np.polynomial.Polynomial, domain=[-1, 1], window=[-1, 1])
    return [float(c) for c in power(np.polynomial.Polynomial([0.5, 1.0])).coef]


def batch_steps():
    steps = []
    blocks = HB + XB
    steps += [("conv", 0, i) for i in range(blocks)]
    steps.append(("head", 0, 0))
    cut = [0, 4, 7, 10]
    for u in range(TB):
        if u < 3:
            steps += [("conv", 1, i) for i in range(cut[u], cut[u + 1])]
        if u + 1 < TB:
            steps.append(("head", u + 1, 0))
        steps.append(("mid", u, 0))
        if u > 0:
            steps.append(("tail", u - 1, 0))
    steps.append(("tail", TB - 1, 0))
    out, a, d = [], 0, 0
    for kind, x, i in steps:
        out.append((kind, x, i, a, d))
        a += {"conv": 1, "head": 3, "mid": 3, "tail": 1}[kind]
        d += {"conv": 0, "head": 1, "mid": 6, "tail": 0}[kind]
    return out, a, d


def mixer_moe_kernel(nc, x_in, w_main, w_dr, conv_c, head_v, norm_c, w_out, w_gate, w_up, w_down,
                     consts, out):
    STEPS, A_BATCH, D_BATCH = batch_steps()
    assert A_BATCH % RING == 0 and D_BATCH % RING == 0
    A_P1 = 4 * GROUPS
    COEF = log1p_coefficients()

    x_dram = x_in.rearrange("(t p) d -> p t d", p=P)
    out_dram = out.rearrange("(t p) d -> p t d", p=P)
    xs_dram = nc.dram_tensor("x_by_expert", [NT * P, DM], FP32).ap()
    ys_dram = nc.dram_tensor("y_by_expert", [NT * P, DM], FP32).ap()
    o_dram = nc.dram_tensor("mixer_rows", [TOK, DM], FP32).ap()
    xs_tiles = xs_dram.rearrange("(t p) d -> p t d", p=P)
    ys_tiles = ys_dram.rearrange("(t p) d -> p t d", p=P)
    o_tiles = o_dram.rearrange("(t p) d -> p t d", p=P)

    with ExitStack() as ctx:
        def sb(name, cols, dt=FP32):
            return ctx.enter_context(nc.sbuf_tensor(name, [P, cols], dt))

        def sem(name):
            return ctx.enter_context(nc.semaphore(name))

        CONST = sb("CONST", N_CONST * P)[:, :].rearrange("p (m t) -> p m t", m=N_CONST)
        W_MAIN = sb("W_MAIN", DK * 2 * (DIN + P))[:, :].rearrange("p (k n) -> p k n", k=DK)
        W_DR = sb("W_DR", DK * RW)[:, :].rearrange("p (k n) -> p k n", k=DK)
        CONVC = sb("CONVC", XB * 5)[:, :].rearrange("p (b j) -> p b j", j=5)
        HEADV = sb("HEADV", 3 * HEADS)
        NORMC = sb("NORMC", HB)
        W_OUT = sb("W_OUT", HB * DM)[:, :].rearrange("p (b n) -> p b n", b=HB)
        XNT = sb("XNT", DK * TOK)[:, :].rearrange("p (k t) -> p k t", k=DK)
        DT = sb("DT", TILES * HEADS)
        DA = sb("DA", TILES * HEADS)
        PROB = sb("PROB", TILES)
        POS = sb("POS", TILES, U32)
        EXPERT_OF = sb("EXPERT_OF", NT + 1, I32)
        VARS = sb("VARS", TILES)
        RNORM = sb("RNORM", TILES)
        MHALF = sb("MHALF", TILES)
        EA = sb("EA", HEADS)
        ZERO = sb("ZERO", DM)[:, :]
        ARENA_COLS = 37700
        ARENA = sb("ARENA", ARENA_COLS)
        EARLY = 0
        WEXP = ARENA[:, 0:EXPERTS * WE].rearrange("p (e c) -> p e c", e=EXPERTS)
        place = [EARLY * WE]

        def part(cols):
            at = place[0]
            place[0] += cols
            assert place[0] <= ARENA_COLS, place[0]
            return ARENA[:, at:at + cols]

        X = part(TILES * DM).rearrange("p (t d) -> p t d", d=DM)
        XNS = part(GT * DM).rearrange("p (c d) -> p c d", c=GT)
        XTS = part(GT * DM).rearrange("p (c k t) -> p c k t", c=GT, k=DK)
        STATS = part(TILES * 6).rearrange("p (t s) -> p t s", t=TILES)
        MV = part(TILES * 2).rearrange("p (t s) -> p t s", t=TILES)
        VE = part(TILES)
        RS = part(TILES)
        DTR = part(TILES * RW)
        SP_V = part(TILES * HEADS)
        SP_U = part(TILES * HEADS)
        SP_W = part(TILES * HEADS)
        SP_P = part(TILES * HEADS)
        TE = TILES * EXPERTS
        SIG, R1, R2, HOT, RANK, TOTS = (part(TE) for _ in range(6))
        CUM = [part(TE), part(TE)]
        IOTA, IOTAF = part(EXPERTS), part(EXPERTS)
        IOTAT, IOTATF = part(NT * EXPERTS), part(NT * EXPERTS)
        FIRST = part(TILES)
        CNTI, CNTS = part(EXPERTS).bitcast(I32), part(EXPERTS).bitcast(I32)
        CNTF, BASE128 = part(EXPERTS), part(EXPERTS)
        ENDS = [part(EXPERTS), part(EXPERTS)]
        LE = part(NT * EXPERTS)
        EXF = part(NT)
        POSF = part(TILES)
        first_end = place[0]

        place[0] = EARLY * WE
        RAW = [part(KC - 1 + GW) for _ in range(2)]
        HIST = [part(XB * (KC - 1)).rearrange("p (b j) -> p b j", b=XB) for _ in range(2)]
        ACC = [part(GW) for _ in range(2)]
        TH = [part(GW) for _ in range(2)]
        GRAW = [part(GW) for _ in range(2)]
        XBC = [part(XB * GW).rearrange("p (b t) -> p b t", b=XB) for _ in range(QB)]
        GATE = [part(HB * GW).rearrange("p (b t) -> p b t", b=HB) for _ in range(QB)]
        XS = part(SLOTS * DIN).rearrange("p (l c) -> p l c", l=SLOTS)
        E = [part(SLOTS * P).rearrange("p (l r h) -> p l r h", l=SLOTS, r=2) for _ in range(2)]
        EST = [part(2 * HEADS).rearrange("p (l h) -> p l h", l=2) for _ in range(2)]
        E2 = [part(SLOTS * HEADS).rearrange("p (l h) -> p l h", l=SLOTS) for _ in range(2)]
        GM = [part(LEVELS * P).rearrange("p (l t) -> p l t", l=LEVELS) for _ in range(2)]
        GD = part(2)
        GJUNK = part(P)
        W0 = [part(P) for _ in range(2)]
        ET = [part((SLOTS + 1) * P).rearrange("p (l t) -> p l t", l=SLOTS + 1) for _ in range(2)]
        Y = part(DIN).rearrange("p (b t) -> p b t", b=HB)
        PR = [part(DIN) for _ in range(3)]
        HG = [part(DIN).rearrange("p (b t) -> p b t", b=HB) for _ in range(2)]
        SQ = [part(DIN).rearrange("p (b t) -> p b t", b=HB) for _ in range(2)]
        S = part(DIN)
        S1 = part(DIN)
        BT = [part(P) for _ in range(2)]
        XT = [part(DIN) for _ in range(2)]
        O = [part(DM) for _ in range(2)]
        mixer_end = place[0]
        place[0] = max(mixer_end, first_end)
        XN = part(TILES * DM)

        place[0] = EXPERTS * WE
        FX = [part(DM) for _ in range(2)]
        FXT = [part(DM).rearrange("p (k t) -> p k t", k=DK) for _ in range(2)]
        FT = [part(DFF) for _ in range(2)]
        FG = [part(DFF) for _ in range(2)]
        FH = [part(DFF) for _ in range(2)]
        FHT = [part(DFF).rearrange("p (k t) -> p k t", k=KF) for _ in range(2)]
        FY = [part(DM) for _ in range(2)]
        ZX = part(TILES * DM)
        ZO = XNT.rearrange("p k t -> p (k t)")
        place[0] = 0
        ZF = part(TILES * DM)
        ZT = [part(GT * DM) for _ in range(2)]

        BA = [ctx.enter_context(nc.psum_tensor(f"BA{i}", [P, 512], FP32)) for i in range(RING)]
        BD = [ctx.enter_context(nc.psum_tensor(f"BD{i}", [P, 512], FP32)) for i in range(RING)]

        def sems(names):
            return [sem(n) for n in names.split()]

        a_written, a_moved, d_written, d_moved = sems("a_written a_moved d_written d_moved")
        dve_chain, pool_chain, act_chain = sems("dve_chain pool_chain act_chain")
        x_loaded = [sem(f"x_loaded{g}") for g in range(GROUPS)]
        consts_in, w_loaded, iota_made, zero_made, slots_zeroed = sems(
            "consts_in w_loaded iota_made zero_made slots_zeroed")
        var_ready, rstd_ready, xn_ready, xn_kept = sems("var_ready rstd_ready xn_ready xn_kept")
        abs_ready, u_ready, ea_ready, da_ready, sig_ready, hot_ready = sems(
            "abs_ready u_ready ea_ready da_ready sig_ready hot_ready")
        v_ready, rank_written, routed, scattered, w_out_scaled = sems(
            "v_ready rank_written routed scattered w_out_scaled")
        conv_done, taps_done, tanh_done, hist_zero, state_zero = sems(
            "conv_done taps_done tanh_done hist_zero state_zero")
        e2_ready, x_scaled, s1_ready, y0_ready = sems("e2_ready x_scaled s1_ready y0_ready")
        w0_ready, hg_ready, sq_ready, p_chain, y_chain = sems("w0_ready hg_ready sq_ready p_chain y_chain")
        conv_chain, gd_ready = sems("conv_chain gd_ready")
        o_stored = sems("o_stored0 o_stored1")
        late_loaded = sem("late_loaded")
        fx_loaded = sems("fx_loaded0 fx_loaded1")
        fy_stored = sems("fy_stored0 fy_stored1")
        fxt_full, fxt_ready, fg_full, fu_full, ft_ready, fa_ready, fh_ready, fht_full, fht_ready, fy_full, fy_ready = sems(
            "fxt_full fxt_ready fg_full fu_full ft_ready fa_ready fh_ready fht_full fht_ready fy_full fy_ready")
        zx_loaded, zo_loaded, rn_var, rn_ready, zo_scaled, z_made, zt_ready, z_out, z_stored = sems(
            "zx_loaded zo_loaded rn_var rn_ready zo_scaled z_made zt_ready z_out z_stored")
        gathered = [sem(f"gathered{g}") for g in range(GROUPS)]

        block = ctx.enter_context(nc.Block())

        def ident():
            return CONST[:, C_ID, :]

        def odd(ap, lev):
            m = 1 << lev
            if len(ap.shape) == 2:
                return ap.rearrange("p (q o m) -> p q o m", o=2, m=m)[:, :, 1, :]
            return ap.rearrange("p b (q o m) -> p b q o m", o=2, m=m)[:, :, :, 1, :]

        BX, BG, BU, BH = ([BA[0], BD[0]], [BA[1], BD[1]], [BA[2], BD[2]], [BA[3], BD[3]])
        WEXP_FLAT = ARENA[:, 0:EXPERTS * WE]
        BLOCKS = HB + XB
        head_a = {u: a for kind, u, _, a, _ in STEPS if kind == "head"}
        mid_d = {u: d for kind, u, _, _, d in STEPS if kind == "mid"}
        tail_a = {u: a for kind, u, _, a, _ in STEPS if kind == "tail"}
        conv_a = {(q, i): a for kind, q, i, a, _ in STEPS if kind == "conv"}
        Z_CHUNKS = (LEVELS + 1) // 2
        OFF, NEW = Z_CHUNKS, Z_CHUNKS + 1

        def a_no(b, i):
            return b * A_BATCH + (A_P1 + i)

        def d_no(b, i):
            return b * D_BATCH + (D_BASE + i)

        def before(at, per_batch, u, back):
            return at[u - back] if u >= back else at[u - back + TB] - per_batch

        def cols_of(u):
            return slice((u % GT) * P, (u % GT + 1) * P)

        def heads_of(ap, b, u):
            return ap[:, bass.ds(b * (TB * HEADS) + u * HEADS, HEADS)]

        @block.sync
        def _(sp):
            for g in range(GROUPS):
                sp.dma_start(X[:, g * GT:(g + 1) * GT, :],
                             x_dram[:, g * GT:(g + 1) * GT, :]).then_inc(x_loaded[g], 16)
            sp.dma_start(CONST, consts.rearrange("p (m t) -> p m t", m=N_CONST)).then_inc(consts_in, 16)
            sp.dma_start(W_DR, w_dr.rearrange("(k p) n -> p k n", p=P)).then_inc(consts_in, 16)
            sp.dma_start(HEADV[:, :], head_v[0:1, :].to_broadcast([P, 3 * HEADS])).then_inc(consts_in, 16)
            sp.dma_start(CONVC, conv_c.rearrange("p (b j) -> p b j", j=KC + 1)).then_inc(consts_in, 16)
            sp.dma_start(NORMC[:, :], norm_c).then_inc(consts_in, 16)
            sp.dma_start(W_OUT, w_out.rearrange("(b p) n -> p b n", p=P)).then_inc(consts_in, 16)
            sp.dma_start(W_MAIN, w_main.rearrange("(k p) n -> p k n", p=P)).then_inc(w_loaded, 16)
            sp.wait_ge(zero_made, 1)
            sp.dma_start(xs_tiles, ZERO.unsqueeze(1).to_broadcast([P, NT, DM])).then_inc(slots_zeroed, 16)

            def load_expert(e, signal):
                sp.dma_start(WEXP[:, e, 0:DK * DFF].rearrange("p (k n) -> p k n", k=DK),
                             w_gate[e].rearrange("(k p) n -> p k n", p=P)).then_inc(signal, 16)
                sp.dma_start(WEXP[:, e, DK * DFF:2 * DK * DFF].rearrange("p (k n) -> p k n", k=DK),
                             w_up[e].rearrange("(k p) n -> p k n", p=P)).then_inc(signal, 16)
                sp.dma_start(WEXP[:, e, 2 * DK * DFF:].rearrange("p (k n) -> p k n", k=KF),
                             w_down[e].rearrange("(k p) n -> p k n", p=P)).then_inc(signal, 16)

            for e in range(EARLY):
                load_expert(e, late_loaded)
            for par in range(2):
                sp.sem_inc(o_stored[par], 16)
            with sp.Fori(0, BATCH) as b:
                for u in range(TB):
                    sp.wait_ge(a_moved, a_no(b, tail_a[u]) + (RING + 1))
                    sp.dma_start(o_tiles[:, bass.ds(b * TB + u, 1), :],
                                 O[u % 2].unsqueeze(1)).then_inc(o_stored[u % 2], 16)
            for par in range(2):
                sp.wait_ge(o_stored[par], 16 + 16 * (TILES // 2))
            sp.wait_ge(scattered, 16 * TILES)
            for e in range(EARLY, EXPERTS):
                load_expert(e, late_loaded)
            for k in range(2):
                sp.dma_start(FX[k].unsqueeze(1), xs_tiles[:, k:k + 1, :]).then_inc(fx_loaded[k], 16)
            sp.dma_start(ZO.rearrange("p (t d) -> p t d", d=DM), o_tiles).then_inc(zo_loaded, 16)
            sp.dma_start(ZX.rearrange("p (t d) -> p t d", d=DM), x_dram).then_inc(zx_loaded, 16)
            for par in range(2):
                sp.sem_inc(fy_stored[par], 16)

            def load_x(k, par):
                sp.wait_ge(fxt_full, k - 1)
                sp.dma_start(FX[par].unsqueeze(1), xs_tiles[:, bass.ds(k, 1), :]).then_inc(fx_loaded[par], 16)

            def store_y(k, par):
                sp.wait_ge(fy_ready, k + 3)
                sp.dma_start(ys_tiles[:, bass.ds(k, 1), :], FY[par].unsqueeze(1)).then_inc(fy_stored[par], 16)

            with sp.Fori(0, (NT - 3) // 2) as i:
                for par in range(2):
                    load_x(i * 2 + (2 + par), par)
                    store_y(i * 2 + par, par)
            load_x(NT - 1, (NT - 1) % 2)
            for k in range(NT - 3, NT):
                store_y(k, k % 2)
            for g in range(GROUPS):
                sp.wait_ge(z_out, g + 1)
                sp.dma_start(out_dram[:, g * GT:(g + 1) * GT, :],
                             ZX[:, g * GT * DM:(g + 1) * GT * DM].rearrange("p (t d) -> p t d", d=DM)).then_inc(z_stored, 16)
            sp.wait_ge(z_stored, 16 * GROUPS)

        @block.gpsimd
        def _(pool):
            nc.gpsimd.memset(ZERO, 0.0).then_inc(zero_made, 1)
            nc.gpsimd.memset(MHALF[:, :], -0.5)
            nc.gpsimd.iota(IOTA.bitcast(I32), pattern=[[1, EXPERTS]], base=-EXPERTS,
                           channel_multiplier=0)
            nc.gpsimd.iota(IOTAT.bitcast(I32).rearrange("p (t e) -> p t e", e=EXPERTS),
                           pattern=[[1, NT], [0, EXPERTS]], base=0, channel_multiplier=0).then_inc(iota_made, 1)
            pool.wait_ge(iota_made, 1)
            pool.sem_inc(xn_kept, 1)
            with pool.Fori(0, GROUPS) as g:
                pool.wait_ge(var_ready, g + 1)
                nc.gpsimd.tensor_tensor(out=RS[:, bass.ds(g * GT, GT)], in0=VE[:, bass.ds(g * GT, GT)],
                                        in1=MHALF[:, 0:GT], op=ALU.pow).then_inc(rstd_ready, 1)
                pool.wait_ge(xn_ready, g + 1)
                nc.gpsimd.tensor_copy(XN[:, bass.ds(g * (GT * DM), GT * DM)],
                                      XNS.rearrange("p c d -> p (c d)")).then_inc(xn_kept, 1)
            pool.wait_ge(routed, 1)
            pool.wait_ge(slots_zeroed, 16)
            pool.wait_ge(xn_kept, 1 + GROUPS)
            for t in range(TILES):
                pool.indirect_dma_start(
                    out=xs_dram, out_offset=bass.IndirectOffsetOnAxis(ap=POS[:, t:t + 1], axis=0),
                    in_=XN[:, t * DM:(t + 1) * DM], in_offset=None).then_inc(scattered, 16)
            pool.sem_inc(e2_ready, 4)
            pool.sem_inc(s1_ready, 2)

            with pool.Fori(0, BATCH) as b:
                pool.wait_ge(d_moved, d_no(b, 0) + RING)
                pool.wait_ge(da_ready, 1)
                zero = ZERO.unsqueeze(1).to_broadcast([P, DIN // DM, DM])
                nc.gpsimd.tensor_tensor(out=S.rearrange("p (r d) -> p r d", d=DM), in0=zero, in1=zero,
                                        op=ALU.add).then_inc(state_zero, 1)
                nc.gpsimd.tensor_copy(HIST[1].rearrange("p b j -> p (b j)"), ZERO[:, 0:XB * (KC - 1)]).then_inc(hist_zero, 1)
                for kind, u, _, a0, d0 in STEPS:
                    if kind != "mid":
                        continue
                    par, q, tile = u % 2, u // GT, b * TB + u
                    dt = heads_of(DT, b, u)
                    pool.wait_ge(a_moved, a_no(b, head_a[u] + 1) + (RING + 1))
                    nc.gpsimd.tensor_tensor(
                        out=E2[par][:, 0:LEVELS, :], in0=E[par][:, 0:LEVELS, 0, :],
                        in1=dt.unsqueeze(1).to_broadcast([P, LEVELS, HEADS]), op=ALU.mult).then_inc(e2_ready, 1)
                    nc.gpsimd.tensor_tensor(out=E2[par][:, LEVELS, :], in0=EST[par][:, SUF, :], in1=dt,
                                            op=ALU.mult).then_inc(e2_ready, 1)
                    pool.wait_ge(e2_ready, tile * 2 + (4 + 2))
                    pool.wait_ge(a_moved, a_no(b, head_a[u] + 2) + (RING + 1))
                    for lev in range(SLOTS):
                        if lev == 2:
                            pool.wait_ge(a_moved, a_no(b, a0 + 2) + (RING + 1))
                            pool.wait_ge(hg_ready, tile + 2)
                            nc.gpsimd.tensor_tensor(
                                out=Y, in0=XBC[q][:, 0:HB, cols_of(u)],
                                in1=ET[par][:, SLOTS, :].unsqueeze(1).to_broadcast([P, HB, P]),
                                op=ALU.mult).then_inc(y0_ready, 1)
                        chunk = lev // 2 if lev < LEVELS else NEW
                        pool.wait_ge(d_moved, d_no(b, before(mid_d, D_BATCH, u, 1) + chunk) + (RING + 1))
                        nc.gpsimd.tensor_tensor(
                            out=XS[:, lev, :].rearrange("p (a h) -> p a h", a=HD),
                            in0=E2[par][:, lev, :].unsqueeze(1).to_broadcast([P, HD, HEADS]),
                            in1=XT[par].rearrange("p (a h) -> p a h", a=HD), op=ALU.mult).then_inc(x_scaled, 1)
                    if u == 0:
                        pool.wait_ge(state_zero, b + 1)
                    nc.gpsimd.tensor_tensor(
                        out=S1.rearrange("p (a h) -> p a h", a=HD), in0=S.rearrange("p (a h) -> p a h", a=HD),
                        in1=EST[par][:, TOT, :].unsqueeze(1).to_broadcast([P, HD, HEADS]),
                        op=ALU.mult).then_inc(s1_ready, 1)

            pool.wait_ge(rn_var, 1)
            nc.gpsimd.tensor_tensor(out=RNORM[:, :], in0=RNORM[:, :], in1=MHALF[:, :], op=ALU.pow).then_inc(rn_ready, 1)
            pool.wait_ge(rn_ready, 1)
            pool.wait_ge(zo_loaded, 16)
            nc.gpsimd.tensor_tensor(
                out=ZO.rearrange("p (t d) -> p t d", d=DM), in0=ZO.rearrange("p (t d) -> p t d", d=DM),
                in1=RNORM[:, :].unsqueeze(2).to_broadcast([P, TILES, DM]), op=ALU.mult).then_inc(zo_scaled, 1)
            for par in range(2):
                pool.wait_ge(fy_stored[par], 16 + 16 * ((NT + 1 - par) // 2))
            for t in range(TILES):
                pool.indirect_dma_start(
                    out=ZF[:, t * DM:(t + 1) * DM], out_offset=None, in_=ys_dram,
                    in_offset=bass.IndirectOffsetOnAxis(ap=POS[:, t:t + 1], axis=0)).then_inc(gathered[t // GT], 16)

        @block.scalar
        def _(act):
            act.sem_inc(a_moved, RING)
            with act.Fori(0, GROUPS) as g:
                for h in range(2):
                    act.wait_ge(a_written, g * 4 + (h + 1))
                    nc.scalar.activation(XTS[:, 2 * h:2 * h + 2, :, :],
                                         BA[h][:, :].rearrange("p (c k t) -> p c k t", c=2, k=DK), ACT.Copy)
                    for c in range(2):
                        ins = nc.scalar.activation(
                            XNT[:, :, bass.ds(g * GW + (2 * h + c) * P, P)],
                            BA[h][:, c * DM:(c + 1) * DM].rearrange("p (k t) -> p k t", k=DK), ACT.Copy)
                    ins.then_inc(a_moved, 1)
                for h in range(2):
                    act.wait_ge(a_written, g * 4 + (2 + h + 1))
                    nc.scalar.activation(DTR[:, bass.ds(g * (GT * RW) + 2 * h * RW, 2 * RW)],
                                         BA[2 + h][:, 0:2 * RW], ACT.Copy).then_inc(a_moved, 1)
            act.wait_ge(consts_in, 16 * 6)
            nc.scalar.activation(EA[:, :], HEADV[:, V_ALOG:V_ALOG + HEADS], ACT.Exp).then_inc(ea_ready, 1)
            act.wait_ge(a_moved, RING + A_P1)
            nc.scalar.activation(SIG.rearrange("p (t e) -> p t e", e=EXPERTS),
                                 DTR.rearrange("p (t c) -> p t c", c=RW)[:, :, HEADS:], ACT.Exp,
                                 scale=-1.0).then_inc(sig_ready, 1)
            act.wait_ge(v_ready, 1)
            nc.scalar.activation(SP_U, SP_V, ACT.Abs).then_inc(abs_ready, 1)
            act.wait_ge(abs_ready, 1)
            nc.scalar.activation(SP_U, SP_U, ACT.Exp, scale=-1.0).then_inc(u_ready, 1)
            act.wait_ge(da_ready, 1)
            act.wait_ge(routed, 1)
            act.wait_ge(xn_kept, 1 + GROUPS)

            def conv_block(b, q, i, a0):
                par, blk = i % 2, i - HB
                bank = BA[a0 % RING]
                act.wait_ge(a_written, a_no(b, a0) + 1)
                act.wait_ge(conv_done, b * (QB * BLOCKS) + (q * BLOCKS + i + 1))
                if i < HB:
                    nc.scalar.activation(TH[par], bank[:, :], ACT.Tanh, scale=0.5)
                    nc.scalar.activation(GRAW[par], bank[:, :], ACT.Copy).then_inc(a_moved, 1)
                    return
                if q == 0:
                    act.wait_ge(hist_zero, b + 1)
                else:
                    act.wait_ge(a_moved, a_no(b, conv_a[0, i]) + (RING + 1))
                nc.scalar.activation(RAW[par][:, 0:KC - 1], HIST[1 - q][:, blk, :], ACT.Copy)
                nc.scalar.activation(RAW[par][:, KC - 1:], bank[:, :], ACT.Copy)
                nc.scalar.activation(ACC[par], bank[:, :], ACT.Identity, scale=CONVC[:, blk, KC - 1:KC],
                                     bias=CONVC[:, blk, KC:KC + 1])
                nc.scalar.activation(HIST[q][:, blk, :], bank[:, GW - (KC - 1):GW], ACT.Copy).then_inc(a_moved, 1)

            def conv_tanh(b, q, i):
                act.wait_ge(taps_done, b * (QB * XB) + (q * XB + i - HB + 1))
                nc.scalar.activation(TH[i % 2], ACC[i % 2], ACT.Tanh).then_inc(tanh_done, 1)

            with act.Fori(0, BATCH) as b:
                for kind, u, i, a0, d0 in STEPS:
                    par, tile = u % 2, b * TB + u
                    if kind == "conv":
                        conv_block(b, u, i, a0)
                        if i > HB:
                            conv_tanh(b, u, i - 1)
                        if i == BLOCKS - 1:
                            conv_tanh(b, u, i)
                    if kind == "head":
                        act.wait_ge(s1_ready, tile + 1)
                        act.wait_ge(a_written, a_no(b, a0) + 1)
                        nc.scalar.activation(
                            E[par], BA[a0 % RING][:, :].rearrange("p (l h) -> p l h", h=HEADS).unsqueeze(2)
                            .to_broadcast([P, SLOTS, 2, HEADS]), ACT.Exp).then_inc(a_moved, 1)
                        act.wait_ge(a_written, a_no(b, a0 + 1) + 1)
                        bank = BA[(a0 + 1) % RING]
                        nc.scalar.activation(EST[par], bank[:, 0:P].rearrange("p (l h) -> p l h", l=2), ACT.Exp)
                        nc.scalar.activation(BT[par], bank[:, P:2 * P], ACT.Copy).then_inc(a_moved, 1)
                        act.wait_ge(a_written, a_no(b, a0 + 2) + 1)
                        nc.scalar.activation(XT[par], BA[(a0 + 2) % RING][:, :], ACT.Copy).then_inc(a_moved, 1)
                    if kind == "mid":
                        act.wait_ge(hg_ready, tile + 1)
                        for j in range(2):
                            act.wait_ge(a_written, a_no(b, a0 + j) + 1)
                            nc.scalar.activation(ET[par][:, 4 * j:4 * j + 4, :],
                                                 BA[(a0 + j) % RING][:, :].rearrange("p (l t) -> p l t", l=4),
                                                 ACT.Copy).then_inc(a_moved, 1)
                        act.wait_ge(a_written, a_no(b, a0 + 2) + 1)
                        nc.scalar.activation(ET[par][:, SLOTS, :], BA[(a0 + 2) % RING][:, 0:P],
                                             ACT.Copy).then_inc(a_moved, 1)
                    if kind == "tail":
                        act.wait_ge(hg_ready, tile + 3)
                        nc.scalar.activation(SQ[par], HG[par], ACT.Square).then_inc(sq_ready, 1)
                        act.wait_ge(a_written, a_no(b, a0) + 1)
                        act.wait_ge(o_stored[par], b * (8 * TB) + (16 * (u // 2) + 16))
                        nc.scalar.activation(VARS[:, bass.ds(tile, 1)], BA[a0 % RING][:, DM:DM + 1], ACT.Copy)
                        nc.scalar.activation(O[par], BA[a0 % RING][:, 0:DM], ACT.Copy).then_inc(a_moved, 1)

            act.sem_inc(fy_ready, 2)

            def front(k, par):
                act.wait_ge(fxt_full, k + 1)
                nc.scalar.activation(FXT[par], BX[par][:, 0:DM].rearrange("p (k t) -> p k t", k=DK),
                                     ACT.Copy).then_inc(fxt_ready, 1)
                act.wait_ge(fg_full, k + 1)
                nc.scalar.activation(FT[par], BG[par][:, :], ACT.Tanh, scale=0.5)
                nc.scalar.activation(FG[par], BG[par][:, :], ACT.Copy).then_inc(ft_ready, 1)

            def back(k, par):
                act.wait_ge(fht_full, k + 1)
                nc.scalar.activation(FHT[par], BH[par][:, :].rearrange("p (k t) -> p k t", k=KF),
                                     ACT.Copy).then_inc(fht_ready, 1)
                act.wait_ge(fy_full, k + 1)
                act.wait_ge(fy_stored[par], (k - par) * 8 + 16)
                nc.scalar.activation(FY[par], BX[par][:, DM:2 * DM], ACT.Copy).then_inc(fy_ready, 1)

            front(0, 0)
            with act.Fori(0, (NT - 1) // 2) as i:
                front(i * 2 + 1, 1)
                back(i * 2, 0)
                front(i * 2 + 2, 0)
                back(i * 2 + 1, 1)
            back(NT - 1, (NT - 1) % 2)
            for g in range(GROUPS):
                act.wait_ge(z_made, g + 1)
                nc.scalar.activation(ZT[g % 2], ZF[:, g * GT * DM:(g + 1) * GT * DM], ACT.Tanh,
                                     scale=0.5).then_inc(zt_ready, 1)

        @block.tensor
        def _(pe):
            pe.wait_ge(consts_in, 16 * 6)
            with pe.Fori(0, GROUPS) as g:
                for h in range(2):
                    pe.wait_ge(a_moved, g * 4 + (h + 1))
                    pe.wait_ge(xn_ready, g + 1)
                    for c in range(2):
                        for k in range(DK):
                            ins = nc.tensor.transpose(BA[h][:, c * DM + k * P:c * DM + (k + 1) * P],
                                                      XNS[:, 2 * h + c, k * P:(k + 1) * P], ident())
                    ins.then_inc(a_written, 1)
                for h in range(2):
                    pe.wait_ge(a_moved, g * 4 + (RING + h + 1))
                    for c in range(2):
                        for k in range(DK):
                            ins = nc.tensor.matmul(BA[2 + h][:, c * RW:(c + 1) * RW], lhsT=XTS[:, 2 * h + c, k, :],
                                                   rhs=W_DR[:, k, :], start=(k == 0), stop=(k == DK - 1))
                    ins.then_inc(a_written, 1)
            pe.wait_ge(hot_ready, 1)
            nc.tensor.matmul(BD[0][:, 0:TE], lhsT=CONST[:, C_TRI, :], rhs=HOT, start=True, stop=True)
            nc.tensor.matmul(BD[0][:, TE:2 * TE], lhsT=CONST[:, C_ONE, :], rhs=HOT, start=True,
                             stop=True).then_inc(rank_written, 1)
            pe.wait_ge(w_loaded, 16)
            pe.wait_ge(da_ready, 1)
            pe.wait_ge(w_out_scaled, 1)

            with pe.Fori(0, BATCH) as b:
                for kind, u, i, a0, d0 in STEPS:
                    par, tile, q = u % 2, b * TB + u, u // GT

                    def bank_a(j):
                        pe.wait_ge(a_moved, a_no(b, a0 + j) + 1)
                        return BA[(a0 + j) % RING]

                    def bank_d(j):
                        pe.wait_ge(d_moved, d_no(b, d0 + j) + 1)
                        return BD[(d0 + j) % RING]

                    if kind == "conv":
                        bank = bank_a(0)
                        for k in range(DK):
                            ins = nc.tensor.matmul(
                                bank[:, :], lhsT=W_MAIN[:, k, i * P:(i + 1) * P],
                                rhs=XNT[:, k, bass.ds(b * SEQ + u * GW, GW)], start=(k == 0), stop=(k == DK - 1))
                        ins.then_inc(a_written, 1)
                    if kind == "head":
                        bank = bank_a(0)
                        for lev in range(SLOTS):
                            ins = nc.tensor.matmul(bank[:, lev * HEADS:(lev + 1) * HEADS],
                                                   lhsT=CONST[:, C_LEV + lev, :], rhs=heads_of(DA, b, u),
                                                   start=True, stop=True)
                        ins.then_inc(a_written, 1)
                        pe.wait_ge(conv_done, b * (QB * BLOCKS) + (2 + (q + 1) * BLOCKS))
                        bank = bank_d(0)
                        nc.tensor.matmul(bank[:, 0:P], lhsT=XBC[q][:, HB, cols_of(u)],
                                         rhs=XBC[q][:, HB + 1, cols_of(u)], start=True, stop=True).then_inc(d_written, 1)
                        bank = bank_a(1)
                        for j, m in enumerate((C_SUF, C_ONE)):
                            nc.tensor.matmul(bank[:, j * HEADS:(j + 1) * HEADS], lhsT=CONST[:, m, :],
                                             rhs=heads_of(DA, b, u), start=True, stop=True)
                        nc.tensor.transpose(bank[:, P:2 * P], XBC[q][:, HB, cols_of(u)], ident()).then_inc(a_written, 1)
                        bank = bank_a(2)
                        for blk in range(HB):
                            ins = nc.tensor.transpose(bank[:, blk * P:(blk + 1) * P], XBC[q][:, blk, cols_of(u)], ident())
                        ins.then_inc(a_written, 1)
                    if kind == "mid":
                        pe.wait_ge(a_moved, a_no(b, head_a[u]) + (RING + 1))
                        for j in range(2):
                            bank = bank_a(j)
                            for lev in range(4 * j, 4 * j + 4):
                                ins = nc.tensor.transpose(bank[:, (lev - 4 * j) * P:(lev - 4 * j + 1) * P],
                                                          E[par][:, lev, :, :].rearrange("p r h -> p (r h)"), ident())
                            ins.then_inc(a_written, 1)
                        bank = bank_a(2)
                        pe.wait_ge(w0_ready, tile + 1)
                        nc.tensor.transpose(bank[:, 0:P], W0[par], ident()).then_inc(a_written, 1)
                        for lev in range(LEVELS):
                            if lev % 2 == 0:
                                bank = bank_d(lev // 2)
                            pe.wait_ge(x_scaled, tile * SLOTS + (lev + 1))
                            for blk in range(HB):
                                at = (lev % 2) * HB * 64 + blk * 64
                                ins = nc.tensor.matmul(bank[:, at:at + 64], lhsT=XS[:, lev, blk * P:(blk + 1) * P],
                                                       rhs=odd(GM[par][:, lev, :], lev), start=True, stop=True)
                            if lev % 2 == 1 or lev == LEVELS - 1:
                                ins.then_inc(d_written, 1)
                        bank = bank_d(OFF)
                        if u == 0:
                            pe.wait_ge(state_zero, b + 1)
                        else:
                            pe.wait_ge(d_moved, d_no(b, mid_d[u - 1] + NEW) + (RING + 1))
                        for blk in range(HB):
                            ins = nc.tensor.matmul(bank[:, blk * P:(blk + 1) * P], lhsT=S[:, blk * P:(blk + 1) * P],
                                                   rhs=XBC[q][:, HB + 1, cols_of(u)], start=True, stop=True)
                        ins.then_inc(d_written, 1)
                        bank = bank_d(NEW)
                        pe.wait_ge(x_scaled, (tile + 1) * SLOTS)
                        pe.wait_ge(a_moved, a_no(b, head_a[u] + 1) + (RING + 1))
                        nc.tensor.matmul(bank[:, :], lhsT=BT[par], rhs=XS[:, LEVELS, :], start=True,
                                         stop=True).then_inc(d_written, 1)
                    if kind == "tail":
                        bank = bank_a(0)
                        pe.wait_ge(hg_ready, tile + 3)
                        for blk in range(HB):
                            nc.tensor.matmul(bank[:, 0:DM], lhsT=HG[par][:, blk, :], rhs=W_OUT[:, blk, :],
                                             start=(blk == 0), stop=(blk == HB - 1))
                        pe.wait_ge(sq_ready, tile + 1)
                        for blk in range(HB):
                            ins = nc.tensor.matmul(bank[:, DM:DM + 1], lhsT=SQ[par][:, blk, :],
                                                   rhs=CONST[:, C_ONE, 0:1], start=(blk == 0), stop=(blk == HB - 1))
                        ins.then_inc(a_written, 1)

            pe.wait_ge(a_moved, RING + A_P1 + BATCH * A_BATCH)
            pe.wait_ge(d_moved, RING + D_BASE + BATCH * D_BATCH)

            def turn(k, par, loads):
                pe.wait_ge(fx_loaded[par], loads)
                for j in range(DK):
                    ins = nc.tensor.transpose(BX[par][:, j * P:(j + 1) * P], FX[par][:, j * P:(j + 1) * P], ident())
                ins.then_inc(fxt_full, 1)

            def gate_up(k, par):
                e = pe.value_load(EXPERT_OF[0:1, bass.ds(k, 1)], min_val=0, max_val=EXPERTS - 1)
                pe.wait_ge(fxt_ready, k + 1)
                for at, bank, full in ((0, BG[par], fg_full), (DK * DFF, BU[par], fu_full)):
                    for j in range(DK):
                        ins = nc.tensor.matmul(bank[:, :], lhsT=FXT[par][:, j, :],
                                               rhs=WEXP_FLAT[:, bass.ds(e * WE + (at + j * DFF), DFF)],
                                               start=(j == 0), stop=(j == DK - 1))
                    ins.then_inc(full, 1)

            def hidden(k, par):
                pe.wait_ge(fh_ready, k + 1)
                for j in range(KF):
                    ins = nc.tensor.transpose(BH[par][:, j * P:(j + 1) * P], FH[par][:, j * P:(j + 1) * P], ident())
                ins.then_inc(fht_full, 1)

            def down(k, par):
                e = pe.value_load(EXPERT_OF[0:1, bass.ds(k, 1)], min_val=0, max_val=EXPERTS - 1)
                pe.wait_ge(fht_ready, k + 1)
                pe.wait_ge(fy_ready, k + 1)
                for j in range(KF):
                    ins = nc.tensor.matmul(BX[par][:, DM:2 * DM], lhsT=FHT[par][:, j, :],
                                           rhs=WEXP_FLAT[:, bass.ds(e * WE + (2 * DK * DFF + j * DM), DM)],
                                           start=(j == 0), stop=(j == KF - 1))
                ins.then_inc(fy_full, 1)

            pe.wait_ge(late_loaded, 16 * 3 * EXPERTS)
            turn(0, 0, 16)
            gate_up(0, 0)
            with pe.Fori(0, (NT - 1) // 2) as i:
                for par in (1, 0):
                    k = i * 2 + (2 - par)
                    pe.wait_ge(fy_ready, k + 1)
                    turn(k, par, i * 16 + (16 if par else 32))
                    gate_up(k, par)
                    hidden(k - 1, 1 - par)
                    down(k - 1, 1 - par)
            hidden(NT - 1, (NT - 1) % 2)
            down(NT - 1, (NT - 1) % 2)

        @block.vector
        def _(dve):
            chain = [0]

            def link(ins):
                chain[0] += 1
                ins.then_inc(dve_chain, 1)
                dve.wait_ge(dve_chain, chain[0])

            def tt(out, a, b, op):
                return nc.vector.tensor_tensor(out=out, in0=a, in1=b, op=op)

            dve.sem_inc(d_moved, RING + D_BASE)
            dve.sem_inc(conv_done, 2)
            dve.sem_inc(hg_ready, 2)

            def variances(g):
                tiles = range(g * GT, (g + 1) * GT)
                dve.wait_ge(x_loaded[g], 16)
                for t in tiles:
                    nc.vector.bn_stats(STATS[:, t, :], X[:, t, :]).then_inc(dve_chain, 1)
                for t in tiles:
                    chain[0] += 1
                    dve.wait_ge(dve_chain, chain[0])
                    nc.vector.bn_aggr(MV[:, t, :], STATS[:, t, :]).then_inc(dve_chain, 1)
                chain[0] += GT
                dve.wait_ge(dve_chain, chain[0])
                nc.vector.tensor_scalar_add(VE[:, g * GT:(g + 1) * GT].unsqueeze(2), MV[:, g * GT:(g + 1) * GT, 1:2],
                                            EPS).then_inc(var_ready, 1)

            variances(0)
            for g in range(GROUPS):
                if g + 1 < GROUPS:
                    variances(g + 1)
                dve.wait_ge(rstd_ready, g + 1)
                if g > 0:
                    dve.wait_ge(xn_kept, g + 1)
                    dve.wait_ge(a_moved, g * 4 + 2)
                for c in range(GT):
                    t = g * GT + c
                    ins = nc.vector.tensor_scalar(XNS[:, c, :], X[:, t, :], MV[:, t, 0:1], RS[:, t:t + 1],
                                                  ALU.subtract, ALU.mult)
                ins.then_inc(xn_ready, 1)

            def by_expert(ap):
                return ap.rearrange("p (t e) -> p t e", e=EXPERTS)

            def over_tiles(ap):
                return ap.unsqueeze(1).to_broadcast([P, TILES, EXPERTS])

            def over_experts(ap):
                return ap.unsqueeze(2).to_broadcast([P, TILES, EXPERTS])

            dve.wait_ge(iota_made, 1)
            link(nc.vector.tensor_copy(IOTAF, IOTA.bitcast(I32)))
            link(nc.vector.tensor_copy(IOTATF, IOTAT.bitcast(I32)))
            dve.wait_ge(sig_ready, 1)
            link(nc.vector.tensor_scalar_add(SIG, SIG, 1.0))
            link(nc.vector.reciprocal(SIG, SIG))
            link(nc.vector.reduce_max(PROB[:, :], by_expert(SIG), AX.X))
            link(tt(by_expert(R1), by_expert(SIG), over_experts(PROB[:, :]), ALU.is_equal))
            link(tt(by_expert(R2), by_expert(R1), over_tiles(IOTAF), ALU.mult))
            link(nc.vector.tensor_reduce(FIRST, by_expert(R2), AX.X, ALU.min))
            tt(by_expert(HOT), over_tiles(IOTAF), over_experts(FIRST), ALU.is_equal).then_inc(hot_ready, 1)
            dve.wait_ge(a_moved, RING + A_P1)
            by_head = DTR.rearrange("p (t c) -> p t c", c=RW)[:, :, 0:HEADS]
            V = SP_V.rearrange("p (t h) -> p t h", h=HEADS)
            tt(V, by_head, HEADV[:, V_BIAS:V_BIAS + HEADS].unsqueeze(1).to_broadcast([P, TILES, HEADS]),
               ALU.add).then_inc(v_ready, 1)
            dve.wait_ge(rank_written, 1)
            nc.vector.tensor_copy(RANK, BD[0][:, 0:TE])
            nc.vector.tensor_copy(TOTS, BD[0][:, TE:2 * TE])
            link(nc.vector.tensor_copy(CUM[0], BD[0][:, TE:2 * TE]))
            src, step = 0, 1
            while step < TILES:
                n = step * EXPERTS
                nc.vector.tensor_copy(CUM[1 - src][:, 0:n], CUM[src][:, 0:n])
                link(tt(CUM[1 - src][:, n:], CUM[src][:, n:], CUM[src][:, 0:TE - n], ALU.add))
                src, step = 1 - src, step * 2
            count = CUM[src][:, TE - EXPERTS:]
            link(nc.vector.tensor_scalar_add(CNTI, count, float(P - 1)))
            link(nc.vector.tensor_single_scalar(CNTS, CNTI, P.bit_length() - 1, ALU.logical_shift_right))
            nc.vector.tensor_copy(CNTF, CNTS)
            link(nc.vector.tensor_copy(ENDS[0], CNTS))
            esrc, step = 0, 1
            while step < EXPERTS:
                nc.vector.tensor_copy(ENDS[1 - esrc][:, 0:step], ENDS[esrc][:, 0:step])
                link(tt(ENDS[1 - esrc][:, step:], ENDS[esrc][:, step:], ENDS[esrc][:, 0:EXPERTS - step], ALU.add))
                esrc, step = 1 - esrc, step * 2
            ends = ENDS[esrc]
            link(tt(LE.rearrange("p (t e) -> p t e", e=EXPERTS), ends.unsqueeze(1).to_broadcast([P, NT, EXPERTS]),
                    IOTATF.rearrange("p (t e) -> p t e", e=EXPERTS), ALU.is_le))
            link(nc.vector.reduce_sum(EXF, LE.rearrange("p (t e) -> p t e", e=EXPERTS)[:, :, 0:EXPERTS - 1], AX.X))
            nc.vector.tensor_copy(EXPERT_OF[:, 0:NT], EXF)
            link(tt(BASE128, ends, CNTF, ALU.subtract))
            link(nc.vector.tensor_scalar(BASE128, BASE128, float(P), None, ALU.mult))
            link(tt(R1, RANK, CUM[src], ALU.add))
            link(tt(R1, R1, TOTS, ALU.subtract))
            link(tt(by_expert(R1), by_expert(R1), over_tiles(BASE128), ALU.add))
            link(tt(R1, R1, HOT, ALU.mult))
            link(nc.vector.reduce_sum(POSF, by_expert(R1), AX.X))
            nc.vector.tensor_copy(POS[:, :], POSF).then_inc(routed, 1)

            dve.wait_ge(u_ready, 1)
            link(nc.vector.tensor_scalar_add(SP_W, SP_U, -0.5))
            link(nc.vector.tensor_scalar(SP_P, SP_W, COEF[-1], COEF[-2], ALU.mult, ALU.add))
            link(tt(SP_P, SP_P, SP_W, ALU.mult))
            for c in COEF[-3:0:-1]:
                link(nc.vector.scalar_tensor_tensor(out=SP_P, in0=SP_P, scalar=c, in1=SP_W, op0=ALU.add, op1=ALU.mult))
            link(nc.vector.scalar_tensor_tensor(out=SP_P, in0=SP_P, scalar=COEF[0], in1=SP_U, op0=ALU.add, op1=ALU.mult))
            link(nc.vector.scalar_tensor_tensor(out=DT[:, :], in0=SP_V, scalar=0.0, in1=SP_P, op0=ALU.max, op1=ALU.add))
            dve.wait_ge(ea_ready, 1)
            link(nc.vector.tensor_scalar(CONVC, CONVC, 0.5, None, ALU.mult))
            for blk in range(HB):
                ins = nc.vector.tensor_scalar(W_OUT[:, blk, :], W_OUT[:, blk, :], NORMC[:, blk:blk + 1], None, ALU.mult)
            ins.then_inc(w_out_scaled, 1)
            nc.vector.scalar_tensor_tensor(
                out=DA[:, :].rearrange("p (t h) -> p t h", h=HEADS), in0=DT[:, :].rearrange("p (t h) -> p t h", h=HEADS),
                scalar=-1.0, in1=EA[:, :].unsqueeze(1).to_broadcast([P, TILES, HEADS]), op0=ALU.mult,
                op1=ALU.mult).then_inc(da_ready, 1)

            def taps(b, q, i):
                par, blk = i % 2, i - HB
                dve.wait_ge(a_moved, a_no(b, conv_a[q, i]) + (RING + 1))
                for j in range(KC - 2, -1, -1):
                    ins = nc.vector.scalar_tensor_tensor(out=ACC[par], in0=RAW[par][:, j:j + GW],
                                                         scalar=CONVC[:, blk, j:j + 1], in1=ACC[par],
                                                         op0=ALU.mult, op1=ALU.add)
                    if j > 0:
                        ins.then_inc(conv_chain, 1)
                        dve.wait_ge(conv_chain, b * (QB * XB * 2) + ((q * XB + blk) * 2 + (KC - 1 - j)))
                ins.then_inc(taps_done, 1)

            def conv_silu(b, q, i):
                dve.wait_ge(tanh_done, b * (QB * XB) + (q * XB + i - HB + 1))
                nc.vector.scalar_tensor_tensor(out=XBC[q][:, i - HB, :], in0=TH[i % 2], scalar=1.0, in1=ACC[i % 2],
                                               op0=ALU.add, op1=ALU.mult).then_inc(conv_done, 1)

            with dve.Fori(0, BATCH) as b:
                for kind, u, i, a0, d0 in STEPS:
                    par, tile, q = u % 2, b * TB + u, u // GT
                    if kind == "conv" and i < HB:
                        dve.wait_ge(a_moved, a_no(b, a0) + (RING + 1))
                        nc.vector.scalar_tensor_tensor(out=GATE[u][:, i, :], in0=TH[i % 2], scalar=1.0,
                                                       in1=GRAW[i % 2], op0=ALU.add, op1=ALU.mult).then_inc(conv_done, 1)
                    if kind == "conv" and i >= HB:
                        taps(b, u, i)
                        if i > HB:
                            conv_silu(b, u, i - 1)
                        if i == BLOCKS - 1:
                            conv_silu(b, u, i)
                    if kind == "head":
                        dve.wait_ge(d_written, b * D_BATCH + (d0 + 1))
                        bank = BD[d0 % RING]
                        nc.vector.tensor_tensor_reduce(out=GJUNK, in0=bank[:, 0:P], in1=ident(), scale=1.0, scalar=0.0,
                                                       op0=ALU.mult, op1=ALU.add, accum_out=GD[:, 0:1]).then_inc(gd_ready, 1)
                        tt(GM[par], bank[:, 0:P].unsqueeze(1).to_broadcast([P, LEVELS, P]),
                           CONST[:, C_MASK:C_MASK + LEVELS, :], ALU.mult).then_inc(d_moved, 1)
                        dve.wait_ge(gd_ready, tile + 1)
                        nc.vector.scalar_tensor_tensor(
                            out=W0[par].rearrange("p (r h) -> p r h", r=2),
                            in0=heads_of(DT, b, u).unsqueeze(1).to_broadcast([P, 2, HEADS]), scalar=GD[:, 0:1],
                            in1=HEADV[:, V_D:V_D + HEADS].unsqueeze(1).to_broadcast([P, 2, HEADS]),
                            op0=ALU.mult, op1=ALU.add).then_inc(w0_ready, 1)
                    if kind == "mid":
                        dve.wait_ge(a_moved, a_no(b, a0 + 1) + (RING + 1))

                        def taken(j):
                            return d_no(b, d0 + j) + (RING + 1)

                        def scale(lev):
                            if lev % 2 == 0:
                                dve.wait_ge(d_written, b * D_BATCH + (d0 + lev // 2 + 1))
                            m = 1 << lev
                            shape = [P, HB, 64 // m, m]
                            at = (lev % 2) * HB * 64
                            z = BD[(d0 + lev // 2) % RING][:, at:at + HB * 64].rearrange(
                                "p (b q m) -> p b q m", b=HB, m=m)
                            ins = tt(PR[lev % 3][:, 0:HB * 64].rearrange("p (b q m) -> p b q m", b=HB, m=m), z,
                                     odd(ET[par][:, lev, :], lev).unsqueeze(1).to_broadcast(shape), ALU.mult)
                            last = lev % 2 == 1 or lev == LEVELS - 1
                            ins.then_inc(d_moved if last else p_chain, 1)

                        def add(lev):
                            if lev % 2 == 1 or lev == LEVELS - 1:
                                dve.wait_ge(d_moved, taken(lev // 2))
                            else:
                                dve.wait_ge(p_chain, tile * P_TILE + (lev // 2 + 1))
                            if lev == 0:
                                dve.wait_ge(y0_ready, tile + 1)
                            else:
                                dve.wait_ge(y_chain, tile * Y_TILE + lev)
                            m = 1 << lev
                            y = odd(Y, lev)
                            tt(y, y, PR[lev % 3][:, 0:HB * 64].rearrange("p (b q m) -> p b q m", b=HB, m=m),
                               ALU.add).then_inc(y_chain, 1)

                        P_TILE, Y_TILE = LEVELS // 2, LEVELS + 1
                        scale(0)
                        for lev in range(1, LEVELS):
                            scale(lev)
                            add(lev - 1)
                        dve.wait_ge(d_written, b * D_BATCH + (d0 + OFF + 1))
                        tt(PR[LEVELS % 3].rearrange("p (b t) -> p b t", b=HB),
                           BD[(d0 + OFF) % RING][:, :].rearrange("p (b t) -> p b t", b=HB),
                           ET[par][:, PRE, :].unsqueeze(1).to_broadcast([P, HB, P]), ALU.mult).then_inc(d_moved, 1)
                        add(LEVELS - 1)
                        dve.wait_ge(d_moved, taken(OFF))
                        dve.wait_ge(y_chain, tile * Y_TILE + LEVELS)
                        tt(Y, Y, PR[LEVELS % 3].rearrange("p (b t) -> p b t", b=HB), ALU.add).then_inc(y_chain, 1)
                        dve.wait_ge(d_written, b * D_BATCH + (d0 + NEW + 1))
                        dve.wait_ge(s1_ready, tile + 3)
                        tt(S, BD[(d0 + NEW) % RING][:, :], S1, ALU.add).then_inc(d_moved, 1)
                        dve.wait_ge(y_chain, (tile + 1) * Y_TILE)
                        dve.wait_ge(a_moved, a_no(b, before(tail_a, A_BATCH, u, 2)) + (RING + 1))
                        tt(HG[par], Y, GATE[q][:, :, cols_of(u)], ALU.mult).then_inc(hg_ready, 1)

            dve.wait_ge(a_moved, RING + A_P1 + BATCH * A_BATCH)
            nc.vector.tensor_scalar(RNORM[:, :], VARS[:, :], 16 * 0.25 / DIN, 16 * EPS, ALU.mult, ALU.add).then_inc(rn_var, 1)

            def expert_half(k, par):
                dve.wait_ge(ft_ready, k + 1)
                nc.vector.scalar_tensor_tensor(out=FG[par], in0=FT[par], scalar=1.0, in1=FG[par],
                                               op0=ALU.add, op1=ALU.mult).then_inc(fa_ready, 1)
                dve.wait_ge(fu_full, k + 1)
                dve.wait_ge(fa_ready, k + 1)
                tt(FH[par], BU[par][:, :], FG[par], ALU.mult).then_inc(fh_ready, 1)

            expert_half(0, 0)
            with dve.Fori(0, (NT - 1) // 2) as i:
                expert_half(i * 2 + 1, 1)
                expert_half(i * 2 + 2, 0)

            nc.vector.tensor_scalar(PROB[:, :], PROB[:, :], 0.5, None, ALU.mult).then_inc(dve_chain, 1)
            chain[0] += 1
            dve.wait_ge(dve_chain, chain[0])
            dve.wait_ge(zx_loaded, 16)
            dve.wait_ge(zo_scaled, 1)
            for g in range(GROUPS):
                cols = slice(g * GT * DM, (g + 1) * GT * DM)
                dve.wait_ge(gathered[g], 16 * GT)
                z = ZF[:, cols]
                tt(z.rearrange("p (t d) -> p t d", d=DM), z.rearrange("p (t d) -> p t d", d=DM),
                   PROB[:, g * GT:(g + 1) * GT].unsqueeze(2).to_broadcast([P, GT, DM]), ALU.mult).then_inc(z_made, 1)
                dve.wait_ge(zt_ready, g + 1)
                link(nc.vector.scalar_tensor_tensor(out=z, in0=ZT[g % 2], scalar=1.0, in1=z, op0=ALU.add, op1=ALU.mult))
                link(tt(z, z, ZO[:, cols], ALU.mult))
                tt(ZX[:, cols], ZX[:, cols], z, ALU.add).then_inc(z_out, 1)


def kernel(**inputs):
    import concourse.bacc as bacc
    from concourse.bass_utils import run_bass_kernel_spmd

    def get(name):
        return np.ascontiguousarray(inputs[name])

    def by_p(a):
        return a.reshape(HEADS, HD, *a.shape[1:]).swapaxes(0, 1).reshape(a.shape)

    w_in = get("L0_attn_in_proj_w")
    gate, x, bc, dt = w_in[:DIN], w_in[DIN:2 * DIN], w_in[2 * DIN:2 * DIN + 2 * NST], w_in[2 * DIN + 2 * NST:]
    conv = np.concatenate([get("L0_attn_conv_w"), get("L0_attn_conv_b")[:, None]], axis=1)
    conv = np.concatenate([by_p(conv[:DIN]), conv[DIN:]])
    arrays = {
        "x": get("L0_attn_hidden_states").reshape(TOK, DM),
        "w_main": np.concatenate([by_p(gate), by_p(x), bc]).T,
        "w_dr": np.concatenate([dt.T, get("L0_ffn_router_w")], axis=1),
        "conv_c": conv.reshape(XB, P, KC + 1).transpose(1, 0, 2).reshape(P, XB * (KC + 1)),
        "head_v": np.concatenate([get("L0_attn_dt_bias"), get("L0_attn_A_log"), get("L0_attn_D")])[None],
        "norm_c": by_p(get("L0_attn_norm_w")).reshape(HB, P).T,
        "w_out": by_p(get("L0_attn_out_proj_w").T),
        "w_gate": get("L0_ffn_gate_w"),
        "w_up": get("L0_ffn_up_w"),
        "w_down": get("L0_ffn_down_w"),
        "consts": constant_matrices().reshape(P, N_CONST * P),
    }
    arrays = {n: np.ascontiguousarray(a) for n, a in arrays.items()}
    nc = bacc.Bacc("TRN2", target_bir_lowering=False, num_devices=1)
    args = [nc.dram_tensor(f"in_{n}", a.shape, FP32, kind="ExternalInput").ap() for n, a in arrays.items()]
    out = nc.dram_tensor("out_0_dram", [TOK, DM], FP32, kind="ExternalOutput").ap()
    mixer_moe_kernel(nc, *args, out)
    r = run_bass_kernel_spmd(nc, [{f"in_{n}": a for n, a in arrays.items()}], core_ids=[0])
    return r.results[0]["out_0_dram"].reshape(BATCH, SEQ, DM)
```

```python
from contextlib import ExitStack

import concourse.bass as bass
import numpy as np
from concourse import mybir

FP32 = mybir.dt.float32
I32 = mybir.dt.int32
U32 = mybir.dt.uint32
ALU = mybir.AluOpType
ACT = mybir.ActivationFunctionType
AX = mybir.AxisListType

P = 128
BATCH, SEQ, DM = 2, 1024, 256
DIN, HEADS, HD, NST, KC = 512, 64, 8, 128, 4
EXPERTS, DFF = 8, 512
EPS = 1e-5
TOK = BATCH * SEQ
TILES = TOK // P
TB = SEQ // P
GT = 4
GROUPS = TILES // GT
GW = GT * P
QB = TB // GT
DK = DM // P
HB = DIN // P
XB = HB + 2
LEVELS = 7
SUF, PRE, NEXT = LEVELS - 1, LEVELS, LEVELS + 1
SLOTS = NEXT + 1
XSLOTS = SUF + 1
M_PRE, M_NEXT, M_SAME = LEVELS - 1, LEVELS, LEVELS + 1
MAPS = LEVELS + 2
KF = DFF // P
NT = TILES + EXPERTS - 1
WE = DK * DFF * 2 + KF * DM
RW = HEADS + EXPERTS
XW = DM + 2
RING = 4

C_ID, C_SUM, C_ONE, C_TRI, C_SHIFT = 0, 1, SLOTS + 1, SLOTS + 2, SLOTS + 3
C_MASK = C_SHIFT + 1
N_CONST = C_MASK + LEVELS - 1
D_BASE = 16
V_BIAS, V_ALOG, V_D = 0, HEADS, 2 * HEADS
LOG1P_DEGREE = 10


def constant_matrices():
    k, t = np.arange(P)[:, None], np.arange(P)[None, :]
    mats = [k == t]
    for lev in range(1, LEVELS):
        same = (k >> lev) == (t >> lev)
        mats.append(same & np.where((t >> lev) & 1, k <= t, k > t))
    mats += [k > t, k <= t, k == t + 1, k >= 0 * t, k < t, t == k + 1]
    for lev in range(1, LEVELS):
        mats.append(((k >> lev) & 1 == 0) & ((t >> lev) & 1 == 1) & ((k >> lev + 1) == (t >> lev + 1)))
    return np.stack([m.astype(np.float32) for m in mats], axis=1)


def log1p_coefficients():
    cheb = np.polynomial.chebyshev.Chebyshev.interpolate(
        lambda u: np.log1p(u) / u, LOG1P_DEGREE, domain=[0, 1])
    power = cheb.convert(kind=np.polynomial.Polynomial, domain=[-1, 1], window=[-1, 1])
    return [float(c) for c in power(np.polynomial.Polynomial([0.5, 1.0])).coef]


def batch_steps():
    steps = []
    blocks = HB + XB
    steps += [("conv", 0, i) for i in range(blocks)]
    steps += [("pair", 0, 0), ("head", 0, 0), ("turn", 0, 0)]
    cut = [0, 4, 7, 10]
    for u in range(TB):
        if u < 3:
            steps += [("conv", 1, i) for i in range(cut[u], cut[u + 1])]
        if u + 1 < TB:
            if u % 2 == 1:
                steps.append(("pair", u + 1, 0))
            steps.append(("head", u + 1, 0))
        if u > 0:
            steps.append(("norm", u - 1, 0))
        steps.append(("mid", u, 0))
        if u + 1 < TB:
            steps.append(("turn", u + 1, 0))
        if u > 0:
            steps.append(("tail", u - 1, 0))
    steps.append(("norm", TB - 1, 0))
    steps.append(("tail", TB - 1, 0))
    out, a, d = [], 0, 0
    for kind, x, i in steps:
        out.append((kind, x, i, a, d))
        a += {"conv": 1, "pair": 3, "head": 1, "mid": 0, "turn": 3, "norm": 0, "tail": 1}[kind]
        d += {"conv": 0, "pair": 0, "head": 1, "mid": 5, "turn": 0, "norm": 0, "tail": 0}[kind]
    return out, a, d


def mixer_moe_kernel(nc, x_in, w_main, w_dr, conv_c, head_v, norm_c, w_out, w_gate, w_up, w_down,
                     consts, out):
    STEPS, A_BATCH, D_BATCH = batch_steps()
    assert A_BATCH % RING == 0 and D_BATCH % RING == 0
    A_P1 = 4 * GROUPS
    COEF = log1p_coefficients()

    x_dram = x_in.rearrange("(t p) d -> p t d", p=P)
    out_dram = out.rearrange("(t p) d -> p t d", p=P)
    xs_dram = nc.dram_tensor("x_by_expert", [NT * P, XW], FP32).ap()
    g_dram = nc.dram_tensor("gate_rows", [TOK + 1, DM], FP32).ap()
    o_dram = nc.dram_tensor("mixer_rows", [TOK, DM], FP32).ap()
    xs_tiles = xs_dram.rearrange("(t p) d -> p t d", p=P)
    g_tiles = g_dram[0:TOK, :].rearrange("(t p) d -> p t d", p=P)
    o_tiles = o_dram.rearrange("(t p) d -> p t d", p=P)

    with ExitStack() as ctx:
        def sb(name, cols, dt=FP32):
            return ctx.enter_context(nc.sbuf_tensor(name, [P, cols], dt))

        def sem(name):
            return ctx.enter_context(nc.semaphore(name))

        CONST = sb("CONST", N_CONST * P)[:, :].rearrange("p (m t) -> p m t", m=N_CONST)
        W_MAIN = sb("W_MAIN", DK * 2 * (DIN + P))[:, :].rearrange("p (k n) -> p k n", k=DK)
        W_DR = sb("W_DR", DK * RW)[:, :].rearrange("p (k n) -> p k n", k=DK)
        CONVC = sb("CONVC", XB * 5)[:, :].rearrange("p (b j) -> p b j", j=5)
        HEADV = sb("HEADV", 3 * HEADS)
        NORMC = sb("NORMC", HB)
        W_OUT = sb("W_OUT", HB * DM)[:, :].rearrange("p (b n) -> p b n", b=HB)
        XNT = sb("XNT", DK * TOK)[:, :].rearrange("p (k t) -> p k t", k=DK)
        DT = sb("DT", TILES * HEADS)
        DA = sb("DA", TILES * HEADS)
        PROB = sb("PROB", TILES)
        POS = sb("POS", TILES, U32)
        EXPERT_OF = sb("EXPERT_OF", NT + 1, I32)
        VARS = sb("VARS", TILES)
        RNORM = sb("RNORM", TILES)
        MHALF = sb("MHALF", TILES)
        EA = sb("EA", HEADS)
        ZERO = sb("ZERO", XW)[:, :]
        ARENA_COLS = 37650
        ARENA = sb("ARENA", ARENA_COLS)
        EARLY = 3
        WEXP = ARENA[:, 0:EXPERTS * WE].rearrange("p (e c) -> p e c", e=EXPERTS)
        place = [0]

        def part(cols):
            at = place[0]
            place[0] += cols
            assert place[0] <= ARENA_COLS, place[0]
            return ARENA[:, at:at + cols]

        RAW = [part(KC - 1 + GW) for _ in range(2)]
        HIST = [part(XB * (KC - 1)).rearrange("p (b j) -> p b j", b=XB) for _ in range(2)]
        ACC = [part(GW) for _ in range(2)]
        TH = [part(GW) for _ in range(2)]
        GRAW = [part(GW) for _ in range(2)]
        XBC, GATE = [], []
        for _ in range(QB):
            XBC.append(part(XB * GW).rearrange("p (b t) -> p b t", b=XB))
            GATE.append(part(HB * GW).rearrange("p (b t) -> p b t", b=HB))
            if len(GATE) == 1:
                assert place[0] >= EARLY * WE
        conv_end = place[0]
        XS = [part(XSLOTS * DIN).rearrange("p (l c) -> p l c", l=XSLOTS) for _ in range(2)]
        E = [part(SLOTS * P).rearrange("p (l r h) -> p l r h", l=SLOTS, r=2) for _ in range(2)]
        ETOT = [part(HEADS) for _ in range(4)]
        E2 = [part(XSLOTS * HEADS).rearrange("p (l h) -> p l h", l=XSLOTS) for _ in range(2)]
        GM = [part((LEVELS - 1) * P).rearrange("p (l t) -> p l t", l=LEVELS - 1) for _ in range(2)]
        GD = part(2)
        GJUNK = part(2 * P)
        W0 = [part(P) for _ in range(2)]
        W1 = [part(P) for _ in range(2)]
        ET = [part(MAPS * P).rearrange("p (l t) -> p l t", l=MAPS) for _ in range(2)]
        Y = [part(DIN).rearrange("p (b t) -> p b t", b=HB) for _ in range(2)]
        PR = [part(DIN if i == LEVELS % 3 else DIN // 2) for i in range(3)]
        HG = [part(DIN).rearrange("p (b t) -> p b t", b=HB) for _ in range(2)]
        SQS = [part(P) for _ in range(2)]
        SQ = [part(DIN).rearrange("p (b t) -> p b t", b=HB) for _ in range(2)]
        S = part(DIN)
        S1 = part(DIN)
        BT = [part(P) for _ in range(2)]
        XT = [part(DIN) for _ in range(2)]
        O = [part(DM) for _ in range(2)]


        place[0] = conv_end
        X = part(TILES * XW).rearrange("p (t d) -> p t d", d=XW)
        XN = X
        XNS = part(GT * DM).rearrange("p (c d) -> p c d", c=GT)
        XTS = part(GT * DM).rearrange("p (c k t) -> p c k t", c=GT, k=DK)
        STATS = part(TILES * 6).rearrange("p (t s) -> p t s", t=TILES)
        MV = part(TILES * 2).rearrange("p (t s) -> p t s", t=TILES)
        VE = part(TILES)
        RS = part(TILES)
        DTR = part(TILES * RW)
        SP_V = part(TILES * HEADS)
        SP_U = part(TILES * HEADS)
        SP_W = part(TILES * HEADS)
        SP_P = part(TILES * HEADS)
        TE = TILES * EXPERTS
        SIG, R1, R2, HOT, RANK, TOTS = (part(TE) for _ in range(6))
        CUM = [part(TE), part(TE)]
        IOTA, IOTAF = part(EXPERTS), part(EXPERTS)
        IOTAT, IOTATF = part(NT * EXPERTS), part(NT * EXPERTS)
        FIRST = part(TILES)
        CNTI, CNTS = part(EXPERTS).bitcast(I32), part(EXPERTS).bitcast(I32)
        CNTF, BASE128 = part(EXPERTS), part(EXPERTS)
        ENDS = [part(EXPERTS), part(EXPERTS)]
        LE = part(NT * EXPERTS)
        EXF = part(NT)
        POSF = part(TILES)
        IOTAK = part(TILES)

        place[0] = EXPERTS * WE
        FX = [part(XW) for _ in range(2)]
        FXT = [part(DM).rearrange("p (k t) -> p k t", k=DK) for _ in range(2)]
        FT = [part(DFF) for _ in range(2)]
        FG = [part(DFF) for _ in range(2)]
        FH = [part(DFF) for _ in range(2)]
        FHT = [part(DFF).rearrange("p (k t) -> p k t", k=KF) for _ in range(2)]
        TZ = [part(DM) for _ in range(2)]
        FY = [part(DM) for _ in range(2)]
        TOKENS = part(NT).bitcast(U32)
        IDX_SEEN = part(1)
        IDX = [part(1).bitcast(U32) for _ in range(2)]
        ZX = part(TILES * DM)
        ZO = XNT.rearrange("p k t -> p (k t)")
        place[0] = 0
        ZF = part(TILES * DM)

        BA = [ctx.enter_context(nc.psum_tensor(f"BA{i}", [P, 512], FP32)) for i in range(RING)]
        BD = [ctx.enter_context(nc.psum_tensor(f"BD{i}", [P, 512], FP32)) for i in range(RING)]

        def sems(names):
            return [sem(n) for n in names.split()]

        a_written, a_moved, d_written, d_moved = sems("a_written a_moved d_written d_moved")
        dve_chain, pool_chain, act_chain = sems("dve_chain pool_chain act_chain")
        x_loaded = [sem(f"x_loaded{g}") for g in range(GROUPS)]
        consts_in, w_loaded, iota_made, zero_made, slots_zeroed = sems(
            "consts_in w_loaded iota_made zero_made slots_zeroed")
        var_ready, rstd_ready, xn_ready, xn_kept = sems("var_ready rstd_ready xn_ready xn_kept")
        abs_ready, u_ready, ea_ready, da_ready, sig_ready, hot_ready = sems(
            "abs_ready u_ready ea_ready da_ready sig_ready hot_ready")
        v_ready, rank_written, routed, scattered, w_out_scaled, taps_halved = sems(
            "v_ready rank_written routed scattered w_out_scaled taps_halved")
        conv_done, taps_done, tanh_done, hist_zero, state_zero = sems(
            "conv_done taps_done tanh_done hist_zero state_zero")
        e2_ready, x_scaled, s1_ready, y0_ready = sems("e2_ready x_scaled s1_ready y0_ready")
        w0_ready, hg_ready, sq_made, sq_ready, p_chain, y_chain = sems(
            "w0_ready hg_ready sq_made sq_ready p_chain y_chain")
        conv_chain, gd_ready = sems("conv_chain gd_ready")
        o_stored = sems("o_stored0 o_stored1")
        expert_loaded = [sem(f"expert_loaded{e}") for e in range(EXPERTS)]
        experts_in = sem("experts_in")
        fx_loaded = sems("fx_loaded0 fx_loaded1")
        fy_stored = sem("fy_stored")
        fxt_full, fxt_ready, fg_full, fu_full, ft_ready, fa_ready, fh_ready, fht_full, fht_ready, fy_full = sems(
            "fxt_full fxt_ready fg_full fu_full ft_ready fa_ready fh_ready fht_full fht_ready fy_full")
        tz_ready, fy_ready, token_kept, idx_made = sems("tz_ready fy_ready token_kept idx_made")
        zx_loaded, zo_loaded, rn_var, rn_ready, zo_scaled, z_stored = sems(
            "zx_loaded zo_loaded rn_var rn_ready zo_scaled z_stored")
        zf_loaded = [sem(f"zf_loaded{g}") for g in range(GROUPS)]
        z_made, z_out = ([sem(f"{n}{g}") for g in range(GROUPS)] for n in ("z_made", "z_out"))

        block = ctx.enter_context(nc.Block())

        def ident():
            return CONST[:, C_ID, :]

        def odd(ap, lev):
            m = 1 << lev
            if len(ap.shape) == 2:
                return ap.rearrange("p (q o m) -> p q o m", o=2, m=m)[:, :, 1, :]
            return ap.rearrange("p b (q o m) -> p b q o m", o=2, m=m)[:, :, :, 1, :]

        BX, BG, BU, BH = ([BA[0], BD[0]], [BA[1], BD[1]], [BA[2], BD[2]], [BA[3], BD[3]])
        WEXP_FLAT = ARENA[:, 0:EXPERTS * WE]
        BLOCKS = HB + XB
        pair_a = {u: a for kind, u, _, a, _ in STEPS if kind == "pair"}
        turn_a = {u: a for kind, u, _, a, _ in STEPS if kind == "turn"}
        head_a = {u: a for kind, u, _, a, _ in STEPS if kind == "head"}
        mid_d = {u: d for kind, u, _, _, d in STEPS if kind == "mid"}
        tail_a = {u: a for kind, u, _, a, _ in STEPS if kind == "tail"}
        conv_a = {(q, i): a for kind, q, i, a, _ in STEPS if kind == "conv"}
        Z_CHUNKS = (LEVELS - 1) // 2
        OFF, NEW = Z_CHUNKS, Z_CHUNKS + 1

        def a_no(b, i):
            return b * A_BATCH + (A_P1 + i)

        def d_no(b, i):
            return b * D_BATCH + (D_BASE + i)

        def before(at, per_batch, u, back):
            return at[u - back] if u >= back else at[u - back + TB] - per_batch

        def cols_of(u):
            return slice((u % GT) * P, (u % GT + 1) * P)

        def heads_of(ap, b, u):
            return ap[:, bass.ds(b * (TB * HEADS) + u * HEADS, HEADS)]

        @block.sync
        def _(sp):
            for g in range(GROUPS):
                sp.dma_start(X[:, g * GT:(g + 1) * GT, 0:DM],
                             x_dram[:, g * GT:(g + 1) * GT, :]).then_inc(x_loaded[g], 16)
            sp.dma_start(CONST, consts.rearrange("p (m t) -> p m t", m=N_CONST)).then_inc(consts_in, 16)
            sp.dma_start(W_DR, w_dr.rearrange("(k p) n -> p k n", p=P)).then_inc(consts_in, 16)
            sp.dma_start(HEADV[:, :], head_v[0:1, :].to_broadcast([P, 3 * HEADS])).then_inc(consts_in, 16)
            sp.dma_start(CONVC, conv_c.rearrange("p (b j) -> p b j", j=KC + 1)).then_inc(consts_in, 16)
            sp.dma_start(NORMC[:, :], norm_c).then_inc(consts_in, 16)
            sp.dma_start(W_OUT, w_out.rearrange("(b p) n -> p b n", p=P)).then_inc(consts_in, 16)
            sp.dma_start(W_MAIN, w_main.rearrange("(k p) n -> p k n", p=P)).then_inc(w_loaded, 16)
            sp.wait_ge(zero_made, 1)
            sp.dma_start(xs_tiles, ZERO.unsqueeze(1).to_broadcast([P, NT, XW])).then_inc(slots_zeroed, 16)

            def load_expert(e):
                signal = expert_loaded[e]
                sp.dma_start(WEXP[:, e, 0:DK * DFF].rearrange("p (k n) -> p k n", k=DK),
                             w_gate[e].rearrange("(k p) n -> p k n", p=P)).then_inc(signal, 16)
                sp.dma_start(WEXP[:, e, DK * DFF:2 * DK * DFF].rearrange("p (k n) -> p k n", k=DK),
                             w_up[e].rearrange("(k p) n -> p k n", p=P)).then_inc(signal, 16)
                sp.dma_start(WEXP[:, e, 2 * DK * DFF:].rearrange("p (k n) -> p k n", k=KF),
                             w_down[e].rearrange("(k p) n -> p k n", p=P)).then_inc(signal, 16)

            for par in range(2):
                sp.sem_inc(o_stored[par], 16)

            def store_mixer(b, u):
                sp.wait_ge(a_moved, a_no(b, tail_a[u]) + (RING + 1))
                sp.dma_start(o_tiles[:, bass.ds(b * TB + u, 1), :], O[u % 2].unsqueeze(1)).then_inc(o_stored[u % 2], 16)

            with sp.Fori(0, BATCH - 1) as b:
                for u in range(TB):
                    store_mixer(b, u)
            for u in range(TB):
                store_mixer(BATCH - 1, u)
                if u == GT:
                    sp.wait_ge(hg_ready, 2 + (BATCH - 1) * TB + GT)
                    for e in range(EARLY):
                        load_expert(e)
            for par in range(2):
                sp.wait_ge(o_stored[par], 16 + 16 * (TILES // 2))
            sp.wait_ge(scattered, 16 * TILES)
            for k in range(2):
                sp.dma_start(FX[k].unsqueeze(1), xs_tiles[:, k:k + 1, :]).then_inc(fx_loaded[k], 16)
            for e in range(EARLY, EXPERTS):
                load_expert(e)

            def load_x(k, par):
                sp.wait_ge(fh_ready, k - 1)
                sp.dma_start(FX[par].unsqueeze(1), xs_tiles[:, bass.ds(k, 1), :]).then_inc(fx_loaded[par], 16)

            load_x(2, 0)
            with sp.Fori(0, (NT - 3) // 2) as i:
                for par in (1, 0):
                    load_x(i * 2 + (4 - par), par)
            sp.wait_ge(fy_stored, 16 * NT)
            for g in range(GROUPS):
                sp.dma_start(ZF[:, g * GT * DM:(g + 1) * GT * DM].rearrange("p (t d) -> p t d", d=DM),
                             g_tiles[:, g * GT:(g + 1) * GT, :]).then_inc(zf_loaded[g], 16)
            for g in range(GROUPS):
                sp.wait_ge(z_out[g], 1)
                sp.dma_start(out_dram[:, g * GT:(g + 1) * GT, :],
                             ZX[:, g * GT * DM:(g + 1) * GT * DM].rearrange("p (t d) -> p t d", d=DM)).then_inc(z_stored, 16)
            sp.wait_ge(z_stored, 16 * GROUPS)

        @block.gpsimd
        def _(pool):
            nc.gpsimd.memset(ZERO[:, 0:DM], 0.0)
            nc.gpsimd.memset(ZERO[:, DM:DM + 1], float(TOK))
            nc.gpsimd.memset(ZERO[:, DM + 1:XW], 0.0).then_inc(zero_made, 1)
            nc.gpsimd.memset(MHALF[:, :], -0.5)
            nc.gpsimd.iota(IOTA.bitcast(I32), pattern=[[1, EXPERTS]], base=-EXPERTS,
                           channel_multiplier=0)
            nc.gpsimd.iota(IOTAK.bitcast(I32), pattern=[[P, TILES]], base=0, channel_multiplier=1)
            nc.gpsimd.iota(IOTAT.bitcast(I32).rearrange("p (t e) -> p t e", e=EXPERTS),
                           pattern=[[1, NT], [0, EXPERTS]], base=0, channel_multiplier=0).then_inc(iota_made, 1)
            pool.wait_ge(iota_made, 1)
            with pool.Fori(0, GROUPS) as g:
                pool.wait_ge(var_ready, g + 1)
                nc.gpsimd.tensor_tensor(out=RS[:, bass.ds(g * GT, GT)], in0=VE[:, bass.ds(g * GT, GT)],
                                        in1=MHALF[:, 0:GT], op=ALU.pow).then_inc(rstd_ready, 1)
            pool.wait_ge(routed, 1)
            pool.wait_ge(slots_zeroed, 16)
            pool.wait_ge(xn_kept, GROUPS)
            for t in range(TILES):
                pool.indirect_dma_start(
                    out=xs_dram, out_offset=bass.IndirectOffsetOnAxis(ap=POS[:, t:t + 1], axis=0),
                    in_=XN[:, t, :], in_offset=None).then_inc(scattered, 16)
            pool.wait_ge(scattered, 16 * TILES)
            pool.sem_inc(e2_ready, 2)
            pool.sem_inc(s1_ready, 2)

            with pool.Fori(0, BATCH) as b:
                pool.wait_ge(d_moved, d_no(b, 0) + RING)
                pool.wait_ge(da_ready, 1)
                zero = ZERO[:, 0:DM].unsqueeze(1).to_broadcast([P, DIN // DM, DM])
                nc.gpsimd.tensor_tensor(out=S.rearrange("p (r d) -> p r d", d=DM), in0=zero, in1=zero,
                                        op=ALU.add).then_inc(state_zero, 1)
                nc.gpsimd.tensor_copy(HIST[1].rearrange("p b j -> p (b j)"), ZERO[:, 0:XB * (KC - 1)]).then_inc(hist_zero, 1)
                for kind, u, _, a0, d0 in STEPS:
                    if kind != "mid":
                        continue
                    par, q, tile = u % 2, u // GT, b * TB + u
                    dt = heads_of(DT, b, u)
                    pool.wait_ge(s1_ready, tile + 2)
                    pool.wait_ge(a_moved, a_no(b, pair_a[u - par] + 1) + (RING + 1))
                    nc.gpsimd.tensor_tensor(
                        out=E2[par], in0=E[par][:, 0:XSLOTS, 0, :],
                        in1=dt.unsqueeze(1).to_broadcast([P, XSLOTS, HEADS]), op=ALU.mult).then_inc(e2_ready, 1)
                    pool.wait_ge(e2_ready, tile + 3)
                    pool.wait_ge(a_moved, a_no(b, head_a[u]) + (RING + 1))
                    for slot in range(XSLOTS):
                        chunk = slot // 2 if slot < SUF else NEW
                        pool.wait_ge(d_moved, d_no(b, before(mid_d, D_BATCH, u, 2) + chunk) + (RING + 1))
                        nc.gpsimd.tensor_tensor(
                            out=XS[par][:, slot, :].rearrange("p (a h) -> p a h", a=HD),
                            in0=E2[par][:, slot, :].unsqueeze(1).to_broadcast([P, HD, HEADS]),
                            in1=XT[par].rearrange("p (a h) -> p a h", a=HD), op=ALU.mult).then_inc(x_scaled, 1)
                    pool.wait_ge(a_moved, a_no(b, turn_a[u] + 2) + (RING + 1))
                    pool.wait_ge(hg_ready, tile + 1)
                    nc.gpsimd.tensor_tensor(
                        out=Y[par], in0=XBC[q][:, 0:HB, cols_of(u)],
                        in1=ET[par][:, M_SAME, :].unsqueeze(1).to_broadcast([P, HB, P]),
                        op=ALU.mult).then_inc(y0_ready, 1)
                    if u == 0:
                        pool.wait_ge(state_zero, b + 1)
                    else:
                        pool.wait_ge(d_moved, d_no(b, mid_d[u - 1] + NEW) + (RING + 1))
                    nc.gpsimd.tensor_tensor(
                        out=S1.rearrange("p (a h) -> p a h", a=HD), in0=S.rearrange("p (a h) -> p a h", a=HD),
                        in1=ETOT[u % 4].unsqueeze(1).to_broadcast([P, HD, HEADS]),
                        op=ALU.mult).then_inc(s1_ready, 1)

            pool.wait_ge(rn_var, 1)
            nc.gpsimd.tensor_tensor(out=RNORM[:, :], in0=RNORM[:, :], in1=MHALF[:, :], op=ALU.pow).then_inc(rn_ready, 1)
            for par in range(2):
                pool.wait_ge(o_stored[par], 16 + 16 * (TILES // 2))
            pool.dma_start(ZO.rearrange("p (t d) -> p t d", d=DM), o_tiles).then_inc(zo_loaded, 16)
            pool.dma_start(ZX.rearrange("p (t d) -> p t d", d=DM), x_dram).then_inc(zx_loaded, 16)
            for e in range(EXPERTS):
                pool.wait_ge(expert_loaded[e], 3 * 16)
                pool.sem_inc(experts_in, 1)

            def scatter_y(k, par):
                pool.wait_ge(token_kept, k + 1)
                nc.gpsimd.tensor_tensor(out=IDX[par], in0=TOKENS[:, bass.ds(k, 1)], in1=ZERO[:, 0:1].bitcast(U32),
                                        op=ALU.add).then_inc(idx_made, 1)
                pool.wait_ge(fy_ready, k + 5)
                if not (isinstance(k, int) and k == 0):
                    pool.wait_ge(fy_stored, k * 16)
                pool.wait_ge(idx_made, k + 1)
                nc.gpsimd.tensor_tensor(out=IDX_SEEN, in0=ZERO[:, 0:1], in1=ZERO[:, 0:1], op=ALU.add)
                pool.indirect_dma_start(
                    out=g_dram, out_offset=bass.IndirectOffsetOnAxis(ap=IDX[par], axis=0),
                    in_=FY[par], in_offset=None).then_inc(fy_stored, 16)

            HALF = NT // 4 * 2
            for k in range(2):
                scatter_y(k, k)
            with pool.Fori(1, HALF // 2) as i:
                for par in range(2):
                    scatter_y(i * 2 + par, par)
            pool.wait_ge(rn_ready, 1)
            pool.wait_ge(zo_loaded, 16)
            nc.gpsimd.tensor_tensor(
                out=ZO.rearrange("p (t d) -> p t d", d=DM), in0=ZO.rearrange("p (t d) -> p t d", d=DM),
                in1=RNORM[:, :].unsqueeze(2).to_broadcast([P, TILES, DM]), op=ALU.mult).then_inc(zo_scaled, 1)
            with pool.Fori(HALF // 2, (NT - 1) // 2) as i:
                for par in range(2):
                    scatter_y(i * 2 + par, par)
            scatter_y(NT - 1, 0)
            pool.wait_ge(zo_scaled, 1)
            pool.wait_ge(zx_loaded, 16)
            g = GROUPS - 1
            cols = slice(g * GT * DM, (g + 1) * GT * DM)
            pool.wait_ge(zf_loaded[g], 16)
            nc.gpsimd.tensor_tensor(out=ZF[:, cols], in0=ZF[:, cols], in1=ZO[:, cols], op=ALU.mult).then_inc(z_made[g], 1)
            pool.wait_ge(z_made[g], 1)
            nc.gpsimd.tensor_tensor(out=ZX[:, cols], in0=ZX[:, cols], in1=ZF[:, cols], op=ALU.add).then_inc(z_out[g], 1)

        @block.scalar
        def _(act):
            act.sem_inc(a_moved, RING)
            with act.Fori(0, GROUPS) as g:
                act.wait_ge(xn_ready, g + 1)
                nc.scalar.activation(XN[:, bass.ds(g * GT, GT), 0:DM], XNS, ACT.Copy).then_inc(xn_kept, 1)
                for h in range(2):
                    act.wait_ge(a_written, g * 4 + (h + 1))
                    nc.scalar.activation(XTS[:, 2 * h:2 * h + 2, :, :],
                                         BA[h][:, :].rearrange("p (c k t) -> p c k t", c=2, k=DK), ACT.Copy)
                    for c in range(2):
                        ins = nc.scalar.activation(
                            XNT[:, :, bass.ds(g * GW + (2 * h + c) * P, P)],
                            BA[h][:, c * DM:(c + 1) * DM].rearrange("p (k t) -> p k t", k=DK), ACT.Copy)
                    ins.then_inc(a_moved, 1)
                for h in range(2):
                    act.wait_ge(a_written, g * 4 + (2 + h + 1))
                    nc.scalar.activation(DTR[:, bass.ds(g * (GT * RW) + 2 * h * RW, 2 * RW)],
                                         BA[2 + h][:, 0:2 * RW], ACT.Copy).then_inc(a_moved, 1)
            act.wait_ge(consts_in, 16 * 6)
            nc.scalar.activation(EA[:, :], HEADV[:, V_ALOG:V_ALOG + HEADS], ACT.Exp).then_inc(ea_ready, 1)
            act.wait_ge(a_moved, RING + A_P1)
            nc.scalar.activation(SIG.rearrange("p (t e) -> p t e", e=EXPERTS),
                                 DTR.rearrange("p (t c) -> p t c", c=RW)[:, :, HEADS:], ACT.Exp,
                                 scale=-1.0).then_inc(sig_ready, 1)
            act.wait_ge(v_ready, 1)
            nc.scalar.activation(SP_U, SP_V, ACT.Abs).then_inc(abs_ready, 1)
            act.wait_ge(abs_ready, 1)
            nc.scalar.activation(SP_U, SP_U, ACT.Exp, scale=-1.0).then_inc(u_ready, 1)
            act.wait_ge(taps_halved, 1)
            for blk in range(HB):
                ins = nc.scalar.activation(W_OUT[:, blk, :], W_OUT[:, blk, :], ACT.Copy, scale=NORMC[:, blk:blk + 1])
            ins.then_inc(w_out_scaled, 1)

            def conv_block(b, q, i, a0):
                par, blk = i % 2, i - HB
                bank = BA[a0 % RING]
                act.wait_ge(a_written, a_no(b, a0) + 1)
                act.wait_ge(conv_done, b * (QB * BLOCKS) + (q * BLOCKS + i + 1))
                if i < HB:
                    nc.scalar.activation(TH[par], bank[:, :], ACT.Tanh, scale=0.5)
                    nc.scalar.activation(GRAW[par], bank[:, :], ACT.Copy).then_inc(a_moved, 1)
                    return
                if q == 0:
                    act.wait_ge(hist_zero, b + 1)
                else:
                    act.wait_ge(a_moved, a_no(b, conv_a[0, i]) + (RING + 1))
                nc.scalar.activation(RAW[par][:, 0:KC - 1], HIST[1 - q][:, blk, :], ACT.Copy)
                nc.scalar.activation(RAW[par][:, KC - 1:], bank[:, :], ACT.Copy)
                nc.scalar.activation(ACC[par], bank[:, :], ACT.Identity, scale=CONVC[:, blk, KC - 1:KC],
                                     bias=CONVC[:, blk, KC:KC + 1])
                nc.scalar.activation(HIST[q][:, blk, :], bank[:, GW - (KC - 1):GW], ACT.Copy).then_inc(a_moved, 1)

            def conv_tanh(b, q, i):
                act.wait_ge(taps_done, b * (QB * XB) + (q * XB + i - HB + 1))
                nc.scalar.activation(TH[i % 2], ACC[i % 2], ACT.Tanh).then_inc(tanh_done, 1)

            with act.Fori(0, BATCH) as b:
                for kind, u, i, a0, d0 in STEPS:
                    par, tile = u % 2, b * TB + u
                    if kind == "conv":
                        conv_block(b, u, i, a0)
                        if i > HB:
                            conv_tanh(b, u, i - 1)
                        if i == BLOCKS - 1:
                            conv_tanh(b, u, i)
                    if kind == "pair":
                        act.wait_ge(e2_ready, tile + 2)
                        for j in range(2):
                            act.wait_ge(a_written, a_no(b, a0 + j) + 1)
                            sums = BA[(a0 + j) % RING][:, :].rearrange("p (l c h) -> p l c h", c=2, h=HEADS)
                            for c in range(2):
                                ins = nc.scalar.activation(
                                    E[c][:, 4 * j:4 * j + 4, :, :],
                                    sums[:, :, c, :].unsqueeze(2).to_broadcast([P, 4, 2, HEADS]), ACT.Exp)
                            ins.then_inc(a_moved, 1)
                        act.wait_ge(a_written, a_no(b, a0 + 2) + 1)
                        bank = BA[(a0 + 2) % RING]
                        for c in range(2):
                            nc.scalar.activation(
                                E[c][:, NEXT, :, :],
                                bank[:, c * HEADS:(c + 1) * HEADS].unsqueeze(1).to_broadcast([P, 2, HEADS]), ACT.Exp)
                            ins = nc.scalar.activation(ETOT[u % 4 + c], bank[:, (2 + c) * HEADS:(3 + c) * HEADS], ACT.Exp)
                        ins.then_inc(a_moved, 1)
                    if kind == "head":
                        act.wait_ge(s1_ready, tile + 1)
                        act.wait_ge(a_written, a_no(b, a0) + 1)
                        nc.scalar.activation(XT[par], BA[a0 % RING][:, :], ACT.Copy).then_inc(a_moved, 1)
                    if kind == "turn":
                        act.wait_ge(hg_ready, tile + 1)
                        for j in range(2):
                            act.wait_ge(a_written, a_no(b, a0 + j) + 1)
                            nc.scalar.activation(ET[par][:, 4 * j:4 * j + 4, :],
                                                 BA[(a0 + j) % RING][:, :].rearrange("p (l t) -> p l t", l=4),
                                                 ACT.Copy).then_inc(a_moved, 1)
                        act.wait_ge(a_written, a_no(b, a0 + 2) + 1)
                        bank = BA[(a0 + 2) % RING]
                        nc.scalar.activation(BT[par], bank[:, 0:P], ACT.Copy)
                        nc.scalar.activation(ET[par][:, M_SAME, :], bank[:, P:2 * P], ACT.Copy).then_inc(a_moved, 1)
                    if kind == "norm":
                        act.wait_ge(hg_ready, tile + 3)
                        act.wait_ge(sq_ready, tile + 1)
                        nc.scalar.activation(SQ[par], HG[par], ACT.Square).then_inc(sq_made, 1)
                    if kind == "tail":
                        act.wait_ge(a_written, a_no(b, a0) + 1)
                        act.wait_ge(o_stored[par], b * (8 * TB) + (16 * (u // 2) + 16))
                        nc.scalar.activation(VARS[:, bass.ds(tile, 1)], BA[a0 % RING][:, DM:DM + 1], ACT.Copy)
                        nc.scalar.activation(O[par], BA[a0 % RING][:, 0:DM], ACT.Copy).then_inc(a_moved, 1)

            def gate(k, par):
                act.wait_ge(fg_full, k + 1)
                nc.scalar.activation(FT[par], BG[par][:, :], ACT.Tanh, scale=0.5)
                nc.scalar.activation(FG[par], BG[par][:, :], ACT.Copy).then_inc(ft_ready, 1)

            def turned(k, par):
                act.wait_ge(fxt_full, k + 1)
                nc.scalar.activation(FXT[par], BX[par][:, 0:DM].rearrange("p (k t) -> p k t", k=DK),
                                     ACT.Copy).then_inc(fxt_ready, 1)

            def hidden(k, par):
                act.wait_ge(fht_full, k + 1)
                nc.scalar.activation(FHT[par], BH[par][:, :].rearrange("p (k t) -> p k t", k=KF),
                                     ACT.Copy).then_inc(fht_ready, 1)

            def output(k, par):
                act.wait_ge(fy_full, k + 1)
                nc.scalar.activation(TZ[par], BX[par][:, DM:2 * DM], ACT.Tanh, scale=0.5).then_inc(tz_ready, 1)

            turned(0, 0)
            gate(0, 0)
            turned(1, 1)
            gate(1, 1)
            turned(2, 0)
            hidden(0, 0)
            with act.Fori(0, (NT - 3) // 2) as i:
                for par in range(2):
                    k = i * 2 + (2 + par)
                    gate(k, par)
                    turned(k + 1, 1 - par)
                    hidden(k - 1, 1 - par)
                    output(k - 2, par)
            gate(NT - 1, 0)
            hidden(NT - 2, 1)
            output(NT - 3, 0)
            hidden(NT - 1, 0)
            output(NT - 2, 1)
            output(NT - 1, 0)

        @block.tensor
        def _(pe):
            pe.wait_ge(consts_in, 16 * 6)
            with pe.Fori(0, GROUPS) as g:
                for h in range(2):
                    pe.wait_ge(a_moved, g * 4 + (h + 1))
                    pe.wait_ge(xn_ready, g + 1)
                    for c in range(2):
                        for k in range(DK):
                            ins = nc.tensor.transpose(BA[h][:, c * DM + k * P:c * DM + (k + 1) * P],
                                                      XNS[:, 2 * h + c, k * P:(k + 1) * P], ident())
                    ins.then_inc(a_written, 1)
                for h in range(2):
                    pe.wait_ge(a_moved, g * 4 + (RING + h + 1))
                    for c in range(2):
                        for k in range(DK):
                            ins = nc.tensor.matmul(BA[2 + h][:, c * RW:(c + 1) * RW], lhsT=XTS[:, 2 * h + c, k, :],
                                                   rhs=W_DR[:, k, :], start=(k == 0), stop=(k == DK - 1))
                    ins.then_inc(a_written, 1)
            pe.wait_ge(hot_ready, 1)
            nc.tensor.matmul(BD[0][:, 0:TE], lhsT=CONST[:, C_TRI, :], rhs=HOT, start=True, stop=True)
            nc.tensor.matmul(BD[0][:, TE:2 * TE], lhsT=CONST[:, C_ONE, :], rhs=HOT, start=True,
                             stop=True).then_inc(rank_written, 1)
            pe.wait_ge(w_loaded, 16)

            with pe.Fori(0, BATCH) as b:
                for kind, u, i, a0, d0 in STEPS:
                    par, tile, q = u % 2, b * TB + u, u // GT

                    def bank_a(j):
                        pe.wait_ge(a_moved, a_no(b, a0 + j) + 1)
                        return BA[(a0 + j) % RING]

                    def bank_d(j):
                        pe.wait_ge(d_moved, d_no(b, d0 + j) + 1)
                        return BD[(d0 + j) % RING]

                    if kind == "conv":
                        bank = bank_a(0)
                        for k in range(DK):
                            ins = nc.tensor.matmul(
                                bank[:, :], lhsT=W_MAIN[:, k, i * P:(i + 1) * P],
                                rhs=XNT[:, k, bass.ds(b * SEQ + u * GW, GW)], start=(k == 0), stop=(k == DK - 1))
                        ins.then_inc(a_written, 1)
                    if kind == "pair":
                        if u == 0:
                            pe.wait_ge(da_ready, 1)
                        da = DA[:, bass.ds(b * (TB * HEADS) + u * HEADS, 2 * HEADS)]
                        for j in range(2):
                            bank = bank_a(j)
                            for slot in range(4 * j, 4 * j + 4):
                                ins = nc.tensor.matmul(bank[:, (slot % 4) * 2 * HEADS:(slot % 4 + 1) * 2 * HEADS],
                                                       lhsT=CONST[:, C_SUM + slot, :], rhs=da, start=True, stop=True)
                            ins.then_inc(a_written, 1)
                        bank = bank_a(2)
                        for j, m in enumerate((C_SUM + NEXT, C_ONE)):
                            ins = nc.tensor.matmul(bank[:, j * 2 * HEADS:(j + 1) * 2 * HEADS], lhsT=CONST[:, m, :],
                                                   rhs=da, start=True, stop=True)
                        ins.then_inc(a_written, 1)
                    if kind == "head":
                        pe.wait_ge(conv_done, b * (QB * BLOCKS) + (2 + (q + 1) * BLOCKS))
                        bank = bank_d(0)
                        nc.tensor.matmul(bank[:, 0:P], lhsT=XBC[q][:, HB, cols_of(u)],
                                         rhs=XBC[q][:, HB + 1, cols_of(u)], start=True, stop=True).then_inc(d_written, 1)
                        bank = bank_a(0)
                        for blk in range(HB):
                            ins = nc.tensor.transpose(bank[:, blk * P:(blk + 1) * P], XBC[q][:, blk, cols_of(u)], ident())
                        ins.then_inc(a_written, 1)
                    if kind == "turn":
                        pe.wait_ge(a_moved, a_no(b, pair_a[u - par] + 2) + (RING + 1))
                        by_token = [E[par][:, slot, :, :].rearrange("p r h -> p (r h)")
                                    for slot in [*range(LEVELS - 1), PRE]] + [W1[par]]
                        for j in range(2):
                            bank = bank_a(j)
                            if j == 1:
                                pe.wait_ge(w0_ready, tile + 1)
                            for at in range(4):
                                ins = nc.tensor.transpose(bank[:, at * P:(at + 1) * P], by_token[4 * j + at], ident())
                            ins.then_inc(a_written, 1)
                        bank = bank_a(2)
                        nc.tensor.transpose(bank[:, 0:P], XBC[q][:, HB, cols_of(u)], ident())
                        nc.tensor.transpose(bank[:, P:2 * P], W0[par], ident()).then_inc(a_written, 1)
                    if kind == "mid":
                        for lev in range(1, LEVELS):
                            if lev % 2 == 1:
                                bank = bank_d(lev // 2)
                            pe.wait_ge(x_scaled, tile * XSLOTS + lev)
                            for blk in range(HB):
                                at = ((lev - 1) % 2) * HB * 64 + blk * 64
                                ins = nc.tensor.matmul(bank[:, at:at + 64], lhsT=XS[par][:, lev - 1, blk * P:(blk + 1) * P],
                                                       rhs=odd(GM[par][:, lev - 1, :], lev), start=True, stop=True)
                            if lev % 2 == 0:
                                ins.then_inc(d_written, 1)
                        bank = bank_d(OFF)
                        if u == 0:
                            pe.wait_ge(state_zero, b + 1)
                        else:
                            pe.wait_ge(d_moved, d_no(b, mid_d[u - 1] + NEW) + (RING + 1))
                        for blk in range(HB):
                            ins = nc.tensor.matmul(bank[:, blk * P:(blk + 1) * P], lhsT=S[:, blk * P:(blk + 1) * P],
                                                   rhs=XBC[q][:, HB + 1, cols_of(u)], start=True, stop=True)
                        ins.then_inc(d_written, 1)
                        bank = bank_d(NEW)
                        pe.wait_ge(x_scaled, (tile + 1) * XSLOTS)
                        pe.wait_ge(a_moved, a_no(b, turn_a[u] + 2) + (RING + 1))
                        nc.tensor.matmul(bank[:, :], lhsT=BT[par], rhs=XS[par][:, SUF, :], start=True,
                                         stop=True).then_inc(d_written, 1)
                    if kind == "tail":
                        bank = bank_a(0)
                        if u == 0:
                            pe.wait_ge(w_out_scaled, 1)
                        pe.wait_ge(hg_ready, tile + 3)
                        for blk in range(HB):
                            nc.tensor.matmul(bank[:, 0:DM], lhsT=HG[par][:, blk, :], rhs=W_OUT[:, blk, :],
                                             start=(blk == 0), stop=(blk == HB - 1))
                        pe.wait_ge(sq_ready, tile + 3)
                        nc.tensor.matmul(bank[:, DM:DM + 1], lhsT=SQS[par], rhs=CONST[:, C_ONE, 0:1], start=True,
                                         stop=True).then_inc(a_written, 1)

            pe.wait_ge(a_moved, RING + A_P1 + BATCH * A_BATCH)
            pe.wait_ge(d_moved, RING + D_BASE + BATCH * D_BATCH)

            def turn(k, par, loads):
                pe.wait_ge(fx_loaded[par], loads)
                pe.wait_ge(fy_ready, k + 1)
                for j in range(DK):
                    ins = nc.tensor.transpose(BX[par][:, j * P:(j + 1) * P], FX[par][:, j * P:(j + 1) * P], ident())
                ins.then_inc(fxt_full, 1)

            def gate_up(k, par):
                e = pe.value_load(EXPERT_OF[0:1, bass.ds(k, 1)], min_val=0, max_val=EXPERTS - 1)
                pe.wait_ge(experts_in, e + 1)
                pe.wait_ge(fxt_ready, k + 1)
                for at, bank, full in ((0, BG[par], fg_full), (DK * DFF, BU[par], fu_full)):
                    for j in range(DK):
                        ins = nc.tensor.matmul(bank[:, :], lhsT=FXT[par][:, j, :],
                                               rhs=WEXP_FLAT[:, bass.ds(e * WE + (at + j * DFF), DFF)],
                                               start=(j == 0), stop=(j == DK - 1))
                    ins.then_inc(full, 1)

            def hidden(k, par):
                pe.wait_ge(fh_ready, k + 1)
                for j in range(KF):
                    ins = nc.tensor.transpose(BH[par][:, j * P:(j + 1) * P], FH[par][:, j * P:(j + 1) * P], ident())
                ins.then_inc(fht_full, 1)

            def down(k, par):
                e = pe.value_load(EXPERT_OF[0:1, bass.ds(k, 1)], min_val=0, max_val=EXPERTS - 1)
                pe.wait_ge(fht_ready, k + 1)
                for j in range(KF):
                    ins = nc.tensor.matmul(BX[par][:, DM:2 * DM], lhsT=FHT[par][:, j, :],
                                           rhs=WEXP_FLAT[:, bass.ds(e * WE + (2 * DK * DFF + j * DM), DM)],
                                           start=(j == 0), stop=(j == KF - 1))
                ins.then_inc(fy_full, 1)

            turn(0, 0, 16)
            gate_up(0, 0)
            turn(1, 1, 16)
            gate_up(1, 1)
            turn(2, 0, 32)
            hidden(0, 0)
            with pe.Fori(0, (NT - 3) // 2) as i:
                for par in range(2):
                    k = i * 2 + (2 + par)
                    gate_up(k, par)
                    turn(k + 1, 1 - par, i * 16 + (32 if par == 0 else 48))
                    hidden(k - 1, 1 - par)
                    down(k - 2, par)
            gate_up(NT - 1, 0)
            hidden(NT - 2, 1)
            down(NT - 3, 0)
            hidden(NT - 1, 0)
            pe.wait_ge(fy_ready, NT - 3 + 5)
            down(NT - 2, 1)
            down(NT - 1, 0)

        @block.vector
        def _(dve):
            chain = [0]

            def link(ins):
                chain[0] += 1
                ins.then_inc(dve_chain, 1)
                dve.wait_ge(dve_chain, chain[0])

            def tt(out, a, b, op):
                return nc.vector.tensor_tensor(out=out, in0=a, in1=b, op=op)

            dve.sem_inc(d_moved, RING + D_BASE)
            dve.sem_inc(conv_done, 2)
            dve.sem_inc(hg_ready, 2)
            dve.sem_inc(sq_ready, 2)

            def variances(g):
                tiles = range(g * GT, (g + 1) * GT)
                dve.wait_ge(x_loaded[g], 16)
                for t in tiles:
                    nc.vector.bn_stats(STATS[:, t, :], X[:, t, 0:DM]).then_inc(dve_chain, 1)
                for t in tiles:
                    chain[0] += 1
                    dve.wait_ge(dve_chain, chain[0])
                    nc.vector.bn_aggr(MV[:, t, :], STATS[:, t, :]).then_inc(dve_chain, 1)
                chain[0] += GT
                dve.wait_ge(dve_chain, chain[0])
                nc.vector.tensor_scalar_add(VE[:, g * GT:(g + 1) * GT].unsqueeze(2), MV[:, g * GT:(g + 1) * GT, 1:2],
                                            EPS).then_inc(var_ready, 1)

            variances(0)
            for g in range(GROUPS):
                if g + 1 < GROUPS:
                    variances(g + 1)
                dve.wait_ge(rstd_ready, g + 1)
                if g > 0:
                    dve.wait_ge(xn_kept, g)
                    dve.wait_ge(a_moved, g * 4 + 2)
                for c in range(GT):
                    t = g * GT + c
                    ins = nc.vector.tensor_scalar(XNS[:, c, :], X[:, t, 0:DM], MV[:, t, 0:1], RS[:, t:t + 1],
                                                  ALU.subtract, ALU.mult)
                ins.then_inc(xn_ready, 1)

            def by_expert(ap):
                return ap.rearrange("p (t e) -> p t e", e=EXPERTS)

            def over_tiles(ap):
                return ap.unsqueeze(1).to_broadcast([P, TILES, EXPERTS])

            def over_experts(ap):
                return ap.unsqueeze(2).to_broadcast([P, TILES, EXPERTS])

            dve.wait_ge(consts_in, 16 * 6)
            nc.vector.tensor_scalar(CONVC, CONVC, 0.5, None, ALU.mult).then_inc(taps_halved, 1)
            dve.wait_ge(iota_made, 1)
            nc.vector.tensor_copy(XN[:, :, DM:DM + 1], IOTAK.bitcast(I32).unsqueeze(2))
            link(nc.vector.tensor_copy(IOTAF, IOTA.bitcast(I32)))
            link(nc.vector.tensor_copy(IOTATF, IOTAT.bitcast(I32)))
            dve.wait_ge(sig_ready, 1)
            link(nc.vector.tensor_scalar_add(SIG, SIG, 1.0))
            link(nc.vector.reciprocal(SIG, SIG))
            link(nc.vector.reduce_max(PROB[:, :], by_expert(SIG), AX.X))
            nc.vector.tensor_scalar(XN[:, :, DM + 1:XW], PROB[:, :].unsqueeze(2), 0.5, None, ALU.mult)
            link(tt(by_expert(R1), by_expert(SIG), over_experts(PROB[:, :]), ALU.is_equal))
            link(tt(by_expert(R2), by_expert(R1), over_tiles(IOTAF), ALU.mult))
            link(nc.vector.tensor_reduce(FIRST, by_expert(R2), AX.X, ALU.min))
            tt(by_expert(HOT), over_tiles(IOTAF), over_experts(FIRST), ALU.is_equal).then_inc(hot_ready, 1)
            dve.wait_ge(a_moved, RING + A_P1)
            by_head = DTR.rearrange("p (t c) -> p t c", c=RW)[:, :, 0:HEADS]
            V = SP_V.rearrange("p (t h) -> p t h", h=HEADS)
            tt(V, by_head, HEADV[:, V_BIAS:V_BIAS + HEADS].unsqueeze(1).to_broadcast([P, TILES, HEADS]),
               ALU.add).then_inc(v_ready, 1)
            dve.wait_ge(rank_written, 1)
            nc.vector.tensor_copy(RANK, BD[0][:, 0:TE])
            nc.vector.tensor_copy(TOTS, BD[0][:, TE:2 * TE])
            link(nc.vector.tensor_copy(CUM[0], BD[0][:, TE:2 * TE]))
            src, step = 0, 1
            while step < TILES:
                n = step * EXPERTS
                nc.vector.tensor_copy(CUM[1 - src][:, 0:n], CUM[src][:, 0:n])
                link(tt(CUM[1 - src][:, n:], CUM[src][:, n:], CUM[src][:, 0:TE - n], ALU.add))
                src, step = 1 - src, step * 2
            count = CUM[src][:, TE - EXPERTS:]
            link(nc.vector.tensor_scalar_add(CNTI, count, float(P - 1)))
            link(nc.vector.tensor_single_scalar(CNTS, CNTI, P.bit_length() - 1, ALU.logical_shift_right))
            nc.vector.tensor_copy(CNTF, CNTS)
            link(nc.vector.tensor_copy(ENDS[0], CNTS))
            esrc, step = 0, 1
            while step < EXPERTS:
                nc.vector.tensor_copy(ENDS[1 - esrc][:, 0:step], ENDS[esrc][:, 0:step])
                link(tt(ENDS[1 - esrc][:, step:], ENDS[esrc][:, step:], ENDS[esrc][:, 0:EXPERTS - step], ALU.add))
                esrc, step = 1 - esrc, step * 2
            ends = ENDS[esrc]
            link(tt(LE.rearrange("p (t e) -> p t e", e=EXPERTS), ends.unsqueeze(1).to_broadcast([P, NT, EXPERTS]),
                    IOTATF.rearrange("p (t e) -> p t e", e=EXPERTS), ALU.is_le))
            link(nc.vector.reduce_sum(EXF, LE.rearrange("p (t e) -> p t e", e=EXPERTS)[:, :, 0:EXPERTS - 1], AX.X))
            nc.vector.tensor_copy(EXPERT_OF[:, 0:NT], EXF)
            link(tt(BASE128, ends, CNTF, ALU.subtract))
            link(nc.vector.tensor_scalar(BASE128, BASE128, float(P), None, ALU.mult))
            link(tt(R1, RANK, CUM[src], ALU.add))
            link(tt(R1, R1, TOTS, ALU.subtract))
            link(tt(by_expert(R1), by_expert(R1), over_tiles(BASE128), ALU.add))
            link(tt(R1, R1, HOT, ALU.mult))
            link(nc.vector.reduce_sum(POSF, by_expert(R1), AX.X))
            nc.vector.tensor_copy(POS[:, :], POSF).then_inc(routed, 1)

            dve.wait_ge(u_ready, 1)
            link(nc.vector.tensor_scalar_add(SP_W, SP_U, -0.5))
            link(nc.vector.tensor_scalar(SP_P, SP_W, COEF[-1], COEF[-2], ALU.mult, ALU.add))
            link(tt(SP_P, SP_P, SP_W, ALU.mult))
            for c in COEF[-3:0:-1]:
                link(nc.vector.scalar_tensor_tensor(out=SP_P, in0=SP_P, scalar=c, in1=SP_W, op0=ALU.add, op1=ALU.mult))
            link(nc.vector.scalar_tensor_tensor(out=SP_P, in0=SP_P, scalar=COEF[0], in1=SP_U, op0=ALU.add, op1=ALU.mult))
            link(nc.vector.scalar_tensor_tensor(out=DT[:, :], in0=SP_V, scalar=0.0, in1=SP_P, op0=ALU.max, op1=ALU.add))
            dve.wait_ge(ea_ready, 1)
            nc.vector.scalar_tensor_tensor(
                out=DA[:, :].rearrange("p (t h) -> p t h", h=HEADS), in0=DT[:, :].rearrange("p (t h) -> p t h", h=HEADS),
                scalar=-1.0, in1=EA[:, :].unsqueeze(1).to_broadcast([P, TILES, HEADS]), op0=ALU.mult,
                op1=ALU.mult).then_inc(da_ready, 1)

            def taps(b, q, i):
                par, blk = i % 2, i - HB
                dve.wait_ge(a_moved, a_no(b, conv_a[q, i]) + (RING + 1))
                for j in range(KC - 2, -1, -1):
                    ins = nc.vector.scalar_tensor_tensor(out=ACC[par], in0=RAW[par][:, j:j + GW],
                                                         scalar=CONVC[:, blk, j:j + 1], in1=ACC[par],
                                                         op0=ALU.mult, op1=ALU.add)
                    if j > 0:
                        ins.then_inc(conv_chain, 1)
                        dve.wait_ge(conv_chain, b * (QB * XB * 2) + ((q * XB + blk) * 2 + (KC - 1 - j)))
                ins.then_inc(taps_done, 1)

            def conv_silu(b, q, i):
                dve.wait_ge(tanh_done, b * (QB * XB) + (q * XB + i - HB + 1))
                nc.vector.scalar_tensor_tensor(out=XBC[q][:, i - HB, :], in0=TH[i % 2], scalar=1.0, in1=ACC[i % 2],
                                               op0=ALU.add, op1=ALU.mult).then_inc(conv_done, 1)

            with dve.Fori(0, BATCH) as b:
                for kind, u, i, a0, d0 in STEPS:
                    par, tile, q = u % 2, b * TB + u, u // GT
                    if kind == "conv" and i < HB:
                        dve.wait_ge(a_moved, a_no(b, a0) + (RING + 1))
                        nc.vector.scalar_tensor_tensor(out=GATE[u][:, i, :], in0=TH[i % 2], scalar=1.0,
                                                       in1=GRAW[i % 2], op0=ALU.add, op1=ALU.mult).then_inc(conv_done, 1)
                    if kind == "conv" and i >= HB:
                        taps(b, u, i)
                        if i > HB:
                            conv_silu(b, u, i - 1)
                        if i == BLOCKS - 1:
                            conv_silu(b, u, i)
                    if kind == "head":
                        dve.wait_ge(d_written, b * D_BATCH + (d0 + 1))
                        bank = BD[d0 % RING]
                        for j, m in enumerate((C_ID, C_SHIFT)):
                            nc.vector.tensor_tensor_reduce(
                                out=GJUNK[:, j * P:(j + 1) * P], in0=bank[:, 0:P], in1=CONST[:, m, :], scale=1.0, scalar=0.0,
                                op0=ALU.mult, op1=ALU.add, accum_out=GD[:, j:j + 1]).then_inc(gd_ready, 1)
                        tt(GM[par], bank[:, 0:P].unsqueeze(1).to_broadcast([P, LEVELS - 1, P]),
                           CONST[:, C_MASK:C_MASK + LEVELS - 1, :], ALU.mult).then_inc(d_moved, 1)
                        dve.wait_ge(gd_ready, (tile + 1) * 2)
                        dve.wait_ge(a_moved, a_no(b, pair_a[u - par] + 2) + (RING + 1))
                        dt = heads_of(DT, b, u).unsqueeze(1).to_broadcast([P, 2, HEADS])
                        nc.vector.scalar_tensor_tensor(
                            out=W1[par].rearrange("p (r h) -> p r h", r=2), in0=E[par][:, NEXT, :, :], scalar=GD[:, 1:2],
                            in1=dt, op0=ALU.mult, op1=ALU.mult)
                        nc.vector.scalar_tensor_tensor(
                            out=W0[par].rearrange("p (r h) -> p r h", r=2), in0=dt, scalar=GD[:, 0:1],
                            in1=HEADV[:, V_D:V_D + HEADS].unsqueeze(1).to_broadcast([P, 2, HEADS]),
                            op0=ALU.mult, op1=ALU.add).then_inc(w0_ready, 1)
                    if kind == "mid":
                        dve.wait_ge(a_moved, a_no(b, turn_a[u] + 1) + (RING + 1))

                        def taken(j):
                            return d_no(b, d0 + j) + (RING + 1)

                        def products(lev):
                            return PR[lev % 3][:, 0:HB * 64]

                        def scale(lev):
                            if lev == 0:
                                pairs = XBC[q][:, 0:HB, cols_of(u)].rearrange("p b (q o) -> p b q o", o=2)[:, :, :, 0]
                                decay = ET[par][:, M_NEXT, :].rearrange("p (q o) -> p q o", o=2)[:, :, 0]
                                tt(products(0).rearrange("p (b q) -> p b q", b=HB), pairs,
                                   decay.unsqueeze(1).to_broadcast([P, HB, 64]), ALU.mult).then_inc(p_chain, 1)
                                return
                            if lev % 2 == 1:
                                dve.wait_ge(d_written, b * D_BATCH + (d0 + lev // 2 + 1))
                            m = 1 << lev
                            shape = [P, HB, 64 // m, m]
                            at = ((lev - 1) % 2) * HB * 64
                            z = BD[(d0 + (lev - 1) // 2) % RING][:, at:at + HB * 64].rearrange(
                                "p (b q m) -> p b q m", b=HB, m=m)
                            ins = tt(products(lev).rearrange("p (b q m) -> p b q m", b=HB, m=m), z,
                                     odd(ET[par][:, lev - 1, :], lev).unsqueeze(1).to_broadcast(shape), ALU.mult)
                            ins.then_inc(d_moved if lev % 2 == 0 else p_chain, 1)

                        def add(lev):
                            if lev % 2 == 0 and lev > 0:
                                dve.wait_ge(d_moved, taken((lev - 1) // 2))
                            else:
                                dve.wait_ge(p_chain, tile * P_TILE + ((lev + 1) // 2 + 1))
                            if lev == 0:
                                dve.wait_ge(y0_ready, tile + 1)
                            else:
                                dve.wait_ge(y_chain, tile * Y_TILE + lev)
                            m = 1 << lev
                            y = odd(Y[par], lev)
                            tt(y, y, products(lev).rearrange("p (b q m) -> p b q m", b=HB, m=m),
                               ALU.add).then_inc(y_chain, 1)

                        P_TILE, Y_TILE = (LEVELS + 1) // 2, LEVELS + 1
                        scale(0)
                        for lev in range(1, LEVELS):
                            scale(lev)
                            add(lev - 1)
                        dve.wait_ge(d_written, b * D_BATCH + (d0 + OFF + 1))
                        tt(PR[LEVELS % 3].rearrange("p (b t) -> p b t", b=HB),
                           BD[(d0 + OFF) % RING][:, :].rearrange("p (b t) -> p b t", b=HB),
                           ET[par][:, M_PRE, :].unsqueeze(1).to_broadcast([P, HB, P]), ALU.mult).then_inc(d_moved, 1)
                        add(LEVELS - 1)
                        dve.wait_ge(d_moved, taken(OFF))
                        dve.wait_ge(y_chain, tile * Y_TILE + LEVELS)
                        tt(Y[par], Y[par], PR[LEVELS % 3].rearrange("p (b t) -> p b t", b=HB), ALU.add).then_inc(y_chain, 1)
                        dve.wait_ge(d_written, b * D_BATCH + (d0 + NEW + 1))
                        dve.wait_ge(s1_ready, tile + 3)
                        tt(S, BD[(d0 + NEW) % RING][:, :], S1, ALU.add).then_inc(d_moved, 1)
                        dve.wait_ge(y_chain, (tile + 1) * Y_TILE)
                        dve.wait_ge(a_moved, a_no(b, before(tail_a, A_BATCH, u, 2)) + (RING + 1))
                        tt(HG[par], Y[par], GATE[q][:, :, cols_of(u)], ALU.mult).then_inc(hg_ready, 1)
                    if kind == "norm":
                        dve.wait_ge(sq_made, tile + 1)
                        dve.wait_ge(a_moved, a_no(b, before(tail_a, A_BATCH, u, 2)) + (RING + 1))
                        nc.vector.tensor_reduce(SQS[par], SQ[par].rearrange("p b t -> p t b"), AX.X,
                                                ALU.add).then_inc(sq_ready, 1)

            dve.wait_ge(a_moved, RING + A_P1 + BATCH * A_BATCH)
            nc.vector.tensor_scalar(RNORM[:, :], VARS[:, :], 16 * 0.25 / DIN, 16 * EPS, ALU.mult, ALU.add).then_inc(rn_var, 1)

            dve.sem_inc(fy_ready, 4)

            def expert_half(k, par):
                dve.wait_ge(ft_ready, k + 1)
                nc.vector.scalar_tensor_tensor(out=FG[par], in0=FT[par], scalar=1.0, in1=FG[par],
                                               op0=ALU.add, op1=ALU.mult).then_inc(fa_ready, 1)
                nc.vector.tensor_copy(TOKENS[:, bass.ds(k, 1)], FX[par][:, DM:DM + 1]).then_inc(token_kept, 1)
                dve.wait_ge(fu_full, k + 1)
                dve.wait_ge(fa_ready, k + 1)
                nc.vector.scalar_tensor_tensor(out=FH[par], in0=BU[par][:, :], scalar=FX[par][:, DM + 1:XW], in1=FG[par],
                                               op0=ALU.mult, op1=ALU.mult).then_inc(fh_ready, 1)

            def expert_output(k, par):
                dve.wait_ge(tz_ready, k + 1)
                if not isinstance(k, int) or k >= 2:
                    dve.wait_ge(fy_stored, (k - 1) * 16)
                nc.vector.scalar_tensor_tensor(out=FY[par], in0=TZ[par], scalar=1.0, in1=BX[par][:, DM:2 * DM],
                                               op0=ALU.add, op1=ALU.mult).then_inc(fy_ready, 1)

            expert_half(0, 0)
            expert_half(1, 1)
            for k in range(2):
                expert_half(k + 2, k)
                expert_output(k, k)
            with dve.Fori(1, (NT - 3) // 2) as i:
                for par in range(2):
                    expert_half(i * 2 + (2 + par), par)
                    expert_output(i * 2 + par, par)
            expert_half(NT - 1, 0)
            for k in range(NT - 3, NT):
                expert_output(k, k % 2)

            dve.wait_ge(zx_loaded, 16)
            dve.wait_ge(zo_scaled, 1)
            for g in range(GROUPS - 1):
                cols = slice(g * GT * DM, (g + 1) * GT * DM)
                dve.wait_ge(zf_loaded[g], 16)
                tt(ZF[:, cols], ZF[:, cols], ZO[:, cols], ALU.mult).then_inc(z_made[g], 1)
                dve.wait_ge(z_made[g], 1)
                tt(ZX[:, cols], ZX[:, cols], ZF[:, cols], ALU.add).then_inc(z_out[g], 1)


def kernel(**inputs):
    import concourse.bacc as bacc
    from concourse.bass_utils import run_bass_kernel_spmd

    def get(name):
        return np.ascontiguousarray(inputs[name])

    def by_p(a):
        return a.reshape(HEADS, HD, *a.shape[1:]).swapaxes(0, 1).reshape(a.shape)

    w_in = get("L0_attn_in_proj_w")
    gate, x, bc, dt = w_in[:DIN], w_in[DIN:2 * DIN], w_in[2 * DIN:2 * DIN + 2 * NST], w_in[2 * DIN + 2 * NST:]
    conv = np.concatenate([get("L0_attn_conv_w"), get("L0_attn_conv_b")[:, None]], axis=1)
    conv = np.concatenate([by_p(conv[:DIN]), conv[DIN:]])
    arrays = {
        "x": get("L0_attn_hidden_states").reshape(TOK, DM),
        "w_main": np.concatenate([by_p(gate), by_p(x), bc]).T,
        "w_dr": np.concatenate([dt.T, get("L0_ffn_router_w")], axis=1),
        "conv_c": conv.reshape(XB, P, KC + 1).transpose(1, 0, 2).reshape(P, XB * (KC + 1)),
        "head_v": np.concatenate([get("L0_attn_dt_bias"), get("L0_attn_A_log"), get("L0_attn_D")])[None],
        "norm_c": by_p(get("L0_attn_norm_w")).reshape(HB, P).T,
        "w_out": by_p(get("L0_attn_out_proj_w").T),
        "w_gate": get("L0_ffn_gate_w"),
        "w_up": get("L0_ffn_up_w"),
        "w_down": get("L0_ffn_down_w"),
        "consts": constant_matrices().reshape(P, N_CONST * P),
    }
    arrays = {n: np.ascontiguousarray(a) for n, a in arrays.items()}
    nc = bacc.Bacc("TRN2", target_bir_lowering=False, num_devices=1)
    args = [nc.dram_tensor(f"in_{n}", a.shape, FP32, kind="ExternalInput").ap() for n, a in arrays.items()]
    out = nc.dram_tensor("out_0_dram", [TOK, DM], FP32, kind="ExternalOutput").ap()
    mixer_moe_kernel(nc, *args, out)
    r = run_bass_kernel_spmd(nc, [{f"in_{n}": a for n, a in arrays.items()}], core_ids=[0])
    return r.results[0]["out_0_dram"].reshape(BATCH, SEQ, DM)
```

```python
from contextlib import ExitStack

import concourse.bass as bass
import numpy as np
from concourse import mybir

FP32 = mybir.dt.float32
I32 = mybir.dt.int32
U32 = mybir.dt.uint32
ALU = mybir.AluOpType
ACT = mybir.ActivationFunctionType
AX = mybir.AxisListType

P = 128
BATCH, SEQ, DM = 2, 1024, 256
DIN, HEADS, HD, NST, KC = 512, 64, 8, 128, 4
EXPERTS, DFF = 8, 512
EPS = 1e-5
TOK = BATCH * SEQ
TILES = TOK // P
TB = SEQ // P
GT = 4
GROUPS = TILES // GT
GW = GT * P
QB = TB // GT
DK = DM // P
HB = DIN // P
XB = HB + 2
LEVELS = 7
SUF, PRE, NEXT = LEVELS - 1, LEVELS, LEVELS + 1
SLOTS = NEXT + 1
XSLOTS = SUF + 1
M_PRE, M_NEXT, M_SAME = LEVELS - 1, LEVELS, LEVELS + 1
MAPS = LEVELS + 2
KF = DFF // P
NT = TILES + EXPERTS - 1
WE = DK * DFF * 2 + KF * DM
RW = HEADS + EXPERTS
XW = DM + 2
FXN = 4
CB = 4
RING = 4

C_ID, C_SUM, C_ONE, C_TRI, C_SHIFT = 0, 1, SLOTS + 1, SLOTS + 2, SLOTS + 3
C_MASK = C_SHIFT + 1
N_CONST = C_MASK + LEVELS - 1
D_BASE = 16
V_BIAS, V_ALOG, V_D = 0, HEADS, 2 * HEADS
LOG1P_DEGREE = 9


def constant_matrices():
    k, t = np.arange(P)[:, None], np.arange(P)[None, :]
    mats = [k == t]
    for lev in range(1, LEVELS):
        same = (k >> lev) == (t >> lev)
        mats.append(same & np.where((t >> lev) & 1, k <= t, k > t))
    mats += [k > t, k <= t, k == t + 1, k >= 0 * t, k < t, t == k + 1]
    for lev in range(1, LEVELS):
        mats.append(((k >> lev) & 1 == 0) & ((t >> lev) & 1 == 1) & ((k >> lev + 1) == (t >> lev + 1)))
    return np.stack([m.astype(np.float32) for m in mats], axis=1)


def log1p_coefficients():
    cheb = np.polynomial.chebyshev.Chebyshev.interpolate(
        lambda u: np.log1p(u) / u, LOG1P_DEGREE, domain=[0, 1])
    power = cheb.convert(kind=np.polynomial.Polynomial, domain=[-1, 1], window=[-1, 1])
    return [float(c) for c in power(np.polynomial.Polynomial([0.5, 1.0])).coef]


BLOCKS = HB + XB
CUT = [0, 2, 5, 8]
CHUNKS = {"conv": (1, 0), "pair": (3, 0), "head": (1, 1), "norm": (0, 0), "mid": (0, 5), "turn": (3, 0),
          "tail": (1, 0)}


def steps_of(last):
    cut = CUT + [BLOCKS]
    order = [*range(HB, BLOCKS), *range(HB)]
    steps = []
    for u in range(TB):
        conv = []
        if u < GT or not last:
            conv = [("conv", u // GT + 1, i) for i in order[cut[u % GT]:cut[u % GT + 1]]]
        ahead = u + 1 < TB or not last
        if ahead:
            steps += [("pair", u + 1, 0)] * (u % 2) + [("head", u + 1, 0)]
        early = u + 1 < TB
        steps += conv * early + [("norm", u - 1, 0)] * (u > 0) + [("mid", u, 0)]
        if ahead:
            steps.append(("turn", u + 1, 0))
        steps += conv * (not early)
        steps += [("tail", u - 1, 0)] * (u > 0)
    return steps + [("norm", TB - 1, 0), ("tail", TB - 1, 0)]


def numbered(steps, a, d):
    out = []
    for step in steps:
        out.append((*step, a, d))
        a, d = a + CHUNKS[step[0]][0], d + CHUNKS[step[0]][1]
    return out, a, d


def schedule():
    body, a_batch, d_batch = numbered(steps_of(False), 0, 0)
    last, a_last, d_last = numbered(steps_of(True), 0, 0)
    places = []
    for steps in (body, last):
        where = {(kind, u): (a, d) for kind, u, i, a, d in steps}
        for kind, u, i, a, d in body:
            if kind != "conv" and (u in (TB - 1, TB - 2) or u == TB):
                where[kind, u - TB] = (a - a_batch, d - d_batch)
        places.append(where)
    first = [("pair", 0, 0, *places[0]["pair", 0]), ("head", 0, 0, *places[0]["head", 0]),
             ("turn", 0, 0, *places[0]["turn", 0])]
    a0, d0 = first[0][3] - BLOCKS, first[1][4]
    first = [("conv", 0, i, a0 + i, d0) for i in range(BLOCKS)] + first
    return first, body, last, places, (a_batch, d_batch), (a_last, d_last), (-a0, -d0)


def mixer_moe_kernel(nc, x_in, w_main, w_dr, conv_c, head_v, norm_c, w_out, w_gate, w_up, w_down,
                     consts, out):
    START, BODY, LAST, PLACES, (A_BATCH, D_BATCH), (A_LAST, D_LAST), (A_AHEAD, D_AHEAD) = schedule()
    assert A_BATCH % RING == 0 and D_BATCH % RING == 0
    A_P1 = 4 * GROUPS
    A_OFF, D_OFF = A_P1 + A_AHEAD, D_BASE + D_AHEAD
    A_END = A_OFF + (BATCH - 1) * A_BATCH + A_LAST
    D_END = D_OFF + (BATCH - 1) * D_BATCH + D_LAST
    A_SKIP = -PLACES[0]["turn", 0][0] - CHUNKS["turn"][0]
    D_SKIP = D_AHEAD - CHUNKS["head"][1]
    COEF = log1p_coefficients()

    x_dram = x_in.rearrange("(t p) d -> p t d", p=P)
    out_dram = out.rearrange("(t p) d -> p t d", p=P)
    xs_dram = nc.dram_tensor("x_by_expert", [NT * P, XW], FP32).ap()
    g_dram = nc.dram_tensor("gate_rows", [TOK + 1, DM], FP32).ap()
    o_dram = nc.dram_tensor("mixer_rows", [TOK, DM], FP32).ap()
    xs_tiles = xs_dram.rearrange("(t p) d -> p t d", p=P)
    g_tiles = g_dram[0:TOK, :].rearrange("(t p) d -> p t d", p=P)
    o_tiles = o_dram.rearrange("(t p) d -> p t d", p=P)

    with ExitStack() as ctx:
        def sb(name, cols, dt=FP32):
            return ctx.enter_context(nc.sbuf_tensor(name, [P, cols], dt))

        def sem(name):
            return ctx.enter_context(nc.semaphore(name))

        CONST = sb("CONST", N_CONST * P)[:, :].rearrange("p (m t) -> p m t", m=N_CONST)
        W_MAIN = sb("W_MAIN", DK * 2 * (DIN + P))[:, :].rearrange("p (k n) -> p k n", k=DK)
        W_DR = sb("W_DR", DK * RW)[:, :].rearrange("p (k n) -> p k n", k=DK)
        CONVC = sb("CONVC", XB * 5)[:, :].rearrange("p (b j) -> p b j", j=5)
        HEADV = sb("HEADV", 3 * HEADS)
        NORMC = sb("NORMC", HB)
        W_OUT = sb("W_OUT", HB * DM)[:, :].rearrange("p (b n) -> p b n", b=HB)
        DT = sb("DT", TILES * HEADS)
        DA = sb("DA", TILES * HEADS)
        PROB = sb("PROB", TILES)
        POS = sb("POS", TILES, U32)
        EXPERT_OF = sb("EXPERT_OF", NT + 1, I32)
        VARS = sb("VARS", TILES)
        RNORM = sb("RNORM", TILES)
        MHALF = sb("MHALF", TILES)
        EA = sb("EA", HEADS)
        ZERO = sb("ZERO", XW)[:, :]
        ARENA_COLS = 41740
        ARENA = sb("ARENA", ARENA_COLS)
        EARLY = 4
        WEXP_FLAT = ARENA[:, FXN * XW:FXN * XW + EXPERTS * WE]
        WEXP = WEXP_FLAT.rearrange("p (e c) -> p e c", e=EXPERTS)
        place = [0]

        def part(cols):
            at = place[0]
            place[0] += cols
            assert place[0] <= ARENA_COLS, place[0]
            return ARENA[:, at:at + cols]

        XNT = part(DK * TOK).rearrange("p (k t) -> p k t", k=DK)
        RAW = [part(KC - 1 + GW) for _ in range(CB)]
        HIST = part(XB * (KC - 1)).rearrange("p (b j) -> p b j", b=XB)
        ACC = [part(GW) for _ in range(CB)]
        TH = [raw[:, 0:GW] for raw in RAW]
        XBC, GATE = [], []
        for _ in range(QB):
            XBC.append(part(XB * GW).rearrange("p (b t) -> p b t", b=XB))
            GATE.append(part(HB * GW).rearrange("p (b t) -> p b t", b=HB))
            if len(GATE) == 1:
                assert place[0] >= FXN * XW + EARLY * WE
        conv_end = place[0]
        XS = [part(XSLOTS * DIN).rearrange("p (l c) -> p l c", l=XSLOTS) for _ in range(2)]
        E = [part(SLOTS * P).rearrange("p (l r h) -> p l r h", l=SLOTS, r=2) for _ in range(2)]
        ETOT = [part(HEADS) for _ in range(4)]
        E2 = [part(XSLOTS * HEADS).rearrange("p (l h) -> p l h", l=XSLOTS) for _ in range(2)]
        GM = [part((LEVELS - 1) * P).rearrange("p (l t) -> p l t", l=LEVELS - 1) for _ in range(2)]
        GD = part(2)
        GJUNK = part(2 * P)
        W0 = [part(P) for _ in range(2)]
        W1 = [part(P) for _ in range(2)]
        ET = [part(MAPS * P).rearrange("p (l t) -> p l t", l=MAPS) for _ in range(2)]
        SPW, SPP = part(2 * HEADS), part(2 * HEADS)
        Y = [part(DIN).rearrange("p (b t) -> p b t", b=HB) for _ in range(2)]
        PR = [part(DIN if i == LEVELS % 3 else DIN // 2) for i in range(3)]
        HG = [part(DIN).rearrange("p (b t) -> p b t", b=HB) for _ in range(2)]
        SQS = [part(P) for _ in range(2)]
        SQ = [part(DIN).rearrange("p (b t) -> p b t", b=HB) for _ in range(2)]
        S = part(DIN)
        S1 = part(DIN)
        BT = [part(P) for _ in range(2)]
        XT = [part(DIN) for _ in range(2)]
        O = [part(DM) for _ in range(2)]


        place[0] = conv_end
        X = part(TILES * XW).rearrange("p (t d) -> p t d", d=XW)
        XN = X
        XNS = [part(GT * DM).rearrange("p (c d) -> p c d", c=GT) for _ in range(2)]
        XTS = [part(GT * DM).rearrange("p (c k t) -> p c k t", c=GT, k=DK) for _ in range(2)]
        STATS = part(TILES * 6).rearrange("p (t s) -> p t s", t=TILES)
        MV = part(TILES * 2).rearrange("p (t s) -> p t s", t=TILES)
        VE = part(TILES)
        RS = part(TILES)
        DTR = part(TILES * RW)
        TE = TILES * EXPERTS
        SIG, R1, R2, HOT, RANK, TOTS = (part(TE) for _ in range(6))
        CUM = [part(TE), part(TE)]
        IOTA, IOTAF = part(EXPERTS), part(EXPERTS)
        IOTAT, IOTATF = part(NT * EXPERTS), part(NT * EXPERTS)
        FIRST = part(TILES)
        CNTI, CNTS = part(EXPERTS).bitcast(I32), part(EXPERTS).bitcast(I32)
        CNTF, BASE128 = part(EXPERTS), part(EXPERTS)
        ENDS = [part(EXPERTS), part(EXPERTS)]
        LE = part(NT * EXPERTS)
        EXF = part(NT)
        POSF = part(TILES)
        IOTAK = part(TILES)

        place[0] = 0
        FX = [part(XW) for _ in range(FXN)]
        place[0] = FXN * XW + EXPERTS * WE
        FXT = [part(DM).rearrange("p (k t) -> p k t", k=DK) for _ in range(2)]
        FT = [part(DFF) for _ in range(2)]
        FG = [part(DFF) for _ in range(2)]
        FH = [part(DFF) for _ in range(2)]
        FHT = [part(DFF).rearrange("p (k t) -> p k t", k=KF) for _ in range(2)]
        TZ = [part(DM) for _ in range(2)]
        FY = [part(DM) for _ in range(2)]
        TOKENS = part(NT).bitcast(U32)
        IDX_SEEN = part(1)
        IDX = [part(1).bitcast(U32) for _ in range(2)]
        ZX = part(TILES * DM)
        ZO = part(TILES * DM)
        place[0] = 0
        ZF = part(TILES * DM)

        BA = [ctx.enter_context(nc.psum_tensor(f"BA{i}", [P, 512], FP32)) for i in range(RING)]
        BD = [ctx.enter_context(nc.psum_tensor(f"BD{i}", [P, 512], FP32)) for i in range(RING)]

        def sems(names):
            return [sem(n) for n in names.split()]

        a_written, a_moved, d_written, d_moved = sems("a_written a_moved d_written d_moved")
        dve_chain, sp_chain, pool_chain = sems("dve_chain sp_chain pool_chain")
        x_loaded = [sem(f"x_loaded{g}") for g in range(GROUPS)]
        ident_in, consts_in, w_loaded, iota_made, zero_made, slots_zeroed = sems(
            "ident_in consts_in w_loaded iota_made zero_made slots_zeroed")
        var_ready, rstd_ready, xn_ready, xn_kept = sems("var_ready rstd_ready xn_ready xn_kept")
        abs_ready, u_ready, ea_ready, da_ready, sig_ready, hot_ready = sems(
            "abs_ready u_ready ea_ready da_ready sig_ready hot_ready")
        v_ready, rank_written, routed, scattered, w_out_scaled, taps_halved = sems(
            "v_ready rank_written routed scattered w_out_scaled taps_halved")
        conv_done, gates_made, taps_done, tanh_done = sems("conv_done gates_made taps_done tanh_done")
        e2_ready, x_scaled, s1_ready, y0_ready = sems("e2_ready x_scaled s1_ready y0_ready")
        w0_ready, hg_ready, sq_made, sq_ready, p_chain, y_chain = sems(
            "w0_ready hg_ready sq_made sq_ready p_chain y_chain")
        conv_chain, gd_ready = sems("conv_chain gd_ready")
        o_stored = sems("o_stored0 o_stored1")
        expert_loaded = [sem(f"expert_loaded{e}") for e in range(EXPERTS)]
        experts_in = sem("experts_in")
        fx_loaded = [sem(f"fx_loaded{i}") for i in range(FXN)]
        fy_stored = sem("fy_stored")
        fxt_full, fxt_ready, fg_full, fu_full, ft_ready, fa_ready, fh_ready, fht_full, fht_ready, fy_full = sems(
            "fxt_full fxt_ready fg_full fu_full ft_ready fa_ready fh_ready fht_full fht_ready fy_full")
        tz_ready, fy_ready, token_kept, idx_made = sems("tz_ready fy_ready token_kept idx_made")
        zx_loaded, zo_loaded, rn_var, rn_ready, zo_scaled, z_stored = sems(
            "zx_loaded zo_loaded rn_var rn_ready zo_scaled z_stored")
        zf_loaded = [sem(f"zf_loaded{g}") for g in range(GROUPS)]
        z_made, z_out = ([sem(f"{n}{g}") for g in range(GROUPS)] for n in ("z_made", "z_out"))

        block = ctx.enter_context(nc.Block())

        def ident():
            return CONST[:, C_ID, :]

        def odd(ap, lev):
            m = 1 << lev
            if len(ap.shape) == 2:
                return ap.rearrange("p (q o m) -> p q o m", o=2, m=m)[:, :, 1, :]
            return ap.rearrange("p b (q o m) -> p b q o m", o=2, m=m)[:, :, :, 1, :]

        BX, BG, BU, BH = ([BA[0], BD[0]], [BA[1], BD[1]], [BA[2], BD[2]], [BA[3], BD[3]])
        Z_CHUNKS = (LEVELS - 1) // 2
        OFF, NEW = Z_CHUNKS, Z_CHUNKS + 1

        def a_no(b, i):
            return b * A_BATCH + (A_OFF + i)

        def d_no(b, i):
            return b * D_BATCH + (D_OFF + i)

        def bank_of_a(i):
            return BA[(A_OFF + i) % RING]

        def bank_of_d(i):
            return BD[(D_OFF + i) % RING]

        def place_of(q, i):
            return q * BLOCKS + (i if q == 0 else (i - HB) % BLOCKS)

        def skipped(u, count):
            return count if u == 0 else 0

        def run_first(step):
            for s in START[:CB - 1]:
                step(0, PLACES[0], *s)

        def run(engine, step, between=lambda n: None):
            for n, s in enumerate(START[CB - 1:]):
                step(0, PLACES[0], *s)
                between(n)
            with engine.Fori(0, BATCH - 1) as b:
                for s in BODY:
                    step(b, PLACES[0], *s)
            for s in LAST:
                step(BATCH - 1, PLACES[1], *s)

        def cols_of(u):
            return slice((u % GT) * P, (u % GT + 1) * P)

        def heads_of(ap, b, u):
            return ap[:, bass.ds(b * (TB * HEADS) + u * HEADS, HEADS)]

        def load_expert(e):
            signal = expert_loaded[e]
            nc.sync.dma_start(WEXP[:, e, 0:DK * DFF].rearrange("p (k n) -> p k n", k=DK),
                            w_gate[e].rearrange("(k p) n -> p k n", p=P)).then_inc(signal, 16)
            nc.sync.dma_start(WEXP[:, e, DK * DFF:2 * DK * DFF].rearrange("p (k n) -> p k n", k=DK),
                            w_up[e].rearrange("(k p) n -> p k n", p=P)).then_inc(signal, 16)
            nc.sync.dma_start(WEXP[:, e, 2 * DK * DFF:].rearrange("p (k n) -> p k n", k=KF),
                            w_down[e].rearrange("(k p) n -> p k n", p=P)).then_inc(signal, 16)

        @block.sync
        def _(sp):
            consts_dram = consts.rearrange("p (m t) -> p m t", m=N_CONST)
            for g in range(GROUPS):
                if g == 1:
                    sp.dma_start(CONST[:, 0:C_SUM, :], consts_dram[:, 0:C_SUM, :]).then_inc(ident_in, 16)
                    sp.dma_start(W_DR, w_dr.rearrange("(k p) n -> p k n", p=P)).then_inc(ident_in, 16)
                sp.dma_start(X[:, g * GT:(g + 1) * GT, 0:DM],
                             x_dram[:, g * GT:(g + 1) * GT, :]).then_inc(x_loaded[g], 16)
            sp.dma_start(CONST[:, C_SUM:, :], consts_dram[:, C_SUM:, :]).then_inc(consts_in, 16)
            sp.dma_start(HEADV[:, :], head_v[0:1, :].to_broadcast([P, 3 * HEADS])).then_inc(consts_in, 16)
            sp.dma_start(CONVC, conv_c.rearrange("p (b j) -> p b j", j=KC + 1)).then_inc(consts_in, 16)
            sp.dma_start(NORMC[:, :], norm_c).then_inc(consts_in, 16)
            sp.dma_start(W_OUT, w_out.rearrange("(b p) n -> p b n", p=P)).then_inc(consts_in, 16)
            sp.dma_start(W_MAIN, w_main.rearrange("(k p) n -> p k n", p=P)).then_inc(w_loaded, 16)
            sp.wait_ge(zero_made, 1)
            sp.dma_start(xs_tiles, ZERO.unsqueeze(1).to_broadcast([P, NT, XW])).then_inc(slots_zeroed, 16)

            for par in range(2):
                sp.sem_inc(o_stored[par], 16)

            def store_mixer(b, where, u):
                sp.wait_ge(a_moved, a_no(b, where["tail", u][0]) + (RING + 1))
                sp.dma_start(o_tiles[:, bass.ds(b * TB + u, 1), :], O[u % 2].unsqueeze(1)).then_inc(o_stored[u % 2], 16)

            with sp.Fori(0, BATCH - 1) as b:
                for u in range(TB):
                    store_mixer(b, PLACES[0], u)
            for u in range(TB):
                store_mixer(BATCH - 1, PLACES[1], u)
                if u == GT:
                    sp.wait_ge(hg_ready, 2 + (BATCH - 1) * TB + GT)
                    sp.wait_ge(scattered, 16 * TILES)
                    for k in range(FXN):
                        sp.dma_start(FX[k].unsqueeze(1), xs_tiles[:, k:k + 1, :]).then_inc(fx_loaded[k], 16)
                    for e in range(EARLY):
                        load_expert(e)
            for par in range(2):
                sp.wait_ge(o_stored[par], 16 + 16 * (TILES // 2))
            for e in range(EARLY, EXPERTS):
                load_expert(e)
            def load_x(k, slot):
                sp.wait_ge(fh_ready, k - (FXN - 1))
                sp.dma_start(FX[slot].unsqueeze(1), xs_tiles[:, bass.ds(k, 1), :]).then_inc(fx_loaded[slot], 16)

            with sp.Fori(1, NT // FXN) as i:
                for slot in range(FXN):
                    load_x(i * FXN + slot, slot)
            for k in range(NT // FXN * FXN, NT):
                load_x(k, k % FXN)
            sp.wait_ge(fy_stored, 16 * NT)
            for g in range(GROUPS):
                sp.dma_start(ZF[:, g * GT * DM:(g + 1) * GT * DM].rearrange("p (t d) -> p t d", d=DM),
                             g_tiles[:, g * GT:(g + 1) * GT, :]).then_inc(zf_loaded[g], 16)
            for g in range(GROUPS):
                sp.wait_ge(z_out[g], 1)
                sp.dma_start(out_dram[:, g * GT:(g + 1) * GT, :],
                             ZX[:, g * GT * DM:(g + 1) * GT * DM].rearrange("p (t d) -> p t d", d=DM)).then_inc(z_stored, 16)
            sp.wait_ge(z_stored, 16 * GROUPS)

        @block.gpsimd
        def _(pool):
            pool.sem_inc(e2_ready, 2)
            pool.sem_inc(s1_ready, 2)
            nc.gpsimd.memset(ZERO[:, 0:DM], 0.0)
            nc.gpsimd.memset(ZERO[:, DM:DM + 1], float(TOK))
            nc.gpsimd.memset(ZERO[:, DM + 1:XW], 0.0).then_inc(zero_made, 1)
            nc.gpsimd.memset(MHALF[:, :], -0.5)
            nc.gpsimd.iota(IOTA.bitcast(I32), pattern=[[1, EXPERTS]], base=-EXPERTS,
                           channel_multiplier=0)
            nc.gpsimd.iota(IOTAK.bitcast(I32), pattern=[[P, TILES]], base=0, channel_multiplier=1)
            nc.gpsimd.iota(IOTAT.bitcast(I32).rearrange("p (t e) -> p t e", e=EXPERTS),
                           pattern=[[1, NT], [0, EXPERTS]], base=0, channel_multiplier=0).then_inc(iota_made, 1)
            pool.wait_ge(iota_made, 1)
            with pool.Fori(0, GROUPS) as g:
                pool.wait_ge(var_ready, g + 1)
                nc.gpsimd.tensor_tensor(out=RS[:, bass.ds(g * GT, GT)], in0=VE[:, bass.ds(g * GT, GT)],
                                        in1=MHALF[:, 0:GT], op=ALU.pow).then_inc(rstd_ready, 1)
            for kind, u, i, a0, d0 in START[:HB]:
                pool.wait_ge(a_moved, a_no(0, a0) + (RING + 1))
                nc.gpsimd.tensor_scalar(TH[i], TH[i], 1.0, None, ALU.add).then_inc(pool_chain, 1)
                pool.wait_ge(pool_chain, i + 1)
                nc.gpsimd.tensor_tensor(out=GATE[0][:, i, :], in0=TH[i], in1=ACC[i],
                                        op=ALU.mult).then_inc(gates_made, 1)
            pool.wait_ge(routed, 1)
            pool.wait_ge(slots_zeroed, 16)
            pool.wait_ge(xn_kept, GROUPS)
            for t in range(TILES):
                pool.indirect_dma_start(
                    out=xs_dram, out_offset=bass.IndirectOffsetOnAxis(ap=POS[:, t:t + 1], axis=0),
                    in_=XN[:, t, :], in_offset=None).then_inc(scattered, 16)
            pool.wait_ge(scattered, 16 * TILES)

            pool.wait_ge(da_ready, 1)

            def pool_step(b, where, kind, u, _, a0, d0):
                if kind == "mid":
                    par, q, tile = u % 2, u // GT, b * TB + u
                    dt = heads_of(DT, b, u)
                    pool.wait_ge(s1_ready, tile + 2)
                    pool.wait_ge(a_moved, a_no(b, where["pair", u - par][0] + 1) + (RING + 1))
                    nc.gpsimd.tensor_tensor(
                        out=E2[par], in0=E[par][:, 0:XSLOTS, 0, :],
                        in1=dt.unsqueeze(1).to_broadcast([P, XSLOTS, HEADS]), op=ALU.mult).then_inc(e2_ready, 1)
                    pool.wait_ge(e2_ready, tile + 3)
                    pool.wait_ge(a_moved, a_no(b, where["head", u][0]) + (RING + 1))
                    for slot in range(XSLOTS):
                        chunk = slot // 2 if slot < SUF else NEW
                        pool.wait_ge(d_moved, d_no(b, where["mid", u - 2][1] + chunk) + (RING + 1))
                        nc.gpsimd.tensor_tensor(
                            out=XS[par][:, slot, :].rearrange("p (a h) -> p a h", a=HD),
                            in0=E2[par][:, slot, :].unsqueeze(1).to_broadcast([P, HD, HEADS]),
                            in1=XT[par].rearrange("p (a h) -> p a h", a=HD), op=ALU.mult).then_inc(x_scaled, 1)
                    pool.wait_ge(a_moved, a_no(b, where["turn", u][0] + 2) + (RING + 1))
                    pool.wait_ge(hg_ready, tile + 1)
                    nc.gpsimd.tensor_tensor(
                        out=Y[par], in0=XBC[q % QB][:, 0:HB, cols_of(u)],
                        in1=ET[par][:, M_SAME, :].unsqueeze(1).to_broadcast([P, HB, P]),
                        op=ALU.mult).then_inc(y0_ready, 1)
                    pool.wait_ge(d_moved, d_no(b, where["mid", u - 1][1] + NEW) + (RING + 1))
                    if u == 0:
                        zero = ZERO[:, 0:DM].unsqueeze(1).to_broadcast([P, DIN // DM, DM])
                        nc.gpsimd.tensor_tensor(out=S1.rearrange("p (r d) -> p r d", d=DM), in0=zero, in1=zero,
                                                op=ALU.add).then_inc(s1_ready, 1)
                    else:
                        nc.gpsimd.tensor_tensor(
                            out=S1.rearrange("p (a h) -> p a h", a=HD), in0=S.rearrange("p (a h) -> p a h", a=HD),
                            in1=ETOT[u % 4].unsqueeze(1).to_broadcast([P, HD, HEADS]),
                            op=ALU.mult).then_inc(s1_ready, 1)

            run(pool, pool_step)

            pool.wait_ge(rn_var, 1)
            nc.gpsimd.tensor_tensor(out=RNORM[:, :], in0=RNORM[:, :], in1=MHALF[:, :], op=ALU.pow).then_inc(rn_ready, 1)
            for e in range(EXPERTS):
                pool.wait_ge(expert_loaded[e], 3 * 16)
                pool.sem_inc(experts_in, 1)
            for par in range(2):
                pool.wait_ge(o_stored[par], 16 + 16 * (TILES // 2))
            pool.dma_start(ZO.rearrange("p (t d) -> p t d", d=DM), o_tiles).then_inc(zo_loaded, 16)
            pool.dma_start(ZX.rearrange("p (t d) -> p t d", d=DM), x_dram).then_inc(zx_loaded, 16)

            def scatter_y(k, par):
                pool.wait_ge(token_kept, k + 1)
                nc.gpsimd.tensor_tensor(out=IDX[par], in0=TOKENS[:, bass.ds(k, 1)], in1=ZERO[:, 0:1].bitcast(U32),
                                        op=ALU.add).then_inc(idx_made, 1)
                pool.wait_ge(fy_ready, k + 5)
                if not (isinstance(k, int) and k == 0):
                    pool.wait_ge(fy_stored, k * 16)
                pool.wait_ge(idx_made, k + 1)
                nc.gpsimd.tensor_tensor(out=IDX_SEEN, in0=ZERO[:, 0:1], in1=ZERO[:, 0:1], op=ALU.add)
                pool.indirect_dma_start(
                    out=g_dram, out_offset=bass.IndirectOffsetOnAxis(ap=IDX[par], axis=0),
                    in_=FY[par], in_offset=None).then_inc(fy_stored, 16)

            HALF = NT // 4 * 2
            for k in range(2):
                scatter_y(k, k)
            with pool.Fori(1, HALF // 2) as i:
                for par in range(2):
                    scatter_y(i * 2 + par, par)
            pool.wait_ge(rn_ready, 1)
            pool.wait_ge(zo_loaded, 16)
            nc.gpsimd.tensor_tensor(
                out=ZO.rearrange("p (t d) -> p t d", d=DM), in0=ZO.rearrange("p (t d) -> p t d", d=DM),
                in1=RNORM[:, :].unsqueeze(2).to_broadcast([P, TILES, DM]), op=ALU.mult).then_inc(zo_scaled, 1)
            with pool.Fori(HALF // 2, (NT - 1) // 2) as i:
                for par in range(2):
                    scatter_y(i * 2 + par, par)
            scatter_y(NT - 1, 0)
            pool.wait_ge(zo_scaled, 1)
            pool.wait_ge(zx_loaded, 16)
            g = GROUPS - 1
            cols = slice(g * GT * DM, (g + 1) * GT * DM)
            pool.wait_ge(zf_loaded[g], 16)
            nc.gpsimd.tensor_tensor(out=ZF[:, cols], in0=ZF[:, cols], in1=ZO[:, cols], op=ALU.mult).then_inc(z_made[g], 1)
            pool.wait_ge(z_made[g], 1)
            nc.gpsimd.tensor_tensor(out=ZX[:, cols], in0=ZX[:, cols], in1=ZF[:, cols], op=ALU.add).then_inc(z_out[g], 1)

        @block.scalar
        def _(act):
            act.sem_inc(a_moved, RING)
            with act.Fori(0, GROUPS // 2) as half:
                for par in range(2):
                    g = half * 2 + par
                    for h in range(2):
                        act.wait_ge(a_written, g * 4 + (h + 1))
                        nc.scalar.activation(XTS[par][:, 2 * h:2 * h + 2, :, :],
                                             BA[h][:, :].rearrange("p (c k t) -> p c k t", c=2, k=DK), ACT.Copy)
                        for c in range(2):
                            ins = nc.scalar.activation(
                                XNT[:, :, bass.ds(g * GW + (2 * h + c) * P, P)],
                                BA[h][:, c * DM:(c + 1) * DM].rearrange("p (k t) -> p k t", k=DK), ACT.Copy)
                        ins.then_inc(a_moved, 1)
                    nc.scalar.activation(XN[:, bass.ds(g * GT, GT), 0:DM], XNS[par], ACT.Copy).then_inc(xn_kept, 1)
                    for h in range(2):
                        act.wait_ge(a_written, g * 4 + (2 + h + 1))
                        nc.scalar.activation(DTR[:, bass.ds(g * (GT * RW) + 2 * h * RW, 2 * RW)],
                                             BA[2 + h][:, 0:2 * RW], ACT.Copy).then_inc(a_moved, 1)
            act.wait_ge(consts_in, 16 * 5)
            nc.scalar.activation(EA[:, :], HEADV[:, V_ALOG:V_ALOG + HEADS], ACT.Exp).then_inc(ea_ready, 1)
            act.wait_ge(a_moved, RING + A_P1)
            nc.scalar.activation(SIG.rearrange("p (t e) -> p t e", e=EXPERTS),
                                 DTR.rearrange("p (t c) -> p t c", c=RW)[:, :, HEADS:], ACT.Exp,
                                 scale=-1.0).then_inc(sig_ready, 1)
            def conv_block(b, q, i, a0):
                par, blk = place_of(q, i) % CB, i - HB
                bank = bank_of_a(a0)
                act.wait_ge(a_written, a_no(b, a0) + 1)
                if q > 0 or i >= HB + CB:
                    act.wait_ge(conv_done, b * (QB * BLOCKS) + (place_of(q, i) + 1))
                elif i >= CB:
                    act.wait_ge(gates_made, i - CB + 1)
                if i < HB:
                    nc.scalar.activation(TH[par], bank[:, :], ACT.Tanh, scale=0.5)
                    nc.scalar.activation(ACC[par], bank[:, :], ACT.Copy).then_inc(a_moved, 1)
                    return
                before = HIST[:, blk, :] if q % QB else ZERO[:, 0:KC - 1]
                nc.scalar.activation(RAW[par][:, 0:KC - 1], before, ACT.Copy)
                nc.scalar.activation(RAW[par][:, KC - 1:], bank[:, :], ACT.Copy)
                ins = nc.scalar.activation(ACC[par], bank[:, :], ACT.Identity, scale=CONVC[:, blk, KC - 1:KC],
                                           bias=CONVC[:, blk, KC:KC + 1])
                if q % QB == 0:
                    ins = nc.scalar.activation(HIST[:, blk, :], bank[:, GW - (KC - 1):GW], ACT.Copy)
                ins.then_inc(a_moved, 1)

            def conv_tanh(b, q, i):
                act.wait_ge(taps_done, b * (QB * XB) + (q * XB + i - HB + 1))
                nc.scalar.activation(TH[place_of(q, i) % CB], ACC[place_of(q, i) % CB], ACT.Tanh).then_inc(tanh_done, 1)

            def act_step(b, where, kind, u, i, a0, d0):
                par, tile = u % 2, b * TB + u
                if kind == "conv":
                    conv_block(b, u, i, a0)
                    if i > HB:
                        conv_tanh(b, u, i - 1)
                    if i == BLOCKS - 1:
                        conv_tanh(b, u, i)
                if kind == "pair":
                    act.wait_ge(e2_ready, tile + 2)
                    for j in range(2):
                        act.wait_ge(a_written, a_no(b, a0 + j) + 1)
                        sums = bank_of_a(a0 + j)[:, :].rearrange("p (l c h) -> p l c h", c=2, h=HEADS)
                        for c in range(2):
                            ins = nc.scalar.activation(
                                E[c][:, 4 * j:4 * j + 4, :, :],
                                sums[:, :, c, :].unsqueeze(2).to_broadcast([P, 4, 2, HEADS]), ACT.Exp)
                        ins.then_inc(a_moved, 1)
                    act.wait_ge(a_written, a_no(b, a0 + 2) + 1)
                    bank = bank_of_a(a0 + 2)
                    for c in range(2):
                        nc.scalar.activation(
                            E[c][:, NEXT, :, :],
                            bank[:, c * HEADS:(c + 1) * HEADS].unsqueeze(1).to_broadcast([P, 2, HEADS]), ACT.Exp)
                        ins = nc.scalar.activation(ETOT[u % 4 + c], bank[:, (2 + c) * HEADS:(3 + c) * HEADS], ACT.Exp)
                    ins.then_inc(a_moved, 1)
                if kind == "head":
                    act.wait_ge(s1_ready, tile + 1)
                    act.wait_ge(a_written, a_no(b, a0) + 1)
                    nc.scalar.activation(XT[par], bank_of_a(a0)[:, :], ACT.Copy).then_inc(a_moved, 1)
                if kind == "turn":
                    act.wait_ge(hg_ready, tile + 1)
                    for j in range(2):
                        act.wait_ge(a_written, a_no(b, a0 + j) + 1)
                        nc.scalar.activation(ET[par][:, 4 * j:4 * j + 4, :],
                                             bank_of_a(a0 + j)[:, :].rearrange("p (l t) -> p l t", l=4),
                                             ACT.Copy).then_inc(a_moved, 1)
                    act.wait_ge(a_written, a_no(b, a0 + 2) + 1)
                    bank = bank_of_a(a0 + 2)
                    nc.scalar.activation(BT[par], bank[:, 0:P], ACT.Copy)
                    nc.scalar.activation(ET[par][:, M_SAME, :], bank[:, P:2 * P], ACT.Copy).then_inc(
                        a_moved, 1 + skipped(u, A_SKIP))
                if kind == "norm":
                    act.wait_ge(hg_ready, tile + 3)
                    act.wait_ge(sq_ready, tile + 1)
                    nc.scalar.activation(SQ[par], HG[par], ACT.Square).then_inc(sq_made, 1)
                if kind == "tail":
                    act.wait_ge(a_written, a_no(b, a0) + 1)
                    act.wait_ge(o_stored[par], b * (8 * TB) + (16 * (u // 2) + 16))
                    nc.scalar.activation(VARS[:, bass.ds(tile, 1)], bank_of_a(a0)[:, DM:DM + 1], ACT.Copy)
                    nc.scalar.activation(O[par], bank_of_a(a0)[:, 0:DM], ACT.Copy).then_inc(a_moved, 1)

            act.wait_ge(taps_halved, 1)
            act.wait_ge(zero_made, 1)
            run_first(act_step)
            act.wait_ge(v_ready, 1)
            nc.scalar.activation(DA[:, :], DT[:, :], ACT.Abs).then_inc(abs_ready, 1)
            act.wait_ge(abs_ready, 1)
            nc.scalar.activation(DA[:, :], DA[:, :], ACT.Exp, scale=-1.0).then_inc(u_ready, 1)
            for blk in range(HB):
                ins = nc.scalar.activation(W_OUT[:, blk, :], W_OUT[:, blk, :], ACT.Copy, scale=NORMC[:, blk:blk + 1])
            ins.then_inc(w_out_scaled, 1)
            run(act, act_step)


            def gate(k, par):
                act.wait_ge(fg_full, k + 1)
                nc.scalar.activation(FT[par], BG[par][:, :], ACT.Tanh, scale=0.5)
                nc.scalar.activation(FG[par], BG[par][:, :], ACT.Copy).then_inc(ft_ready, 1)

            def turned(k, par):
                act.wait_ge(fxt_full, k + 1)
                nc.scalar.activation(FXT[par], BX[par][:, 0:DM].rearrange("p (k t) -> p k t", k=DK),
                                     ACT.Copy).then_inc(fxt_ready, 1)

            def hidden(k, par):
                act.wait_ge(fht_full, k + 1)
                nc.scalar.activation(FHT[par], BH[par][:, :].rearrange("p (k t) -> p k t", k=KF),
                                     ACT.Copy).then_inc(fht_ready, 1)

            def output(k, par):
                act.wait_ge(fy_full, k + 1)
                nc.scalar.activation(TZ[par], BX[par][:, DM:2 * DM], ACT.Tanh, scale=0.5).then_inc(tz_ready, 1)

            turned(0, 0)
            gate(0, 0)
            turned(1, 1)
            gate(1, 1)
            turned(2, 0)
            hidden(0, 0)
            with act.Fori(0, (NT - 3) // 2) as i:
                for par in range(2):
                    k = i * 2 + (2 + par)
                    gate(k, par)
                    turned(k + 1, 1 - par)
                    hidden(k - 1, 1 - par)
                    output(k - 2, par)
            gate(NT - 1, 0)
            hidden(NT - 2, 1)
            output(NT - 3, 0)
            hidden(NT - 1, 0)
            output(NT - 2, 1)
            output(NT - 1, 0)

        @block.tensor
        def _(pe):
            pe.wait_ge(ident_in, 16 * 2)
            with pe.Fori(0, GROUPS // 2) as half:
                for par in range(2):
                    g = half * 2 + par
                    for h in range(2):
                        pe.wait_ge(a_moved, g * 4 + (h + 1))
                        pe.wait_ge(xn_ready, g + 1)
                        for c in range(2):
                            for k in range(DK):
                                ins = nc.tensor.transpose(BA[h][:, c * DM + k * P:c * DM + (k + 1) * P],
                                                          XNS[par][:, 2 * h + c, k * P:(k + 1) * P], ident())
                        ins.then_inc(a_written, 1)
                    for h in range(2):
                        pe.wait_ge(a_moved, g * 4 + (RING + h + 1))
                        for c in range(2):
                            for k in range(DK):
                                ins = nc.tensor.matmul(BA[2 + h][:, c * RW:(c + 1) * RW], lhsT=XTS[par][:, 2 * h + c, k, :],
                                                       rhs=W_DR[:, k, :], start=(k == 0), stop=(k == DK - 1))
                        ins.then_inc(a_written, 1)
            def pe_step(b, where, kind, u, i, a0, d0):
                par, tile, q = u % 2, b * TB + u, u // GT

                def bank_a(j):
                    pe.wait_ge(a_moved, a_no(b, a0 + j) + 1)
                    return bank_of_a(a0 + j)

                def bank_d(j):
                    pe.wait_ge(d_moved, d_no(b, d0 + j) + 1)
                    return bank_of_d(d0 + j)

                if kind == "conv":
                    bank = bank_a(0)
                    for k in range(DK):
                        ins = nc.tensor.matmul(
                            bank[:, :], lhsT=W_MAIN[:, k, i * P:(i + 1) * P],
                            rhs=XNT[:, k, bass.ds(b * SEQ + u * GW, GW)], start=(k == 0), stop=(k == DK - 1))
                    ins.then_inc(a_written, 1)
                if kind == "pair":
                    pe.wait_ge(da_ready, b * (TB // 2) + (u // 2 + 1))
                    da = DA[:, bass.ds(b * (TB * HEADS) + u * HEADS, 2 * HEADS)]
                    for j in range(2):
                        bank = bank_a(j)
                        for slot in range(4 * j, 4 * j + 4):
                            ins = nc.tensor.matmul(bank[:, (slot % 4) * 2 * HEADS:(slot % 4 + 1) * 2 * HEADS],
                                                   lhsT=CONST[:, C_SUM + slot, :], rhs=da, start=True, stop=True)
                        ins.then_inc(a_written, 1)
                    bank = bank_a(2)
                    for j, m in enumerate((C_SUM + NEXT, C_ONE)):
                        ins = nc.tensor.matmul(bank[:, j * 2 * HEADS:(j + 1) * 2 * HEADS], lhsT=CONST[:, m, :],
                                               rhs=da, start=True, stop=True)
                    ins.then_inc(a_written, 1)
                if kind == "head":
                    pe.wait_ge(conv_done, b * (QB * BLOCKS) + (CB + q * BLOCKS + (BLOCKS if u == 0 else XB)))
                    bank = bank_d(0)
                    nc.tensor.matmul(bank[:, 0:P], lhsT=XBC[q % QB][:, HB, cols_of(u)],
                                     rhs=XBC[q % QB][:, HB + 1, cols_of(u)], start=True,
                                     stop=True).then_inc(d_written, 1 + skipped(u, D_SKIP))
                    bank = bank_a(0)
                    for blk in range(HB):
                        ins = nc.tensor.transpose(bank[:, blk * P:(blk + 1) * P], XBC[q % QB][:, blk, cols_of(u)], ident())
                    ins.then_inc(a_written, 1)
                if kind == "turn":
                    pe.wait_ge(a_moved, a_no(b, where["pair", u - par][0] + 2) + (RING + 1))
                    by_token = [E[par][:, slot, :, :].rearrange("p r h -> p (r h)")
                                for slot in [*range(LEVELS - 1), PRE]] + [W1[par]]
                    for j in range(2):
                        bank = bank_a(j)
                        if j == 1:
                            pe.wait_ge(w0_ready, tile + 1)
                        for at in range(4):
                            ins = nc.tensor.transpose(bank[:, at * P:(at + 1) * P], by_token[4 * j + at], ident())
                        ins.then_inc(a_written, 1)
                    bank = bank_a(2)
                    nc.tensor.transpose(bank[:, 0:P], XBC[q % QB][:, HB, cols_of(u)], ident())
                    nc.tensor.transpose(bank[:, P:2 * P], W0[par], ident()).then_inc(
                        a_written, 1 + skipped(u, A_SKIP))
                if kind == "mid":
                    for lev in range(1, LEVELS):
                        if lev % 2 == 1:
                            bank = bank_d(lev // 2)
                        pe.wait_ge(x_scaled, tile * XSLOTS + lev)
                        for blk in range(HB):
                            at = ((lev - 1) % 2) * HB * 64 + blk * 64
                            ins = nc.tensor.matmul(bank[:, at:at + 64], lhsT=XS[par][:, lev - 1, blk * P:(blk + 1) * P],
                                                   rhs=odd(GM[par][:, lev - 1, :], lev), start=True, stop=True)
                        if lev % 2 == 0:
                            ins.then_inc(d_written, 1)
                    bank = bank_d(OFF)
                    state = S1 if u == 0 else S
                    if u == 0:
                        pe.wait_ge(s1_ready, tile + 3)
                    else:
                        pe.wait_ge(d_moved, d_no(b, where["mid", u - 1][1] + NEW) + (RING + 1))
                    for blk in range(HB):
                        ins = nc.tensor.matmul(bank[:, blk * P:(blk + 1) * P], lhsT=state[:, blk * P:(blk + 1) * P],
                                               rhs=XBC[q % QB][:, HB + 1, cols_of(u)], start=True, stop=True)
                    ins.then_inc(d_written, 1)
                    bank = bank_d(NEW)
                    pe.wait_ge(x_scaled, (tile + 1) * XSLOTS)
                    pe.wait_ge(a_moved, a_no(b, where["turn", u][0] + 2) + (RING + 1))
                    nc.tensor.matmul(bank[:, :], lhsT=BT[par], rhs=XS[par][:, SUF, :], start=True,
                                     stop=True).then_inc(d_written, 1)
                if kind == "tail":
                    bank = bank_a(0)
                    if u == 0:
                        pe.wait_ge(w_out_scaled, 1)
                    pe.wait_ge(hg_ready, tile + 3)
                    for blk in range(HB):
                        nc.tensor.matmul(bank[:, 0:DM], lhsT=HG[par][:, blk, :], rhs=W_OUT[:, blk, :],
                                         start=(blk == 0), stop=(blk == HB - 1))
                    pe.wait_ge(sq_ready, tile + 3)
                    nc.tensor.matmul(bank[:, DM:DM + 1], lhsT=SQS[par], rhs=CONST[:, C_ONE, 0:1], start=True,
                                     stop=True).then_inc(a_written, 1)

            pe.wait_ge(w_loaded, 16)
            run_first(pe_step)
            pe.wait_ge(consts_in, 16 * 5)
            pe.wait_ge(hot_ready, 1)
            nc.tensor.matmul(BD[0][:, 0:TE], lhsT=CONST[:, C_TRI, :], rhs=HOT, start=True, stop=True)
            nc.tensor.matmul(BD[0][:, TE:2 * TE], lhsT=CONST[:, C_ONE, :], rhs=HOT, start=True,
                             stop=True).then_inc(rank_written, 1)
            run(pe, pe_step)

            pe.wait_ge(a_moved, RING + A_END)
            pe.wait_ge(d_moved, RING + D_END)

            def turn(k, par, slot, loads):
                pe.wait_ge(fx_loaded[slot], loads)
                pe.wait_ge(fy_ready, k + 1)
                for j in range(DK):
                    ins = nc.tensor.transpose(BX[par][:, j * P:(j + 1) * P], FX[slot][:, j * P:(j + 1) * P], ident())
                ins.then_inc(fxt_full, 1)

            def gate_up(k, par):
                e = pe.value_load(EXPERT_OF[0:1, bass.ds(k, 1)], min_val=0, max_val=EXPERTS - 1)
                pe.wait_ge(experts_in, e + 1)
                pe.wait_ge(fxt_ready, k + 1)
                for at, bank, full in ((0, BG[par], fg_full), (DK * DFF, BU[par], fu_full)):
                    for j in range(DK):
                        ins = nc.tensor.matmul(bank[:, :], lhsT=FXT[par][:, j, :],
                                               rhs=WEXP_FLAT[:, bass.ds(e * WE + (at + j * DFF), DFF)],
                                               start=(j == 0), stop=(j == DK - 1))
                    ins.then_inc(full, 1)

            def hidden(k, par):
                pe.wait_ge(fh_ready, k + 1)
                for j in range(KF):
                    ins = nc.tensor.transpose(BH[par][:, j * P:(j + 1) * P], FH[par][:, j * P:(j + 1) * P], ident())
                ins.then_inc(fht_full, 1)

            def down(k, par):
                e = pe.value_load(EXPERT_OF[0:1, bass.ds(k, 1)], min_val=0, max_val=EXPERTS - 1)
                pe.wait_ge(fht_ready, k + 1)
                for j in range(KF):
                    ins = nc.tensor.matmul(BX[par][:, DM:2 * DM], lhsT=FHT[par][:, j, :],
                                           rhs=WEXP_FLAT[:, bass.ds(e * WE + (2 * DK * DFF + j * DM), DM)],
                                           start=(j == 0), stop=(j == KF - 1))
                ins.then_inc(fy_full, 1)

            turn(0, 0, 0, 16)
            gate_up(0, 0)
            turn(1, 1, 1, 16)
            gate_up(1, 1)
            turn(2, 0, 2, 16)
            hidden(0, 0)
            with pe.Fori(0, (NT - 3) // FXN) as i:
                for j in range(FXN):
                    k, par, slot = i * FXN + (2 + j), j % 2, (3 + j) % FXN
                    gate_up(k, par)
                    turn(k + 1, 1 - par, slot, i * 16 + (16 if slot == 3 else 32))
                    hidden(k - 1, 1 - par)
                    down(k - 2, par)
            gate_up(NT - 1, 0)
            hidden(NT - 2, 1)
            down(NT - 3, 0)
            hidden(NT - 1, 0)
            pe.wait_ge(fy_ready, NT - 3 + 5)
            down(NT - 2, 1)
            down(NT - 1, 0)

        @block.vector
        def _(dve):
            chain = [0]

            def link(ins):
                chain[0] += 1
                ins.then_inc(dve_chain, 1)
                dve.wait_ge(dve_chain, chain[0])

            def tt(out, a, b, op):
                return nc.vector.tensor_tensor(out=out, in0=a, in1=b, op=op)

            dve.sem_inc(d_moved, RING + D_BASE)
            dve.sem_inc(conv_done, CB + HB)
            dve.sem_inc(hg_ready, 2)
            dve.sem_inc(sq_ready, 2)

            def variances(g):
                tiles = range(g * GT, (g + 1) * GT)
                dve.wait_ge(x_loaded[g], 16)
                for t in tiles:
                    nc.vector.bn_stats(STATS[:, t, :], X[:, t, 0:DM]).then_inc(dve_chain, 1)
                for t in tiles:
                    chain[0] += 1
                    dve.wait_ge(dve_chain, chain[0])
                    nc.vector.bn_aggr(MV[:, t, :], STATS[:, t, :]).then_inc(dve_chain, 1)
                chain[0] += GT
                dve.wait_ge(dve_chain, chain[0])
                nc.vector.tensor_scalar_add(VE[:, g * GT:(g + 1) * GT].unsqueeze(2), MV[:, g * GT:(g + 1) * GT, 1:2],
                                            EPS).then_inc(var_ready, 1)

            variances(0)
            for g in range(GROUPS):
                if g + 1 < GROUPS:
                    variances(g + 1)
                dve.wait_ge(rstd_ready, g + 1)
                if g > 1:
                    dve.wait_ge(xn_kept, g - 1)
                for c in range(GT):
                    t = g * GT + c
                    ins = nc.vector.tensor_scalar(XNS[g % 2][:, c, :], X[:, t, 0:DM], MV[:, t, 0:1], RS[:, t:t + 1],
                                                  ALU.subtract, ALU.mult)
                ins.then_inc(xn_ready, 1)

            def by_expert(ap):
                return ap.rearrange("p (t e) -> p t e", e=EXPERTS)

            def over_tiles(ap):
                return ap.unsqueeze(1).to_broadcast([P, TILES, EXPERTS])

            def over_experts(ap):
                return ap.unsqueeze(2).to_broadcast([P, TILES, EXPERTS])

            dve.wait_ge(consts_in, 16 * 5)
            nc.vector.tensor_scalar(CONVC, CONVC, 0.5, None, ALU.mult).then_inc(taps_halved, 1)
            dve.wait_ge(iota_made, 1)
            nc.vector.tensor_copy(XN[:, :, DM:DM + 1], IOTAK.bitcast(I32).unsqueeze(2))
            link(nc.vector.tensor_copy(IOTAF, IOTA.bitcast(I32)))
            link(nc.vector.tensor_copy(IOTATF, IOTAT.bitcast(I32)))
            dve.wait_ge(sig_ready, 1)
            link(nc.vector.tensor_scalar_add(SIG, SIG, 1.0))
            link(nc.vector.reciprocal(SIG, SIG))
            link(nc.vector.reduce_max(PROB[:, :], by_expert(SIG), AX.X))
            nc.vector.tensor_scalar(XN[:, :, DM + 1:XW], PROB[:, :].unsqueeze(2), 0.5, None, ALU.mult)
            link(tt(by_expert(R1), by_expert(SIG), over_experts(PROB[:, :]), ALU.is_equal))
            link(tt(by_expert(R2), by_expert(R1), over_tiles(IOTAF), ALU.mult))
            link(nc.vector.tensor_reduce(FIRST, by_expert(R2), AX.X, ALU.min))
            tt(by_expert(HOT), over_tiles(IOTAF), over_experts(FIRST), ALU.is_equal).then_inc(hot_ready, 1)
            dve.wait_ge(a_moved, RING + A_P1)
            by_head = DTR.rearrange("p (t c) -> p t c", c=RW)[:, :, 0:HEADS]
            tt(DT[:, :].rearrange("p (t h) -> p t h", h=HEADS), by_head,
               HEADV[:, V_BIAS:V_BIAS + HEADS].unsqueeze(1).to_broadcast([P, TILES, HEADS]), ALU.add).then_inc(v_ready, 1)
            dve.wait_ge(rank_written, 1)
            nc.vector.tensor_copy(RANK, BD[0][:, 0:TE])
            nc.vector.tensor_copy(TOTS, BD[0][:, TE:2 * TE])
            link(nc.vector.tensor_copy(CUM[0], BD[0][:, TE:2 * TE]))
            src, step = 0, 1
            while step < TILES:
                n = step * EXPERTS
                nc.vector.tensor_copy(CUM[1 - src][:, 0:n], CUM[src][:, 0:n])
                link(tt(CUM[1 - src][:, n:], CUM[src][:, n:], CUM[src][:, 0:TE - n], ALU.add))
                src, step = 1 - src, step * 2
            count = CUM[src][:, TE - EXPERTS:]
            link(nc.vector.tensor_scalar_add(CNTI, count, float(P - 1)))
            link(nc.vector.tensor_single_scalar(CNTS, CNTI, P.bit_length() - 1, ALU.logical_shift_right))
            nc.vector.tensor_copy(CNTF, CNTS)
            link(nc.vector.tensor_copy(ENDS[0], CNTS))
            esrc, step = 0, 1
            while step < EXPERTS:
                nc.vector.tensor_copy(ENDS[1 - esrc][:, 0:step], ENDS[esrc][:, 0:step])
                link(tt(ENDS[1 - esrc][:, step:], ENDS[esrc][:, step:], ENDS[esrc][:, 0:EXPERTS - step], ALU.add))
                esrc, step = 1 - esrc, step * 2
            ends = ENDS[esrc]
            link(tt(LE.rearrange("p (t e) -> p t e", e=EXPERTS), ends.unsqueeze(1).to_broadcast([P, NT, EXPERTS]),
                    IOTATF.rearrange("p (t e) -> p t e", e=EXPERTS), ALU.is_le))
            link(nc.vector.reduce_sum(EXF, LE.rearrange("p (t e) -> p t e", e=EXPERTS)[:, :, 0:EXPERTS - 1], AX.X))
            nc.vector.tensor_copy(EXPERT_OF[:, 0:NT], EXF)
            link(tt(BASE128, ends, CNTF, ALU.subtract))
            link(nc.vector.tensor_scalar(BASE128, BASE128, float(P), None, ALU.mult))
            link(tt(R1, RANK, CUM[src], ALU.add))
            link(tt(R1, R1, TOTS, ALU.subtract))
            link(tt(by_expert(R1), by_expert(R1), over_tiles(BASE128), ALU.add))
            link(tt(R1, R1, HOT, ALU.mult))
            link(nc.vector.reduce_sum(POSF, by_expert(R1), AX.X))
            nc.vector.tensor_copy(POS[:, :], POSF).then_inc(routed, 1)

            def softplus(b, u, k):
                cols = bass.ds(b * (TB * HEADS) + u * HEADS, 2 * HEADS)
                dt, da = DT[:, cols], DA[:, cols]
                if k > 0:
                    dve.wait_ge(sp_chain, b * (TB // 2 * SOFTPLUS) + (u // 2 * SOFTPLUS + k))
                if k == 0:
                    ins = nc.vector.tensor_scalar_add(SPW, da, -0.5)
                elif k == 1:
                    ins = nc.vector.tensor_scalar(SPP, SPW, COEF[-1], COEF[-2], ALU.mult, ALU.add)
                elif k == 2:
                    ins = tt(SPP, SPP, SPW, ALU.mult)
                elif k <= LOG1P_DEGREE:
                    ins = nc.vector.scalar_tensor_tensor(out=SPP, in0=SPP, scalar=COEF[LOG1P_DEGREE + 1 - k], in1=SPW,
                                                         op0=ALU.add, op1=ALU.mult)
                elif k == LOG1P_DEGREE + 1:
                    ins = nc.vector.scalar_tensor_tensor(out=SPP, in0=SPP, scalar=COEF[0], in1=da, op0=ALU.add,
                                                         op1=ALU.mult)
                elif k == LOG1P_DEGREE + 2:
                    ins = nc.vector.scalar_tensor_tensor(out=dt, in0=dt, scalar=0.0, in1=SPP, op0=ALU.max, op1=ALU.add)
                else:
                    nc.vector.scalar_tensor_tensor(
                        out=da.rearrange("p (t h) -> p t h", h=HEADS), in0=dt.rearrange("p (t h) -> p t h", h=HEADS),
                        scalar=-1.0, in1=EA[:, :].unsqueeze(1).to_broadcast([P, 2, HEADS]), op0=ALU.mult,
                        op1=ALU.mult).then_inc(da_ready, 1)
                    return
                ins.then_inc(sp_chain, 1 if k < SOFTPLUS - 2 else 2)

            SOFTPLUS = LOG1P_DEGREE + 4

            def first_softplus(n):
                if n == 0:
                    dve.wait_ge(u_ready, 1)
                    dve.wait_ge(ea_ready, 1)
                for k in range(FIRST_SP * n, min(FIRST_SP * (n + 1), 2 * SOFTPLUS)):
                    softplus(0, k // SOFTPLUS * 2, k % SOFTPLUS)

            FIRST_SP = 5

            def taps(b, q, i, a0):
                par, blk = place_of(q, i) % CB, i - HB
                dve.wait_ge(a_moved, a_no(b, a0) + (RING + 1))
                for j in range(KC - 2, -1, -1):
                    ins = nc.vector.scalar_tensor_tensor(out=ACC[par], in0=RAW[par][:, j:j + GW],
                                                         scalar=CONVC[:, blk, j:j + 1], in1=ACC[par],
                                                         op0=ALU.mult, op1=ALU.add)
                    if j > 0:
                        ins.then_inc(conv_chain, 1)
                        dve.wait_ge(conv_chain, b * (QB * XB * 2) + ((q * XB + blk) * 2 + (KC - 1 - j)))
                ins.then_inc(taps_done, 1)

            def conv_silu(b, q, i):
                dve.wait_ge(tanh_done, b * (QB * XB) + (q * XB + i - HB + 1))
                nc.vector.scalar_tensor_tensor(out=XBC[q % QB][:, i - HB, :], in0=TH[place_of(q, i) % CB],
                                               scalar=1.0, in1=ACC[place_of(q, i) % CB],
                                               op0=ALU.add, op1=ALU.mult).then_inc(conv_done, 1)

            def dve_step(b, where, kind, u, i, a0, d0):
                par, tile, q = u % 2, b * TB + u, u // GT
                if kind == "conv" and i == HB and u > 0:
                    dve.wait_ge(hg_ready, b * TB + ((u - 1) * GT + 2))
                if kind == "conv" and i < HB and u > 0:
                    slot = place_of(u, i) % CB
                    dve.wait_ge(a_moved, a_no(b, a0) + (RING + 1))
                    nc.vector.scalar_tensor_tensor(out=GATE[u % QB][:, i, :], in0=TH[slot], scalar=1.0,
                                                   in1=ACC[slot], op0=ALU.add, op1=ALU.mult).then_inc(conv_done, 1)
                if kind == "conv" and i >= HB:
                    taps(b, u, i, a0)
                    if i > HB:
                        conv_silu(b, u, i - 1)
                    if i == BLOCKS - 1:
                        conv_silu(b, u, i)
                if kind == "head":
                    dve.wait_ge(d_written, d_no(b, d0) - (D_BASE - 1))
                    bank = bank_of_d(d0)
                    for j, m in enumerate((C_ID, C_SHIFT)):
                        nc.vector.tensor_tensor_reduce(
                            out=GJUNK[:, j * P:(j + 1) * P], in0=bank[:, 0:P], in1=CONST[:, m, :], scale=1.0, scalar=0.0,
                            op0=ALU.mult, op1=ALU.add, accum_out=GD[:, j:j + 1]).then_inc(gd_ready, 1)
                    tt(GM[par], bank[:, 0:P].unsqueeze(1).to_broadcast([P, LEVELS - 1, P]),
                       CONST[:, C_MASK:C_MASK + LEVELS - 1, :], ALU.mult).then_inc(d_moved, 1 + skipped(u, D_SKIP))
                    dve.wait_ge(gd_ready, (tile + 1) * 2)
                    dve.wait_ge(a_moved, a_no(b, where["pair", u - par][0] + 2) + (RING + 1))
                    dt = heads_of(DT, b, u).unsqueeze(1).to_broadcast([P, 2, HEADS])
                    nc.vector.scalar_tensor_tensor(
                        out=W1[par].rearrange("p (r h) -> p r h", r=2), in0=E[par][:, NEXT, :, :], scalar=GD[:, 1:2],
                        in1=dt, op0=ALU.mult, op1=ALU.mult)
                    nc.vector.scalar_tensor_tensor(
                        out=W0[par].rearrange("p (r h) -> p r h", r=2), in0=dt, scalar=GD[:, 0:1],
                        in1=HEADV[:, V_D:V_D + HEADS].unsqueeze(1).to_broadcast([P, 2, HEADS]),
                        op0=ALU.mult, op1=ALU.add).then_inc(w0_ready, 1)
                if kind == "mid":
                    dve.wait_ge(a_moved, a_no(b, where["turn", u][0] + 1) + (RING + 1))

                    def taken(j):
                        return d_no(b, d0 + j) + (RING + 1)

                    def products(lev):
                        return PR[lev % 3][:, 0:HB * 64]

                    def scale(lev):
                        if lev == 0:
                            pairs = XBC[q % QB][:, 0:HB, cols_of(u)].rearrange("p b (q o) -> p b q o", o=2)[:, :, :, 0]
                            decay = ET[par][:, M_NEXT, :].rearrange("p (q o) -> p q o", o=2)[:, :, 0]
                            tt(products(0).rearrange("p (b q) -> p b q", b=HB), pairs,
                               decay.unsqueeze(1).to_broadcast([P, HB, 64]), ALU.mult).then_inc(p_chain, 1)
                            return
                        if lev % 2 == 1:
                            dve.wait_ge(d_written, d_no(b, d0 + lev // 2) - (D_BASE - 1))
                        m = 1 << lev
                        shape = [P, HB, 64 // m, m]
                        at = ((lev - 1) % 2) * HB * 64
                        z = bank_of_d(d0 + (lev - 1) // 2)[:, at:at + HB * 64].rearrange(
                            "p (b q m) -> p b q m", b=HB, m=m)
                        ins = tt(products(lev).rearrange("p (b q m) -> p b q m", b=HB, m=m), z,
                                 odd(ET[par][:, lev - 1, :], lev).unsqueeze(1).to_broadcast(shape), ALU.mult)
                        ins.then_inc(d_moved if lev % 2 == 0 else p_chain, 1)

                    def add(lev):
                        if lev % 2 == 0 and lev > 0:
                            dve.wait_ge(d_moved, taken((lev - 1) // 2))
                        else:
                            dve.wait_ge(p_chain, tile * P_TILE + ((lev + 1) // 2 + 1))
                        if lev == 0:
                            dve.wait_ge(y0_ready, tile + 1)
                        else:
                            dve.wait_ge(y_chain, tile * Y_TILE + lev)
                        m = 1 << lev
                        y = odd(Y[par], lev)
                        tt(y, y, products(lev).rearrange("p (b q m) -> p b q m", b=HB, m=m),
                           ALU.add).then_inc(y_chain, 1)

                    first_of = u + 4 - u % 2
                    if not (first_of < TB or where is PLACES[0]):
                        first_of = 0
                    half = (SOFTPLUS + 1) // 2
                    todo = range(half) if u % 2 == 0 else range(half, SOFTPLUS)
                    between = [todo[j:j + 1] if j < LEVELS - 2 else todo[j:] for j in range(LEVELS - 1)]
                    P_TILE, Y_TILE = (LEVELS + 1) // 2, LEVELS + 1
                    scale(0)
                    for lev in range(1, LEVELS):
                        scale(lev)
                        add(lev - 1)
                        if first_of:
                            for k in between[lev - 1]:
                                softplus(b, first_of, k)
                    dve.wait_ge(d_written, d_no(b, d0 + OFF) - (D_BASE - 1))
                    tt(PR[LEVELS % 3].rearrange("p (b t) -> p b t", b=HB),
                       bank_of_d(d0 + OFF)[:, :].rearrange("p (b t) -> p b t", b=HB),
                       ET[par][:, M_PRE, :].unsqueeze(1).to_broadcast([P, HB, P]), ALU.mult).then_inc(d_moved, 1)
                    add(LEVELS - 1)
                    dve.wait_ge(d_moved, taken(OFF))
                    dve.wait_ge(y_chain, tile * Y_TILE + LEVELS)
                    tt(Y[par], Y[par], PR[LEVELS % 3].rearrange("p (b t) -> p b t", b=HB), ALU.add).then_inc(y_chain, 1)
                    dve.wait_ge(d_written, d_no(b, d0 + NEW) - (D_BASE - 1))
                    dve.wait_ge(s1_ready, tile + 3)
                    tt(S, bank_of_d(d0 + NEW)[:, :], S1, ALU.add).then_inc(d_moved, 1)
                    dve.wait_ge(y_chain, (tile + 1) * Y_TILE)
                    dve.wait_ge(conv_done, b * (QB * BLOCKS) + (CB + (q + 1) * BLOCKS))
                    if u == 0:
                        dve.wait_ge(gates_made, HB)
                    dve.wait_ge(a_moved, a_no(b, where["tail", u - 2][0]) + (RING + 1))
                    tt(HG[par], Y[par], GATE[q % QB][:, :, cols_of(u)], ALU.mult).then_inc(hg_ready, 1)
                if kind == "norm":
                    dve.wait_ge(sq_made, tile + 1)
                    dve.wait_ge(a_moved, a_no(b, where["tail", u - 2][0]) + (RING + 1))
                    nc.vector.tensor_reduce(SQS[par], SQ[par].rearrange("p b t -> p t b"), AX.X,
                                            ALU.add).then_inc(sq_ready, 1)

            run_first(dve_step)
            run(dve, dve_step, first_softplus)

            dve.wait_ge(a_moved, RING + A_END)
            nc.vector.tensor_scalar(RNORM[:, :], VARS[:, :], 16 * 0.25 / DIN, 16 * EPS, ALU.mult, ALU.add).then_inc(rn_var, 1)

            dve.sem_inc(fy_ready, 4)

            def expert_half(k, par, slot):
                dve.wait_ge(ft_ready, k + 1)
                nc.vector.scalar_tensor_tensor(out=FG[par], in0=FT[par], scalar=1.0, in1=FG[par],
                                               op0=ALU.add, op1=ALU.mult).then_inc(fa_ready, 1)
                nc.vector.tensor_copy(TOKENS[:, bass.ds(k, 1)], FX[slot][:, DM:DM + 1]).then_inc(token_kept, 1)
                dve.wait_ge(fu_full, k + 1)
                dve.wait_ge(fa_ready, k + 1)
                nc.vector.scalar_tensor_tensor(out=FH[par], in0=BU[par][:, :], scalar=FX[slot][:, DM + 1:XW], in1=FG[par],
                                               op0=ALU.mult, op1=ALU.mult).then_inc(fh_ready, 1)

            def expert_output(k, par):
                dve.wait_ge(tz_ready, k + 1)
                if not isinstance(k, int) or k >= 2:
                    dve.wait_ge(fy_stored, (k - 1) * 16)
                nc.vector.scalar_tensor_tensor(out=FY[par], in0=TZ[par], scalar=1.0, in1=BX[par][:, DM:2 * DM],
                                               op0=ALU.add, op1=ALU.mult).then_inc(fy_ready, 1)

            expert_half(0, 0, 0)
            expert_half(1, 1, 1)
            for k in range(2, 2 + FXN):
                expert_half(k, k % 2, k % FXN)
                expert_output(k - 2, k % 2)
            with dve.Fori(1, (NT - 3) // FXN) as i:
                for j in range(FXN):
                    expert_half(i * FXN + (2 + j), j % 2, (2 + j) % FXN)
                    expert_output(i * FXN + j, j % 2)
            expert_half(NT - 1, 0, (NT - 1) % FXN)
            for k in range(NT - 3, NT):
                expert_output(k, k % 2)

            dve.wait_ge(zx_loaded, 16)
            dve.wait_ge(zo_scaled, 1)
            for g in range(GROUPS - 1):
                cols = slice(g * GT * DM, (g + 1) * GT * DM)
                dve.wait_ge(zf_loaded[g], 16)
                tt(ZF[:, cols], ZF[:, cols], ZO[:, cols], ALU.mult).then_inc(z_made[g], 1)
                dve.wait_ge(z_made[g], 1)
                tt(ZX[:, cols], ZX[:, cols], ZF[:, cols], ALU.add).then_inc(z_out[g], 1)


def kernel(**inputs):
    import concourse.bacc as bacc
    from concourse.bass_utils import run_bass_kernel_spmd

    def get(name):
        return np.ascontiguousarray(inputs[name])

    def by_p(a):
        return a.reshape(HEADS, HD, *a.shape[1:]).swapaxes(0, 1).reshape(a.shape)

    w_in = get("L0_attn_in_proj_w")
    gate, x, bc, dt = w_in[:DIN], w_in[DIN:2 * DIN], w_in[2 * DIN:2 * DIN + 2 * NST], w_in[2 * DIN + 2 * NST:]
    conv = np.concatenate([get("L0_attn_conv_w"), get("L0_attn_conv_b")[:, None]], axis=1)
    conv = np.concatenate([by_p(conv[:DIN]), conv[DIN:]])
    arrays = {
        "x": get("L0_attn_hidden_states").reshape(TOK, DM),
        "w_main": np.concatenate([by_p(gate), by_p(x), bc]).T,
        "w_dr": np.concatenate([dt.T, get("L0_ffn_router_w")], axis=1),
        "conv_c": conv.reshape(XB, P, KC + 1).transpose(1, 0, 2).reshape(P, XB * (KC + 1)),
        "head_v": np.concatenate([get("L0_attn_dt_bias"), get("L0_attn_A_log"), get("L0_attn_D")])[None],
        "norm_c": by_p(get("L0_attn_norm_w")).reshape(HB, P).T,
        "w_out": by_p(get("L0_attn_out_proj_w").T),
        "w_gate": get("L0_ffn_gate_w"),
        "w_up": get("L0_ffn_up_w"),
        "w_down": get("L0_ffn_down_w"),
        "consts": constant_matrices().reshape(P, N_CONST * P),
    }
    arrays = {n: np.ascontiguousarray(a) for n, a in arrays.items()}
    nc = bacc.Bacc("TRN2", target_bir_lowering=False, num_devices=1)
    args = [nc.dram_tensor(f"in_{n}", a.shape, FP32, kind="ExternalInput").ap() for n, a in arrays.items()]
    out = nc.dram_tensor("out_0_dram", [TOK, DM], FP32, kind="ExternalOutput").ap()
    mixer_moe_kernel(nc, *args, out)
    r = run_bass_kernel_spmd(nc, [{f"in_{n}": a for n, a in arrays.items()}], core_ids=[0])
    return r.results[0]["out_0_dram"].reshape(BATCH, SEQ, DM)
```
